# Optimizing a Trainium2 kernel written in Bass

```python
import numpy as np
import jax
import jax.numpy as jnp

def _softmax(x, axis=-1):
    return jax.nn.softmax(x, axis=axis)

def _gelu(x):
    return jax.nn.gelu(x, approximate=True)

def _silu(x):
    return jax.nn.silu(x)

def _sigmoid(x):
    return jax.nn.sigmoid(x)

def _layernorm(x, axis=-1, eps=1e-05):
    m = jnp.mean(x, axis=axis, keepdims=True)
    v = jnp.var(x, axis=axis, keepdims=True)
    return (x - m) / jnp.sqrt(v + eps)

def _scatter_add(tgt, idx, src, axis=0):
    return tgt.at[idx].add(src)

def _segment_sum(src, seg, n):
    return jax.ops.segment_sum(src, seg, n)
kernel_name = 'mk_macaron_d2_jaxref_r8_2eadec'

def setup_inputs(seed: int=0):
    np.random.seed(seed)
    _w = jnp.asarray

    def _L0_attn_setup():
        import jax, jax.numpy as jnp
        import numpy as np
        EMB_DIM = 128
        N_HEADS = 16
        HEAD_DIM = EMB_DIM // N_HEADS
        SEQ = 256
        BSZ = 2

        def _rope_pair(q, k):
            bsz, seq_len, d_model = q.shape
            freq_range = jnp.arange(d_model // 2, dtype=jnp.float32)
            freq_cis = jnp.power(10000.0, -2.0 * freq_range / d_model)
            pos = jnp.arange(seq_len, dtype=jnp.float32)
            freq = jnp.einsum('i,j->ij', pos, freq_cis)
            sin_e = jnp.sin(freq)[None]
            cos_e = jnp.cos(freq)[None]
            q_even, q_odd = (q[..., ::2], q[..., 1::2])
            k_even, k_odd = (k[..., ::2], k[..., 1::2])
            q_rot = jnp.concatenate([q_even * cos_e - q_odd * sin_e, q_even * sin_e - q_odd * cos_e], axis=-1)
            k_rot = jnp.concatenate([k_even * cos_e - k_odd * sin_e, k_even * sin_e - k_odd * cos_e], axis=-1)
            return (q_rot, k_rot)
        key = jax.random.key(seed)
        ks = jax.random.split(key, 9)
        s = 1.0 / np.sqrt(EMB_DIM)
        return {'x': jax.random.normal(ks[0], (BSZ, SEQ, EMB_DIM), dtype=jnp.float32), 'Wq': jax.random.normal(ks[1], (EMB_DIM, EMB_DIM), dtype=jnp.float32) * s, 'bq': jax.random.normal(ks[2], (EMB_DIM,), dtype=jnp.float32) * 0.02, 'Wk': jax.random.normal(ks[3], (EMB_DIM, EMB_DIM), dtype=jnp.float32) * s, 'bk': jax.random.normal(ks[4], (EMB_DIM,), dtype=jnp.float32) * 0.02, 'Wv': jax.random.normal(ks[5], (EMB_DIM, EMB_DIM), dtype=jnp.float32) * s, 'bv': jax.random.normal(ks[6], (EMB_DIM,), dtype=jnp.float32) * 0.02, 'Wo': jax.random.normal(ks[7], (EMB_DIM, EMB_DIM), dtype=jnp.float32) * s, 'bo': jax.random.normal(ks[8], (EMB_DIM,), dtype=jnp.float32) * 0.02}
    _L0_attn_in = _L0_attn_setup()

    def _L0_ffn_setup():
        import jax, jax.numpy as jnp
        import numpy as np
        D_MODEL = 128
        N_EXPERTS = 8
        TOP_K = 2
        key = jax.random.key(seed)
        k1, k2, k3, k4 = jax.random.split(key, 4)
        B, S, D, E = (4, 256, D_MODEL, N_EXPERTS)
        dff = 4 * D
        lim = float(np.sqrt(6.0 / (D + dff)))
        return {'x': jax.random.normal(k1, (B, S, D), dtype=jnp.float32), 'router_w': jax.random.normal(k2, (D, E), dtype=jnp.float32) * (1.0 / np.sqrt(D)), 'router_b': jnp.zeros((E,), dtype=jnp.float32), 'expert_up': jax.random.uniform(k3, (E, dff, D), dtype=jnp.float32, minval=-lim, maxval=lim), 'expert_down': jax.random.uniform(k4, (E, D, dff), dtype=jnp.float32, minval=-lim, maxval=lim)}
    _L0_ffn_in = _L0_ffn_setup()

    def _L1_attn_setup():
        import jax, jax.numpy as jnp
        import numpy as np
        DIM = 128
        CHUNK = 64
        STATE = 64
        DT_RANK = (DIM + 15) // 16
        EPS = 1e-06

        def _rmsnorm(x, w):
            var = jnp.mean(x * x, axis=-1, keepdims=True)
            return x * jax.lax.rsqrt(var + EPS) * w
        key = jax.random.key(seed)
        ks = jax.random.split(key, 6)
        B, L = (2, 512)
        x = jax.random.normal(ks[0], (B, L, DIM), dtype=jnp.float32)
        norm_w = jnp.ones((DIM,), dtype=jnp.float32)
        x_proj_w = jax.random.normal(ks[1], (DT_RANK + 2 * STATE, DIM), dtype=jnp.float32) * 0.02
        dt_proj_w = jax.random.normal(ks[2], (DIM, DT_RANK), dtype=jnp.float32) * 0.02
        dt_proj_b = jnp.zeros((DIM,), dtype=jnp.float32)
        A_log = jnp.zeros((DIM, STATE), dtype=jnp.float32)
        D = jnp.ones((DIM,), dtype=jnp.float32)
        out_proj_w = jax.random.normal(ks[3], (DIM, DIM), dtype=jnp.float32) * 0.02
        return {'x': x, 'norm_w': norm_w, 'x_proj_w': x_proj_w, 'dt_proj_w': dt_proj_w, 'dt_proj_b': dt_proj_b, 'A_log': A_log, 'D': D, 'out_proj_w': out_proj_w}
    _L1_attn_in = _L1_attn_setup()

    def _L1_ffn_setup():
        import jax, jax.numpy as jnp
        import numpy as np
        B, S, D, E = (4, 256, 128, 8)
        H = 2 * D
        key = jax.random.key(seed)
        ks = jax.random.split(key, 7)
        s_d = 1.0 / np.sqrt(D)
        s_h = 1.0 / np.sqrt(H)
        return {'x': jax.random.normal(ks[0], (B, S, D), dtype=jnp.float32), 'w_router': jax.random.normal(ks[1], (D, E), dtype=jnp.float32) * s_d, 'b_router': jnp.zeros((E,), dtype=jnp.float32), 'w1': jax.random.normal(ks[2], (E, D, H), dtype=jnp.float32) * s_d, 'b1': jnp.zeros((E, H), dtype=jnp.float32), 'w2': jax.random.normal(ks[3], (E, H, D), dtype=jnp.float32) * s_h, 'b2': jnp.zeros((E, D), dtype=jnp.float32)}
    _L1_ffn_in = _L1_ffn_setup()
    _d = {'L0_attn_x': _L0_attn_in['x'], 'L0_attn_Wq': _L0_attn_in['Wq'], 'L0_attn_bq': _L0_attn_in['bq'], 'L0_attn_Wk': _L0_attn_in['Wk'], 'L0_attn_bk': _L0_attn_in['bk'], 'L0_attn_Wv': _L0_attn_in['Wv'], 'L0_attn_bv': _L0_attn_in['bv'], 'L0_attn_Wo': _L0_attn_in['Wo'], 'L0_attn_bo': _L0_attn_in['bo'], 'L0_ffn_router_w': _L0_ffn_in['router_w'], 'L0_ffn_router_b': _L0_ffn_in['router_b'], 'L0_ffn_expert_up': _L0_ffn_in['expert_up'], 'L0_ffn_expert_down': _L0_ffn_in['expert_down'], 'L1_attn_norm_w': _L1_attn_in['norm_w'], 'L1_attn_x_proj_w': _L1_attn_in['x_proj_w'], 'L1_attn_dt_proj_w': _L1_attn_in['dt_proj_w'], 'L1_attn_dt_proj_b': _L1_attn_in['dt_proj_b'], 'L1_attn_A_log': _L1_attn_in['A_log'], 'L1_attn_D': _L1_attn_in['D'], 'L1_attn_out_proj_w': _L1_attn_in['out_proj_w'], 'L1_ffn_w_router': _L1_ffn_in['w_router'], 'L1_ffn_b_router': _L1_ffn_in['b_router'], 'L1_ffn_w1': _L1_ffn_in['w1'], 'L1_ffn_b1': _L1_ffn_in['b1'], 'L1_ffn_w2': _L1_ffn_in['w2'], 'L1_ffn_b2': _L1_ffn_in['b2']}
    _x0 = _d['L0_attn_x']
    _d['L0_attn_x'] = jax.random.normal(jax.random.fold_in(jax.random.key(seed), 1), (2, 1024, 128), dtype=_x0.dtype)
    del _x0
    return _d

def reference(L0_attn_x, L0_attn_Wq, L0_attn_bq, L0_attn_Wk, L0_attn_bk, L0_attn_Wv, L0_attn_bv, L0_attn_Wo, L0_attn_bo, L0_ffn_router_w, L0_ffn_router_b, L0_ffn_expert_up, L0_ffn_expert_down, L1_attn_norm_w, L1_attn_x_proj_w, L1_attn_dt_proj_w, L1_attn_dt_proj_b, L1_attn_A_log, L1_attn_D, L1_attn_out_proj_w, L1_ffn_w_router, L1_ffn_b_router, L1_ffn_w1, L1_ffn_b1, L1_ffn_w2, L1_ffn_b2):

    def _L0_attn_ref(x, Wq, bq, Wk, bk, Wv, bv, Wo, bo):
        import jax, jax.numpy as jnp
        import numpy as np
        EMB_DIM = 128
        N_HEADS = 16
        HEAD_DIM = EMB_DIM // N_HEADS
        SEQ = 256
        BSZ = 2

        def _rope_pair(q, k):
            bsz, seq_len, d_model = q.shape
            freq_range = jnp.arange(d_model // 2, dtype=jnp.float32)
            freq_cis = jnp.power(10000.0, -2.0 * freq_range / d_model)
            pos = jnp.arange(seq_len, dtype=jnp.float32)
            freq = jnp.einsum('i,j->ij', pos, freq_cis)
            sin_e = jnp.sin(freq)[None]
            cos_e = jnp.cos(freq)[None]
            q_even, q_odd = (q[..., ::2], q[..., 1::2])
            k_even, k_odd = (k[..., ::2], k[..., 1::2])
            q_rot = jnp.concatenate([q_even * cos_e - q_odd * sin_e, q_even * sin_e - q_odd * cos_e], axis=-1)
            k_rot = jnp.concatenate([k_even * cos_e - k_odd * sin_e, k_even * sin_e - k_odd * cos_e], axis=-1)
            return (q_rot, k_rot)
        bsz, n, d = x.shape
        Q = x @ Wq + bq
        K = x @ Wk + bk
        V = x @ Wv + bv
        Q, K = _rope_pair(Q, K)
        Q = Q.reshape(bsz, n, N_HEADS, HEAD_DIM).transpose(0, 2, 1, 3)
        K = K.reshape(bsz, n, N_HEADS, HEAD_DIM).transpose(0, 2, 1, 3)
        V = V.reshape(bsz, n, N_HEADS, HEAD_DIM).transpose(0, 2, 1, 3)
        scores = jnp.einsum('bhqd,bhkd->bhqk', Q, K)
        causal = jnp.triu(jnp.ones((n, n), dtype=bool), k=1)
        scores = jnp.where(causal, -jnp.inf, scores)
        attn = jax.nn.softmax(scores / jnp.sqrt(jnp.float32(HEAD_DIM)), axis=-1)
        ctx = jnp.einsum('bhqk,bhkd->bhqd', attn, V)
        ctx = ctx.transpose(0, 2, 1, 3).reshape(bsz, n, d)
        return ctx @ Wo + bo

    def _L0_ffn_ref(x, router_w, router_b, expert_up, expert_down):
        import jax, jax.numpy as jnp
        import numpy as np
        D_MODEL = 128
        N_EXPERTS = 8
        TOP_K = 2
        B, S, D = x.shape
        E = expert_up.shape[0]
        x_flat = x.reshape(-1, D)
        logits = x_flat @ router_w + router_b
        probs = jax.nn.softmax(logits, axis=-1)
        top_w, top_idx = jax.lax.top_k(probs, TOP_K)
        comb = jnp.sum(top_w[..., None] * jax.nn.one_hot(top_idx, E, dtype=x.dtype), axis=1)
        output = jnp.zeros_like(x_flat)
        for e in range(E):
            h = jax.nn.gelu(x_flat @ expert_up[e].T, approximate=False)
            out_e = h @ expert_down[e].T
            output = output + comb[:, e:e + 1] * out_e
        return output.reshape(B, S, D)

    def _L1_attn_ref(x, norm_w, x_proj_w, dt_proj_w, dt_proj_b, A_log, D, out_proj_w):
        import jax, jax.numpy as jnp
        import numpy as np
        DIM = 128
        CHUNK = 64
        STATE = 64
        DT_RANK = (DIM + 15) // 16
        EPS = 1e-06

        def _rmsnorm(x, w):
            var = jnp.mean(x * x, axis=-1, keepdims=True)
            return x * jax.lax.rsqrt(var + EPS) * w
        B, L, Dm = x.shape
        assert L % CHUNK == 0
        nc = L // CHUNK
        M = B * nc
        xn = _rmsnorm(x, norm_w)
        proj = jnp.einsum('bld,pd->blp', xn, x_proj_w)
        delta_lo, Bs, Cs = jnp.split(proj, [DT_RANK, DT_RANK + STATE], axis=-1)
        delta = jax.nn.softplus(jnp.einsum('blr,dr->bld', delta_lo, dt_proj_w) + dt_proj_b)
        A = -jnp.exp(A_log)

        def to_tm(t, feat):
            return t.reshape(B, nc, CHUNK, feat).reshape(M, CHUNK, feat).transpose(1, 0, 2)
        dt_seq = to_tm(delta, Dm)
        b_seq = to_tm(Bs, STATE)
        c_seq = to_tm(Cs, STATE)
        x_seq = to_tm(xn, Dm)

        def step(h, inp):
            dt, bt, ct, xt = inp
            dA = jnp.exp(dt[..., None] * A)
            h = dA * h + dt[..., None] * bt[:, None, :] * xt[..., None]
            y = jnp.einsum('mdn,mn->md', h, ct)
            return (h, y)
        h0 = jnp.zeros((M, Dm, STATE), dtype=x.dtype)
        _, ys = jax.lax.scan(step, h0, (dt_seq, b_seq, c_seq, x_seq))
        y = ys.transpose(1, 0, 2).reshape(B, nc, CHUNK, Dm).reshape(B, L, Dm)
        return jnp.einsum('bld,od->blo', y + x * D, out_proj_w)

    def _L1_ffn_ref(x, w_router, b_router, w1, b1, w2, b2):
        import jax, jax.numpy as jnp
        import numpy as np
        B, S, D, E = (4, 256, 128, 8)
        H = 2 * D
        scores = jax.nn.softmax(x @ w_router + b_router, axis=2)
        expert_probs = jnp.max(scores, axis=2)
        expert_idx = jnp.argmax(scores, axis=2)
        h = jax.nn.relu(jnp.einsum('bsd,edh->ebsh', x, w1) + b1[:, None, None, :])
        y = jnp.einsum('ebsh,ehd->ebsd', h, w2) + b2[:, None, None, :]
        onehot = jax.nn.one_hot(expert_idx, E, dtype=x.dtype)
        out = jnp.einsum('ebsd,bse->bsd', y, onehot)
        return out * expert_probs[..., None]
    x = L0_attn_x
    x = x + 0.5 * _L0_ffn_ref(_layernorm(x, axis=-1), L0_ffn_router_w, L0_ffn_router_b, L0_ffn_expert_up, L0_ffn_expert_down)
    x = x + _L0_attn_ref(_layernorm(x, axis=-1), L0_attn_Wq, L0_attn_bq, L0_attn_Wk, L0_attn_bk, L0_attn_Wv, L0_attn_bv, L0_attn_Wo, L0_attn_bo)
    x = x + 0.5 * _L0_ffn_ref(_layernorm(x, axis=-1), L0_ffn_router_w, L0_ffn_router_b, L0_ffn_expert_up, L0_ffn_expert_down)
    x = x + 0.5 * _L1_ffn_ref(_layernorm(x, axis=-1), L1_ffn_w_router, L1_ffn_b_router, L1_ffn_w1, L1_ffn_b1, L1_ffn_w2, L1_ffn_b2)
    x = x + _L1_attn_ref(_layernorm(x, axis=-1), L1_attn_norm_w, L1_attn_x_proj_w, L1_attn_dt_proj_w, L1_attn_dt_proj_b, L1_attn_A_log, L1_attn_D, L1_attn_out_proj_w)
    x = x + 0.5 * _L1_ffn_ref(_layernorm(x, axis=-1), L1_ffn_w_router, L1_ffn_b_router, L1_ffn_w1, L1_ffn_b1, L1_ffn_w2, L1_ffn_b2)
    return x

_drawn_inputs = setup_inputs


def setup_inputs(seed=0):
    import zlib

    import numpy as np

    out = dict(_drawn_inputs(seed))
    spreads = {'L0_ffn_router_b': (0.0, 0.1),
     'L1_attn_norm_w': (1.0, 0.2),
     'L1_attn_dt_proj_b': (0.0, 0.8),
     'L1_attn_A_log': (0.0, 0.8),
     'L1_attn_D': (1.0, 0.2),
     'L1_ffn_b_router': (0.0, 0.1),
     'L1_ffn_b1': (0.0, 0.296),
     'L1_ffn_b2': (0.0, 0.1)}
    factors = {'L0_attn_bq': 5.267, 'L0_attn_bk': 8.0, 'L1_attn_dt_proj_w': 42.35}
    for name, (base, spread) in spreads.items():
        noise = np.random.default_rng([zlib.crc32(name.encode()), seed]).standard_normal(out[name].shape)
        drawn = base * np.exp(spread * noise) if base else spread * noise
        out[name] = jnp.asarray(drawn.astype(out[name].dtype))
    for name, factor in factors.items():
        out[name] = (out[name] * factor).astype(out[name].dtype)
    return out
```

```python
from contextlib import ExitStack

import numpy as np

import concourse.bass as bass
from concourse import mybir

ACT = mybir.ActivationFunctionType
ALU = mybir.AluOpType
AX = mybir.AxisListType
F32 = mybir.dt.float32
F32R = mybir.dt.float32r
BF16 = mybir.dt.bfloat16

P = 128
D = 128
B, S = 2, 1024
T = B * S
NT = T // P
TB = 512
NTB = T // TB
TPB = TB // P
E = 8
F0 = 512
F1 = 256
LN_EPS = 1e-5
H, HD = 16, 8
HG = 4
NG = H // HG
NU = B * NG
ST_ = S // P
SCALE = HD ** -0.5
MASKED = -1e30
STATE = 64
RANK = 8
CHUNK = 64
RMS_EPS = 1e-6
TR, DQ = 128, 32
NTR, NDQ = S // TR, D // DQ
NSU = NTR * NDQ
DG = 16
ROWS = B * 3 * DG
ARENA = 134 * 256
PLAN = [("a", 0), ("b", "attention"), ("c", 0), ("d", 1), ("e", "scan"), ("f", 1)]
CONSTS = 16 * 24
ACC_END = NTB * E + 2


def build(nc, t_in, scratch, out):
    with ExitStack() as ctx:
        def sb(name, shape, dt=F32):
            return ctx.enter_context(nc.sbuf_tensor(name, shape, dt))

        def sem(name):
            return ctx.enter_context(nc.semaphore(name))

        x = sb("x", [P, NT, D])
        xf = x[:].rearrange("p i d -> p (i d)")
        xn = sb("xn", [P, NT, D])
        xnT = sb("xnT", [P, T])
        ident = sb("ident", [P, P])
        stats = sb("stats", [P, NT, 6])
        mv = sb("mv", [P, NT, 2])
        veps = sb("veps", [P, NT])
        std = sb("std", [P, NT])
        rstd = sb("rstd", [P, NT])
        lg = sb("lg", [P, NT, E])
        rowmax = sb("rowmax", [P, NT])
        probs = sb("probs", [P, NT, E])
        earlier = sb("earlier", [P, E, E])
        rank = sb("rank", [P, NT, E])
        comb = sb("comb", [P, NT, E])
        combf = comb[:].rearrange("p i e -> p (i e)")
        rw = [sb("rw0", [P, E]), sb("rw1", [P, E])]
        rb = [sb("rb0", [P, E]), sb("rb1", [P, E])]
        b1c = sb("b1c", [P, E, F1 // P])
        b2r = sb("b2r", [E, D])
        wqkv = sb("wqkv", [P, 3 * D])
        bqkv = sb("bqkv", [P, 3 * D])
        wo = sb("wo", [P, D])
        bo = sb("bo", [P, D])
        identb = sb("identb", [P, P], BF16)
        hide_q = sb("hide_q", [P, P], BF16)
        hide_k = sb("hide_k", [P, P], BF16)
        qT = sb("qT", [P, S], F32R)
        qmT = sb("qmT", [P, 2, S], F32R)
        kT = sb("kT", [P, 2, S], F32R)
        maxima = sb("maxima", [P, ST_, HG, 2])
        maxf = maxima[:].rearrange("p i h t -> p (i h t)")
        osum = sb("osum", [P, 4, HG, 1])
        xpw = sb("xpw", [P, RANK + 2 * STATE])
        dtw = sb("dtw", [RANK, D])
        dtb = sb("dtb", [P, 1])
        dskip = sb("dskip", [P, 1])
        nw = sb("nw", [P, D])
        opw = sb("opw", [P, D])
        arate = sb("arate", [P, D])
        up1 = sb("up1", [P, E, F1])
        dn1 = sb("dn1", [P, E, F1 // P, D])

        arena = sb("arena", [P, ARENA])
        top = [0]

        def carve(n):
            top[0] += n
            assert top[0] <= ARENA, top[0]
            return arena[:, top[0] - n:top[0]]

        hidf = carve(2 * F0 // P * TB)
        hid = hidf.rearrange("p (a c t) -> p a c t", a=2, c=F0 // P)
        beats = carve(NT * E * E).rearrange("p (r e) -> p r e", e=E)
        tiesf = carve(NT * E * E)
        ties = tiesf.rearrange("p (r e) -> p r e", e=E)
        spare = carve(2 * T - NT * E * E)
        combT = arena[0:E, top[0] - T:top[0]]
        up0 = carve(E * F0).rearrange("p (e f) -> p e f", e=E)
        dn0 = carve(F0 // P * E * D).rearrange("p (e c d) -> p e c d", e=E, c=F0 // P)
        rtmp = hidf
        qkf = carve(NT * 2 * D)
        qk = qkf.rearrange("p (i c d) -> p i c d", c=2, d=D)
        probT = qkf.rearrange("p (s h q) -> p s h q", s=2, h=HG)
        rot = carve(2 * T).rearrange("p (c i d) -> p c i d", c=2, d=D)
        vall = carve(T).rearrange("p (i d) -> p i d", d=D)
        cos = carve(ST_ * D // 2).rearrange("p (i f) -> p i f", i=ST_)
        sin = carve(ST_ * D // 2).rearrange("p (i f) -> p i f", i=ST_)
        maskf = carve(2 * P).rearrange("p (a b) -> p a b", a=2)
        ctxv = xn[:]
        qpad = carve(ST_ * HG * 32).rearrange("p (i h c) -> p i h c", i=ST_, h=HG)
        kpad = carve(ST_ * HG * 32).rearrange("p (i h c) -> p i h c", i=ST_, h=HG)
        vpad = carve(2 * ST_ * HG * 32).rearrange("p (s i h c) -> p s i h c", s=2, i=ST_, h=HG)
        oT = carve(2 * 512).rearrange("p (a q) -> p a q", a=2)
        top[0] = 0
        dtp = carve(D // DG * S // 2).bitcast(BF16).rearrange("p (g t) -> p g t", t=S)
        upp = carve(D // DG * S // 2).bitcast(BF16).rearrange("p (g t) -> p g t", t=S)
        sel = carve(DG * P // 2).bitcast(BF16).rearrange("p (r m) -> p r m", m=P)
        bT = carve(S)
        cT = carve(S)
        cz = carve(TR * 32).rearrange("p (t c) -> p t c", c=32)
        ysb = carve(T).rearrange("p (r d) -> p r d", d=D)
        prep0 = top[0]
        da = carve(2 * DQ * TR).rearrange("p (s n) -> p s n", s=2)
        hs = carve(2 * DQ * TR).rearrange("p (s n) -> p s n", s=2)
        top[0] = prep0
        xr = carve(T).rearrange("p (i d) -> p i d", d=D)
        z = carve(T)
        soft = carve(T)
        parts = carve(3 * T).bitcast(BF16).rearrange("p (v a t) -> p v a t", v=2, a=3)
        selftmp = carve(DG * P)
        loT = arena[0:RANK, prep0 + 8 * T - T:prep0 + 8 * T]
        ps = ctx.enter_context(nc.psum_tensor("ps", [P, 8, 512], F32))

        consts_in = sem("consts_in")
        x_in = sem("x_in")
        w_in = sem("w_in")
        stored = sem("stored")
        x_final = sem("x_final")
        parts_out = sem("parts_out")
        parts_in = sem("parts_in")
        chain = sem("chain")
        chained = [0]

        MOE = {}
        for name in ("a", "c", "d", "f"):
            MOE[name] = {k: sem(f"{name}_{k}") for k in (
                "var_ready", "std_ready", "xn_ready", "tp_done", "xnT_ready", "logits_done", "shifted",
                "exp_done", "comb_ready", "comb_turned", "combT_ready", "bias_done", "bias_added", "up_done", "act_done", "down_done", "acc_done")}
        AT = {k: sem(f"att_{k}") for k in (
            "var_ready", "std_ready", "xn_ready", "tp_done", "xnT_ready", "qkv_done", "qkv_copied", "rotated",
            "masks_ready", "pads_ready", "parts", "waited", "unit_split", "turned", "turned_copied", "s_done", "max_done", "negmax_ready",
            "st_done", "exp_done", "pv_done", "o_copied", "o_turned", "o_summed", "o_normed", "ctxT_turned", "ctxT_ready",
            "proj_done", "proj_added")}
        SC = {k: sem(f"scan_{k}") for k in (
            "var_ready", "std_ready", "xn_ready", "tp_done", "xnT_ready", "arena_free", "sel_in", "sel_ready", "rms_ready",
            "rms_std", "xr_ready", "xr_turned", "xrT_ready", "bc_done", "lo_done", "bT_ready", "loT_ready", "dt_done",
            "z_ready", "abs_ready", "exp_ready", "ln_ready", "rate_exp", "rate_ready", "split", "c_zeroed", "c_placed",
            "dt_cast", "da_done", "da_cut", "u_cast", "in_done", "h_done", "y_done", "y_copied", "xs_turned",
            "xsT_ready", "yT_turned", "yT_ready", "g_ready", "waited", "proj_done", "proj_added", "prep_done")}
        plan = PLAN

        block = ctx.enter_context(nc.Block())

        s_blocks = [(h, group, w)
                    for group, w in [([(0, 0), (4, 1)], P), ([(1, 0), (5, 1)], 2 * P), ([(2, 0)], 3 * P),
                                     ([(3, 0)], 4 * P), ([(6, 1)], 3 * P), ([(7, 1)], 4 * P)]
                    + [([(i, 0)], 4 * P) for i in range(4, ST_)]
                    for h in range(HG)]
        NSB = len(s_blocks)
        steps = [(0, j) for j in range(4)] + [(1, j) for j in range(ST_)]
        NST = len(steps)

        def span(m):
            half, j = steps[m]
            q0 = max(0, j * P - half * 512)
            return q0, 512 - q0

        def order(main, pre):
            todo = [("s", n) for n in range(NSB)] if pre else []
            if pre and main:
                per = -(-NSB // 9)
            else:
                per = NSB
            if not main:
                yield ("turn", 0)
                yield from todo
                yield ("returned", 0)
                return
            for m in range(NST):
                yield ("st", m)
                if m == 0 and pre:
                    yield ("turn", 0)
                if m >= 1:
                    yield ("pv", m - 1)
                if m == 5:
                    yield ("ocopy", 0)
                if m == 6:
                    yield ("oturn", 0)
                if m >= 1:
                    yield from todo[:per]
                    todo = todo[per:]
                if m == NST - 1 and pre:
                    yield ("returned", 0)
            yield ("pv", NST - 1)
            yield ("ocopy", 1)
            yield ("oturn", 1)

        @block.sync
        def _(sp):
            sp.dma_start(x[:], t_in["x"].rearrange("(i p) d -> p i d", p=P)).then_inc(x_in, 16)
            for dst, name in ((ident[:], "ident"), (rw[0][:], "rw0"), (rw[1][:], "rw1"), (b2r[:], "b2")):
                sp.dma_start(dst, t_in[name]).then_inc(consts_in, 16)
            sp.dma_start(rb[0][:], t_in["rb0"].partition_broadcast(P)).then_inc(consts_in, 16)
            sp.dma_start(rb[1][:], t_in["rb1"].partition_broadcast(P)).then_inc(consts_in, 16)
            sp.dma_start(earlier[:], t_in["earlier"].partition_broadcast(P)).then_inc(consts_in, 16)
            sp.dma_start(b1c[:], t_in["b1"]).then_inc(consts_in, 16)
            for dst, name in ((wqkv, "wqkv"), (wo, "wo"), (cos, "cos"), (sin, "sin"), (maskf, "masks")):
                sp.dma_start(dst[:], t_in[name]).then_inc(consts_in, 16)
            for n, name in enumerate(("bq", "bk", "bv")):
                sp.dma_start(bqkv[:, n * D:(n + 1) * D], t_in[name].partition_broadcast(P)).then_inc(consts_in, 16)
            sp.dma_start(bo[:], t_in["bo"].partition_broadcast(P)).then_inc(consts_in, 16)
            for dst, name in ((xpw, "xpw"), (dtw, "dtw"), (dtb, "dtb"), (dskip, "dskip"), (opw, "opw"),
                              (arate, "a_log")):
                sp.dma_start(dst[:], t_in[name]).then_inc(consts_in, 16)
            sp.dma_start(nw[:], t_in["norm_w"].partition_broadcast(P)).then_inc(consts_in, 16)
            for dst, name in ((up0, "up0"), (dn0, "dn0"), (up1, "up1"), (dn1, "dn1")):
                sp.dma_start(dst[:], t_in[name]).then_inc(w_in, 16)
            if ("e", "scan") in plan:
                sp.wait_ge(SC["arena_free"], 1)
                sp.dma_start(selftmp[0:ROWS, :], t_in["sel"]).then_inc(SC["sel_in"], 16)
                for v, dst in enumerate((dtp, upp)):
                    sp.wait_ge(SC["split"], v + 1)
                    sp.dma_start(scratch[v].rearrange("a d t -> d a t"), parts[:, v]).then_inc(parts_out, 16)
                    sp.wait_ge(parts_out, 16 * (v + 1))
                    for b in range(B):
                        for a in range(3):
                            r0 = (b * 3 + a) * DG
                            sp.dma_start(dst[r0:r0 + DG], scratch[v, a].rearrange("(g r) t -> r g t", r=DG)[
                                :, :, b * S:(b + 1) * S]).then_inc(parts_in, 16)
            sp.wait_ge(x_final, 1)
            sp.dma_start(out.rearrange("(i p) d -> p i d", p=P), x[:]).then_inc(stored, 16)
            sp.wait_ge(stored, 16)

        def moe_tensor(e, s, kind):
            nf = (F0, F1)[kind] // P
            up, dn = ((up0, dn0), (up1, dn1))[kind]
            turn_tokens(e, s)
            for i in range(NT):
                mm = e.matmul(ps[:, 6, i * E:(i + 1) * E], xnT[:, i * P:(i + 1) * P], rw[kind][:],
                              start=True, stop=True)
            mm.then_inc(s["logits_done"], 1)
            if kind == 1:
                e.wait_ge(s["comb_ready"], 1)
                for i in range(NT):
                    mm = e.transpose(ps[0:E, i // TPB, i % TPB * P:(i % TPB + 1) * P], comb[:, i, :], ident[:])
                mm.then_inc(s["comb_turned"], 1)
                e.wait_ge(s["combT_ready"], 1)
                for i in range(NT):
                    mm = e.matmul(ps[:, i // TPB, i % TPB * P:(i % TPB + 1) * P], combT[:, i * P:(i + 1) * P], b2r[:],
                                  start=True, stop=True)
                mm.then_inc(s["bias_done"], 1)
                e.wait_ge(s["bias_added"], 1)
            e.sem_inc(s["down_done"], 2)
            e.wait_ge(w_in, 64)
            with e.Fori(0, NTB) as tb:
                for ex in range(E + 1):
                    if ex < E:
                        for fc in range(nf):
                            e.wait_ge(s["act_done"], tb * (E * nf) + ex * nf + fc + 1)
                            e.matmul(ps[:, fc, :], up[:, ex, fc * P:(fc + 1) * P], xnT[:, bass.ts(tb, TB)],
                                     start=True, stop=True).then_inc(s["up_done"], 1)
                    if ex >= 1:
                        k = ex - 1
                        e.wait_ge(s["acc_done"], tb * E + k + 1)
                        e.wait_ge(s["act_done"], tb * (E * nf) + (k + 2) * nf)
                        for j in range(TPB):
                            for fc in range(nf):
                                mm = e.matmul(ps[:, 4 + k % 2, j * P:(j + 1) * P],
                                              hid[:, k % 2, fc, j * P:(j + 1) * P], dn[:, k, fc, :],
                                              start=(fc == 0), stop=(fc == nf - 1))
                        mm.then_inc(s["down_done"], 1)

        def turn_tokens(e, s):
            for g in range(NTB):
                for j in range(TPB):
                    e.wait_ge(s["xn_ready"], TPB * g + j + 1)
                    mm = e.transpose(ps[:, 6 + g % 2, j * P:(j + 1) * P], xn[:, TPB * g + j, :], ident[:])
                mm.then_inc(s["tp_done"], 1)
                if g >= 1:
                    e.wait_ge(s["xnT_ready"], g)
            e.wait_ge(s["xnT_ready"], NTB)

        def unit_tensor(e, u, par, main, pre):
            v, vp = u + 1, 1 - par
            if not main:
                v, vp = u, par
            first = not main
            for what, n in order(main, pre):
                if what == "turn":
                    e.wait_ge(AT["unit_split"], v + 1)
                    for c, pad in enumerate((qpad, kpad)):
                        for half in range(2):
                            if c == 1:
                                e.wait_ge(AT["turned_copied"], 6 * v + half + 1)
                            elif not first:
                                e.wait_ge(AT["turned_copied"], 6 * v - 1 + half)
                            for j in range(4):
                                mm = e.transpose(ps[:, half, j * P:(j + 1) * P],
                                                 pad[:, 4 * half + j].rearrange("p h c -> p (h c)"),
                                                 ident[:])
                            mm.then_inc(AT["turned"], 1)
                elif what == "s":
                    h, group, w = s_blocks[n]
                    r = 32 * h
                    if n < 2:
                        e.wait_ge(AT["turned_copied"], 6 * v + 4)
                    else:
                        e.wait_ge(AT["max_done"], NSB * v + n - 1)
                    for k, (i, half) in enumerate(group):
                        diag = i // 4 == half
                        mm = e.matmul(ps[:, n % 2, k * w:(k + 1) * w], qT[r:r + 24, i * P:(i + 1) * P],
                                      kT[r:r + 24, vp, half * 512:half * 512 + w], start=True, stop=not diag)
                        if diag:
                            mm = e.matmul(ps[:, n % 2, (k + 1) * w - P:(k + 1) * w], identb[:], hide_q[:],
                                          start=False, stop=True)
                    mm.then_inc(AT["s_done"], 1)
                elif what == "returned":
                    e.wait_ge(AT["negmax_ready"], v + 1)
                    for half in range(2):
                        for j in range(4):
                            mm = e.transpose(ps[:, half, j * P:(j + 1) * P],
                                             qpad[:, 4 * half + j].rearrange("p h c -> p (h c)"), ident[:])
                        mm.then_inc(AT["turned"], 1)
                elif what == "st":
                    half, j = steps[n]
                    q0, w = span(n)
                    if n == 0:
                        e.wait_ge(AT["turned_copied"], 6 * u + 6)
                    for pair in range(2):
                        e.wait_ge(AT["exp_done"], 2 * NST * u + 2 * n + pair + 1)
                        for h in range(2):
                            r = 32 * (2 * pair + h)
                            bank = 2 + 2 * pair + h
                            diag = j // 4 == half
                            mm = e.matmul(ps[:, bank, 0:w], kT[r:r + 25, par, j * P:(j + 1) * P],
                                          qmT[r:r + 25, par, half * 512 + q0:half * 512 + 512],
                                          start=True, stop=not diag)
                            if diag:
                                mm = e.matmul(ps[:, bank, 0:P], identb[:], hide_k[:], start=False, stop=True)
                        mm.then_inc(AT["st_done"], 1)
                elif what == "pv":
                    half, j = steps[n]
                    q0, w = span(n)
                    e.wait_ge(AT["exp_done"], 2 * NST * u + 2 * n + 4)
                    if j == 0:
                        e.wait_ge(AT["o_normed"], 2 * u + half + 1)
                    for h in range(HG):
                        mm = e.matmul(ps[32 * h:32 * h + 32, 6 + half, q0:512], vpad[:, par, j, h, :],
                                      probT[:, n % 2, h, 0:w], start=(j == 0), stop=(w == P),
                                      skip_group_check=True)
                    mm.then_inc(AT["pv_done"], 1)
                elif what == "oturn":
                    e.wait_ge(AT["o_copied"], 2 * u + n + 1)
                    for j in range(4):
                        mm = e.transpose(ps[:, 6 + n, j * P:(j + 1) * P], oT[:, n, j * P:(j + 1) * P], ident[:])
                    mm.then_inc(AT["o_turned"], 1)

        def attention_tensor(e):
            turn_tokens(e, AT)
            for i in range(NT):
                if i >= 4:
                    e.wait_ge(AT["qkv_copied"], 2 * (i - 3))
                e.matmul(ps[:, i % 4, 0:3 * D], xnT[:, i * P:(i + 1) * P], wqkv[:],
                         start=True, stop=True).then_inc(AT["qkv_done"], 1)
            e.wait_ge(AT["masks_ready"], 3)
            e.wait_ge(AT["qkv_copied"], 2 * NT)
            e.sem_inc(AT["pv_done"], 2)
            unit_tensor(e, 0, 0, False, True)
            with e.Fori(0, NU // 2 - 1) as i:
                unit_tensor(e, 2 * i, 0, True, True)
                unit_tensor(e, 2 * i + 1, 1, True, True)
            unit_tensor(e, NU - 2, 0, True, True)
            unit_tensor(e, NU - 1, 1, True, False)
            e.wait_ge(AT["o_normed"], 2 * NU + 2)
            for g in range(NTB):
                if g >= 2:
                    e.wait_ge(AT["ctxT_ready"], g - 1)
                for j in range(TPB):
                    mm = e.transpose(ps[:, g % 2, j * P:(j + 1) * P], ctxv[:, TPB * g + j, :], ident[:])
                mm.then_inc(AT["ctxT_turned"], 1)
            for g in range(NTB):
                e.wait_ge(AT["ctxT_ready"], g + 1)
                for j in range(TPB):
                    i = TPB * g + j
                    mm = e.matmul(ps[:, 2 + g, j * P:(j + 1) * P], xnT[:, i * P:(i + 1) * P], wo[:],
                                  start=True, stop=True)
                mm.then_inc(AT["proj_done"], 1)

        def scan_spread(e, q, par, g0, t0):
            for c in range(DQ // 8):
                for k in range(2):
                    n = 2 * c + k
                    e.wait_ge(SC["da_done"], 8 * q + n + 1)
                    for j in range(4):
                        r = 8 * c + 4 * k + j
                        mm = e.matmul(ps[:, k, j * TR:(j + 1) * TR], sel[0:ROWS, r % DG, :],
                                      dtp[0:ROWS].rearrange("p g t -> p (g t)")[
                                          :, bass.ds(g0 + r // DG * S + t0, TR)], start=True, stop=True)
                    mm.then_inc(SC["dt_cast"], 1)
                e.wait_ge(SC["in_done"], 4 * q + c + 1)
                for k in range(2):
                    for j in range(4):
                        r = 8 * c + 4 * k + j
                        mm = e.matmul(ps[:, 2 + 2 * (c % 2) + k, j * TR:(j + 1) * TR], sel[0:ROWS, r % DG, :],
                                      upp[0:ROWS].rearrange("p g t -> p (g t)")[
                                          :, bass.ds(g0 + r // DG * S + t0, TR)], start=True, stop=True)
                mm.then_inc(SC["u_cast"], 1)

        def scan_out(e, q, par, tr):
            e.wait_ge(SC["h_done"], q + 3)
            e.wait_ge(SC["c_placed"], 2 * tr + 2)
            e.wait_ge(SC["y_copied"], q + 1)
            h = hs[:, par, :].rearrange("p (d t) -> p d t", t=TR)
            for rb in range(2):
                for k in range(16):
                    for j in range(4):
                        t = rb * 64 + j * 16 + k
                        mm = e.matmul(ps[32 * j:32 * j + 32, 6 + par, rb * DQ:(rb + 1) * DQ], cz[:, t, :], h[:, :, t],
                                      start=(k == 0), stop=(k == 15), skip_group_check=True)
            mm.then_inc(SC["y_done"], 1)

        def scan_tensor(e):
            for g in range(NTB):
                for j in range(TPB):
                    e.wait_ge(SC["xr_ready"], TPB * g + j + 1)
                    mm = e.transpose(ps[:, g % 2, j * P:(j + 1) * P], xr[:, TPB * g + j, :], ident[:])
                mm.then_inc(SC["xr_turned"], 1)
                if g >= 1:
                    e.wait_ge(SC["xrT_ready"], g)
            e.wait_ge(SC["xrT_ready"], NTB)
            for h in range(2):
                for b in range(B):
                    for c in range(2):
                        mm = e.matmul(ps[64 * b:64 * b + 64, 2 + 2 * c + h, :],
                                      xpw[:, RANK + c * STATE:RANK + (c + 1) * STATE],
                                      xnT[:, b * S + h * 512:b * S + (h + 1) * 512], start=True, stop=True)
            mm.then_inc(SC["bc_done"], 1)
            for g in range(NTB):
                if g >= 2:
                    e.wait_ge(SC["loT_ready"], g - 1)
                e.matmul(ps[0:RANK, 6 + g % 2, :], xpw[:, 0:RANK], xnT[:, g * TB:(g + 1) * TB],
                         start=True, stop=True).then_inc(SC["lo_done"], 1)
            e.wait_ge(SC["loT_ready"], NTB)
            e.wait_ge(SC["bT_ready"], 2)
            for g in range(NTB):
                mm = e.matmul(ps[:, g, :], dtw[:], loT[:, g * TB:(g + 1) * TB], start=True, stop=True)
            mm.then_inc(SC["dt_done"], 1)
            e.wait_ge(SC["z_ready"], 1)
            e.wait_ge(SC["sel_ready"], 1)
            e.wait_ge(parts_in, 16 * 12)
            e.sem_inc(SC["y_done"], 2)
            scan_spread(e, 0, 0, 0, 0)
            with e.Fori(0, NSU // 2 - 1) as i:
                scan_spread(e, 2 * i + 1, 1, (i % 2) * (4 * S) + 2 * S, (i // 2) * TR)
                scan_out(e, 2 * i, 0, i // 2)
                scan_spread(e, 2 * i + 2, 0, ((i + 1) % 2) * (4 * S), ((i + 1) // 2) * TR)
                scan_out(e, 2 * i + 1, 1, i // 2)
            scan_spread(e, NSU - 1, 1, 6 * S, (NTR - 1) * TR)
            scan_out(e, NSU - 2, 0, NTR - 1)
            scan_out(e, NSU - 1, 1, NTR - 1)
            for g in range(NTB):
                if g >= 2:
                    e.wait_ge(SC["xsT_ready"], g - 1)
                for j in range(TPB):
                    mm = e.transpose(ps[:, g % 2, j * P:(j + 1) * P], xn[:, TPB * g + j, :], ident[:])
                mm.then_inc(SC["xs_turned"], 1)
            e.wait_ge(SC["y_copied"], NSU + 2)
            for g in range(NTB):
                if g >= 2:
                    e.wait_ge(SC["yT_ready"], g - 1)
                for j in range(TPB):
                    mm = e.transpose(ps[:, 2 + g % 2, j * P:(j + 1) * P], ysb[:, TPB * g + j, :], ident[:])
                mm.then_inc(SC["yT_turned"], 1)
            e.wait_ge(SC["g_ready"], 1)
            for g in range(NTB):
                for j in range(TPB):
                    i = TPB * g + j
                    mm = e.matmul(ps[:, 4 + g, j * P:(j + 1) * P], xnT[:, i * P:(i + 1) * P], opw[:],
                                  start=True, stop=True)
                mm.then_inc(SC["proj_done"], 1)

        @block.tensor
        def _(e):
            e.wait_ge(consts_in, CONSTS)
            for name, kind in plan:
                if kind == "attention":
                    attention_tensor(e)
                elif kind == "scan":
                    scan_tensor(e)
                else:
                    moe_tensor(e, MOE[name], kind)

        def moe_scalar(e, s, kind):
            nf = (F0, F1)[kind] // P
            e.wait_ge(s["var_ready"], 1)
            e.activation(std[:], veps[:], ACT.Sqrt).then_inc(s["std_ready"], 1)
            for g in range(NTB):
                e.wait_ge(s["tp_done"], g + 1)
                e.copy(xnT[:, g * TB:(g + 1) * TB], ps[:, 6 + g % 2, :]).then_inc(s["xnT_ready"], 1)
            e.wait_ge(s["shifted"], 1)
            e.activation(lg[:], lg[:], ACT.Exp).then_inc(s["exp_done"], 1)
            if kind == 1:
                e.wait_ge(s["comb_turned"], 1)
                e.copy(combT, ps[0:E, 0:4, :].rearrange("p a b -> p (a b)")).then_inc(s["combT_ready"], 1)
            e.sem_inc(s["act_done"], nf)
            with e.Fori(0, NTB) as tb:
                for ex in range(E):
                    e.wait_ge(s["down_done"], tb * E + ex + 1)
                    for fc in range(nf):
                        e.wait_ge(s["up_done"], tb * (E * nf) + ex * nf + fc + 1)
                        if kind == 0:
                            a = e.activation(hid[:, ex % 2, fc, :], ps[:, fc, :], ACT.Gelu)
                        else:
                            a = e.activation(hid[:, ex % 2, fc, :], ps[:, fc, :], ACT.Relu, bias=b1c[:, ex, fc:fc + 1])
                        a.then_inc(s["act_done"], 1)

        def unit_scalar(e, u, par, main, pre):
            v, vp = u + 1, 1 - par
            if not main:
                v, vp = u, par
            for what, n in order(main, pre):
                if what == "turn":
                    for c, dst in enumerate((qT, kT)):
                        for half in range(2):
                            e.wait_ge(AT["turned"], 6 * v + 2 * c + half + 1)
                            to = qT[:, half * 512:half * 512 + 512] if c == 0 else \
                                kT[:, vp, half * 512:half * 512 + 512]
                            e.copy(to, ps[:, half, :]).then_inc(AT["turned_copied"], 1)
                elif what == "returned":
                    for half in range(2):
                        e.wait_ge(AT["turned"], 6 * v + 4 + half + 1)
                        e.copy(qmT[:, vp, half * 512:half * 512 + 512],
                               ps[:, half, :]).then_inc(AT["turned_copied"], 1)
                elif what == "st":
                    q0, w = span(n)
                    e.wait_ge(AT["pv_done"], NST * u + n + 1)
                    for pair in range(2):
                        e.wait_ge(AT["st_done"], 2 * NST * u + 2 * n + pair + 1)
                        e.activation(probT[:, n % 2, 2 * pair:2 * pair + 2, 0:w],
                                     ps[:, 2 + 2 * pair:4 + 2 * pair, 0:w], ACT.Exp,
                                     scale=SCALE).then_inc(AT["exp_done"], 1)
                elif what == "ocopy":
                    e.wait_ge(AT["pv_done"], NST * u + (4, NST)[n] + 2)
                    e.copy(oT[:, n, :], ps[:, 6 + n, :]).then_inc(AT["o_copied"], 1)

        def attention_scalar(e):
            e.wait_ge(AT["var_ready"], 1)
            e.activation(std[:], veps[:], ACT.Sqrt).then_inc(AT["std_ready"], 1)
            for g in range(NTB):
                e.wait_ge(AT["tp_done"], g + 1)
                e.copy(xnT[:, g * TB:(g + 1) * TB], ps[:, 6 + g % 2, :]).then_inc(AT["xnT_ready"], 1)
            e.copy(identb[:], ident[:]).then_inc(AT["masks_ready"], 1)
            e.copy(hide_q[:], maskf[:, 0, :]).then_inc(AT["masks_ready"], 1)
            e.copy(hide_k[:], maskf[:, 1, :]).then_inc(AT["masks_ready"], 1)
            e.wait_ge(AT["rotated"], 1)
            e.sem_inc(AT["exp_done"], 2)
            unit_scalar(e, 0, 0, False, True)
            with e.Fori(0, NU // 2 - 1) as i:
                unit_scalar(e, 2 * i, 0, True, True)
                unit_scalar(e, 2 * i + 1, 1, True, True)
            unit_scalar(e, NU - 2, 0, True, True)
            unit_scalar(e, NU - 1, 1, True, False)
            for g in range(NTB):
                e.wait_ge(AT["ctxT_turned"], g + 1)
                e.copy(xnT[:, g * TB:(g + 1) * TB], ps[:, g % 2, :]).then_inc(AT["ctxT_ready"], 1)

        def scan_exp(e, q, par, d0):
            e.wait_ge(SC["h_done"], q + 1)
            for n in range(8):
                e.wait_ge(SC["dt_cast"], 8 * q + n + 1)
                for j in range(4):
                    r = 4 * n + j
                    ins = e.activation(da[:, par, r * TR:(r + 1) * TR], ps[:, n % 2, j * TR:(j + 1) * TR], ACT.Exp,
                                       scale=arate[:, bass.ds(d0 + r, 1)])
                ins.then_inc(SC["da_done"], 1)

        def scan_keep(e, q, par, row, d0):
            e.wait_ge(SC["y_done"], q + 3)
            e.copy(ysb.rearrange("p r d -> p (r d)")[:, bass.ds(row * D + d0, D + DQ)].rearrange(
                "p (r d) -> p r d", d=DQ)[:, 0:D // DQ + 1:D // DQ, :],
                ps[:, 6 + par, 0:2 * DQ].rearrange("p (r d) -> p r d", d=DQ)).then_inc(SC["y_copied"], 1)

        def scan_scalar(e):
            e.wait_ge(SC["var_ready"], 1)
            e.activation(std[:], veps[:], ACT.Sqrt).then_inc(SC["std_ready"], 1)
            e.wait_ge(SC["rms_ready"], 1)
            e.activation(std[:], veps[:], ACT.Sqrt).then_inc(SC["rms_std"], 1)
            for g in range(NTB):
                e.wait_ge(SC["xr_turned"], g + 1)
                e.copy(xnT[:, g * TB:(g + 1) * TB], ps[:, g % 2, :]).then_inc(SC["xrT_ready"], 1)
            e.wait_ge(SC["bc_done"], 1)
            e.copy(bT, ps[:, 2:4, :].rearrange("p a b -> p (a b)")).then_inc(SC["bT_ready"], 1)
            e.copy(cT, ps[:, 4:6, :].rearrange("p a b -> p (a b)")).then_inc(SC["bT_ready"], 1)
            for g in range(NTB):
                e.wait_ge(SC["lo_done"], g + 1)
                e.copy(loT[:, g * TB:(g + 1) * TB], ps[0:RANK, 6 + g % 2, :]).then_inc(SC["loT_ready"], 1)
            e.activation(arate[:], arate[:], ACT.Exp).then_inc(SC["rate_exp"], 1)
            e.wait_ge(SC["z_ready"], 1)
            e.activation(soft, z, ACT.Abs).then_inc(SC["abs_ready"], 1)
            e.wait_ge(SC["abs_ready"], 1)
            e.activation(soft, soft, ACT.Exp, scale=-1.0).then_inc(SC["exp_ready"], 1)
            e.wait_ge(SC["exp_ready"], 1)
            e.activation(soft, soft, ACT.Ln, bias=1.0).then_inc(SC["ln_ready"], 1)
            e.wait_ge(SC["sel_in"], 16)
            e.copy(sel[0:ROWS].rearrange("p r m -> p (r m)"), selftmp[0:ROWS, :]).then_inc(SC["sel_ready"], 1)
            e.wait_ge(SC["prep_done"], 1)
            e.wait_ge(SC["rate_ready"], 1)
            e.wait_ge(parts_out, 32)
            e.sem_inc(SC["da_done"], 2)
            e.sem_inc(SC["y_copied"], 2)
            scan_exp(e, 0, 0, 0)
            with e.Fori(0, NSU // 2 - 1) as i:
                scan_exp(e, 2 * i + 1, 1, (i % 2) * (2 * DQ) + DQ)
                scan_keep(e, 2 * i, 0, (i // 2) * 2, (i % 2) * (2 * DQ))
                scan_exp(e, 2 * i + 2, 0, ((i + 1) % 2) * (2 * DQ))
                scan_keep(e, 2 * i + 1, 1, (i // 2) * 2, (i % 2) * (2 * DQ) + DQ)
            scan_exp(e, NSU - 1, 1, 3 * DQ)
            scan_keep(e, NSU - 2, 0, 2 * NTR - 2, 2 * DQ)
            scan_keep(e, NSU - 1, 1, 2 * NTR - 2, 3 * DQ)
            for g in range(NTB):
                e.wait_ge(SC["xs_turned"], g + 1)
                e.activation(xnT[:, g * TB:(g + 1) * TB], ps[:, g % 2, :], ACT.Copy,
                             scale=dskip[:, 0:1]).then_inc(SC["xsT_ready"], 1)

        @block.scalar
        def _(e):
            e.wait_ge(consts_in, CONSTS)
            for name, kind in plan:
                if kind == "attention":
                    attention_scalar(e)
                elif kind == "scan":
                    scan_scalar(e)
                else:
                    moe_scalar(e, MOE[name], kind)

        @block.gpsimd
        def _(e):
            def split(u, par, tok):
                for c, (pad, again, rest) in enumerate(((qpad, 1, 2), (kpad, 2, 1))):
                    for t in range(ST_):
                        src = rot[:, c].rearrange("p i d -> p (i d)")[:, bass.ds(tok(u) + t * D, HG * HD)].rearrange(
                            "p (h c) -> p h c", h=HG)
                        e.tensor_copy(pad[:, t, :, 0:HD].bitcast(F32R), src).then_inc(AT["parts"], 1)
                        e.tensor_copy(pad[:, t, :, again * HD:(again + 1) * HD].bitcast(F32R), src)
                    e.wait_ge(AT["parts"], 2 * ST_ * u + ST_ * (c + 1))
                    e.sem_inc(AT["waited"], 1)
                    for t in range(ST_):
                        src = rot[:, c].rearrange("p i d -> p (i d)")[:, bass.ds(tok(u) + t * D, HG * HD)].rearrange(
                            "p (h c) -> p h c", h=HG)
                        e.tensor_tensor(pad[:, t, :, rest * HD:(rest + 1) * HD].bitcast(F32R), src, pad[:, t, :, 0:HD],
                                        ALU.subtract)
                for t in range(ST_):
                    src = vall[:].rearrange("p i d -> p (i d)")[:, bass.ds(tok(u) + t * D, HG * HD)].rearrange(
                        "p (h c) -> p h c", h=HG)
                    ins = e.tensor_copy(vpad[:, par, t, :, 0:HD], src)
                ins.then_inc(AT["unit_split"], 1)

            def split_when_free(u, par, tok):
                e.wait_ge(AT["turned"], 6 * u)
                e.wait_ge(AT["pv_done"], NST * (u - 1) + 2)
                e.sem_inc(AT["waited"], 1)
                split(u, par, tok)

            if ("b", "attention") in plan:
                e.memset(qpad[:], 0.0)
                e.memset(kpad[:], 0.0).then_inc(AT["pads_ready"], 1)
                e.memset(vpad[:], 0.0).then_inc(AT["pads_ready"], 1)
                e.wait_ge(AT["pads_ready"], 2)
                e.memset(kpad[:, :, :, 24:25], 1.0)
                e.memset(vpad[:, :, :, :, HD:HD + 1], 1.0)
                e.wait_ge(AT["rotated"], 1)
                first = lambda u: (u // NG) * (ST_ * D) + (u % NG) * (HG * HD)
                split(0, 0, first)
                e.wait_ge(AT["turned"], 6)
                split(1, 1, first)
                with e.Fori(1, NU // 2) as i:
                    split_when_free(2 * i, 0, lambda u: (i // 2) * (ST_ * D) + (i % 2) * (2 * HG * HD))
                    split_when_free(2 * i + 1, 1, lambda u: (i // 2) * (ST_ * D) + (i % 2) * (2 * HG * HD) + HG * HD)

            if ("e", "scan") in plan:
                e.wait_ge(SC["arena_free"], 1)
                e.memset(cz, 0.0).then_inc(SC["c_zeroed"], 1)
                e.wait_ge(SC["c_zeroed"], 1)
                e.sem_inc(SC["waited"], 1)
                e.wait_ge(SC["bT_ready"], 2)
                czf = cz.rearrange("p t c -> p (t c)")

                def place_c(tr):
                    for b in range(B):
                        rows = slice(64 * b, 64 * b + 64)
                        to = czf[rows].rearrange("p (g k) -> p g k", g=TR // 16)[:, :, 16 * b:16 * b + 15 * 33 + 1:33]
                        e.tensor_copy(to, cT[rows, bass.ds(tr * TR, TR)].rearrange("p (g k) -> p g k", k=16)
                                      ).then_inc(SC["c_placed"], 1)
                    e.wait_ge(SC["c_placed"], 2 * tr + 2)
                    e.sem_inc(SC["waited"], 1)

                def cut(q, par):
                    e.wait_ge(SC["da_done"], 8 * q + 8 + 2)
                    e.sem_inc(SC["waited"], 1)
                    e.memset(da[:, par, 0::CHUNK], 0.0).then_inc(SC["da_cut"], 1)

                place_c(0)
                for dq in range(NDQ):
                    cut(dq, dq % 2)
                with e.Fori(1, NTR) as tr:
                    cut(4 * tr, 0)
                    e.wait_ge(SC["da_cut"], 4 * tr + 1)
                    e.wait_ge(SC["y_done"], 4 * tr + 2)
                    e.sem_inc(SC["waited"], 1)
                    place_c(tr)
                    for dq in range(1, NDQ):
                        cut(4 * tr + dq, dq % 2)

        @block.vector
        def _(e):
            def link(ins):
                chained[0] += 1
                ins.then_inc(chain, 1)
                e.wait_ge(chain, chained[0])

            def layernorm(s):
                for i in range(NT):
                    ins = e.bn_stats(stats[:, i, :], x[:, i, :])
                link(ins)
                for i in range(NT):
                    ins = e.bn_aggr(mv[:, i, :], stats[:, i, :])
                link(ins)
                e.tensor_scalar(veps[:], mv[:, :, 1], LN_EPS, None, ALU.add).then_inc(s["var_ready"], 1)
                e.wait_ge(s["std_ready"], 1)
                link(e.reciprocal(rstd[:], std[:]))
                for i in range(NT):
                    e.tensor_scalar(xn[:, i, :], x[:, i, :], mv[:, i, 0:1], rstd[:, i:i + 1],
                                    ALU.subtract, ALU.mult).then_inc(s["xn_ready"], 1)

            def route(s, kind):
                def per_token(v):
                    return v.unsqueeze(2).to_broadcast([P, NT, E])
                e.wait_ge(s["logits_done"], 1)
                link(e.tensor_tensor(lg[:], ps[:, 6, 0:NT * E].rearrange("p (i e) -> p i e", e=E),
                                     rb[kind][:].unsqueeze(1).to_broadcast([P, NT, E]), ALU.add))
                link(e.tensor_reduce(rowmax[:], lg[:], AX.X, ALU.max))
                e.tensor_tensor(lg[:], lg[:], per_token(rowmax[:]), ALU.subtract).then_inc(s["shifted"], 1)
                e.wait_ge(s["exp_done"], 1)
                link(e.tensor_reduce(rowmax[:], lg[:], AX.X, ALU.add))
                link(e.reciprocal(rowmax[:], rowmax[:]))
                link(e.tensor_tensor(probs[:], lg[:], per_token(rowmax[:]), ALU.mult))
                pr = probs[:].rearrange("p i e -> p (i e)")
                mine = pr.unsqueeze(2).to_broadcast([P, NT * E, E])
                beats4 = beats[:].rearrange("p (i e) f -> p i e f", e=E)
                ties4 = ties[:].rearrange("p (i e) f -> p i e f", e=E)
                mine4 = probs[:].unsqueeze(3).to_broadcast([P, NT, E, E])
                other4 = probs[:].unsqueeze(2).to_broadcast([P, NT, E, E])
                e.tensor_tensor(beats4, other4, mine4, ALU.is_gt)
                link(e.tensor_tensor(ties4, other4, mine4, ALU.is_equal))
                link(e.tensor_tensor(ties4, ties4, earlier[:].unsqueeze(1).to_broadcast([P, NT, E, E]), ALU.mult))
                link(e.tensor_tensor(beats[:], beats[:], ties[:], ALU.add))
                link(e.tensor_reduce(rank[:].rearrange("p i e -> p (i e)"), beats[:], AX.X, ALU.add))
                link(e.tensor_scalar(rank[:], rank[:], float((2, 1)[kind]), 0.5, ALU.is_lt, ALU.mult))
                link(e.tensor_tensor(comb[:], probs[:], rank[:], ALU.mult))
                e.sem_inc(s["comb_ready"], 1)
                if kind == 1:
                    e.wait_ge(s["bias_done"], 1)
                    e.tensor_tensor(xf, xf, ps[:, 0:4, :].rearrange("p a b -> p (a b)"),
                                    ALU.add).then_inc(s["bias_added"], 1)
                    e.wait_ge(s["bias_added"], 1)

            def moe_vector(s, kind):
                layernorm(s)
                route(s, kind)
                e.sem_inc(s["acc_done"], 2)
                with e.Fori(0, NTB) as tb:
                    for ex in range(E):
                        e.wait_ge(s["acc_done"], tb * E + ex + 2)
                        e.wait_ge(s["down_done"], tb * E + ex + 3)
                        for j in range(TPB):
                            xs = xf[:, bass.ds(tb * TB + j * P, P)]
                            ins = e.scalar_tensor_tensor(out=xs, in0=ps[:, 4 + ex % 2, j * P:(j + 1) * P],
                                                         scalar=combf[:, bass.ds(tb * (TPB * E) + j * E + ex, 1)],
                                                         in1=xs, op0=ALU.mult, op1=ALU.add)
                        ins.then_inc(s["acc_done"], 1)
                e.wait_ge(s["acc_done"], ACC_END)

            def unit_vector(u, par, main, pre, b):
                v = u + 1 if main else u
                for what, n in order(main, pre):
                    if what == "s":
                        h, group, w = s_blocks[n]
                        ng = len(group)
                        at = [i * HG * 2 + h * 2 + half for i, half in group]
                        e.wait_ge(AT["s_done"], NSB * v + n + 1)
                        e.tensor_reduce(maxf[:, at[0]:at[-1] + 1:max(1, at[-1] - at[0])],
                                        ps[:, n % 2, 0:ng * w].rearrange("p (g k) -> p g k", g=ng),
                                        AX.X, ALU.max).then_inc(AT["max_done"], 1)
                        if n == NSB - 1:
                            e.wait_ge(AT["max_done"], NSB * v + NSB)
                            e.tensor_reduce(qpad[:, :, :, 24].bitcast(F32R), maxima[:], AX.X, ALU.max,
                                            negate=True).then_inc(AT["negmax_ready"], 1)
                    elif what == "oturn":
                        e.wait_ge(AT["o_turned"], 2 * u + n + 1)
                        o = ps[:, 6 + n, :].rearrange("p (i h c) -> p i h c", i=4, h=HG)
                        e.wait_ge(AT["o_normed"], 2 * u + n + 2)
                        ins = e.reciprocal(osum[:], o[:, :, :, HD:HD + 1])
                        ins.then_inc(AT["o_summed"], 1)
                        e.wait_ge(AT["o_summed"], 2 * u + n + 1)
                        t0 = b(u)
                        for i in range(4):
                            ins = e.tensor_tensor(
                                ctxv.rearrange("p i d -> p (i d)")[:, bass.ds(t0 + (4 * n + i) * D, HG * HD)].rearrange(
                                    "p (h c) -> p h c", h=HG),
                                o[:, i, :, 0:HD], osum[:, i, :, :].to_broadcast([P, HG, HD]), ALU.mult)
                        ins.then_inc(AT["o_normed"], 1)

            def attention_vector():
                layernorm(AT)
                for i in range(NT):
                    e.wait_ge(AT["qkv_done"], i + 1)
                    e.tensor_tensor(qk[:, i].rearrange("p c d -> p (c d)"), ps[:, i % 4, 0:2 * D], bqkv[:, 0:2 * D],
                                    ALU.add).then_inc(AT["qkv_copied"], 1)
                    e.tensor_tensor(vall[:, i, :], ps[:, i % 4, 2 * D:3 * D], bqkv[:, 2 * D:3 * D],
                                    ALU.add).then_inc(AT["qkv_copied"], 1)
                e.wait_ge(AT["qkv_copied"], 2 * NT)
                half = D // 2
                t1 = rtmp[:, 0:ST_ * half].rearrange("p (i f) -> p i f", f=half)
                t2 = rtmp[:, ST_ * half:2 * ST_ * half].rearrange("p (i f) -> p i f", f=half)
                for c in range(2):
                    for b in range(B):
                        tiles = slice(b * ST_, (b + 1) * ST_)
                        even, odd = qk[:, tiles, c, 0::2], qk[:, tiles, c, 1::2]
                        for part, (ea, oa) in enumerate(((cos, sin), (sin, cos))):
                            e.tensor_tensor(t1, even, ea[:], ALU.mult)
                            link(e.tensor_tensor(t2, odd, oa[:], ALU.mult))
                            link(e.tensor_tensor(rot[:, c, tiles, part * half:(part + 1) * half], t1, t2,
                                                 ALU.subtract))
                link(e.memset(maxima[:], MASKED))
                e.sem_inc(AT["rotated"], 1)
                e.sem_inc(AT["o_normed"], 2)
                first = lambda u: (u // NG) * (ST_ * D) + (u % NG) * (HG * HD)
                unit_vector(0, 0, False, True, first)
                with e.Fori(0, NU // 2 - 1) as i:
                    unit_vector(2 * i, 0, True, True, lambda u: (i // 2) * (ST_ * D) + (i % 2) * (2 * HG * HD))
                    unit_vector(2 * i + 1, 1, True, True,
                                lambda u: (i // 2) * (ST_ * D) + (i % 2) * (2 * HG * HD) + HG * HD)
                unit_vector(NU - 2, 0, True, True, first)
                unit_vector(NU - 1, 1, True, False, first)
                for g in range(NTB):
                    e.wait_ge(AT["proj_done"], g + 1)
                    xs = xf[:, g * TB:(g + 1) * TB]
                    e.tensor_tensor(xs, xs, ps[:, 2 + g, :], ALU.add).then_inc(AT["proj_added"], 1)
                e.wait_ge(AT["proj_added"], NTB)
                link(e.tensor_tensor(x[:], x[:], bo[:].unsqueeze(1).to_broadcast([P, NT, D]), ALU.add))

            def scan_unit(q, par, t0):
                for c in range(DQ // 8):
                    e.wait_ge(SC["u_cast"], 4 * q + c + 1)
                    if c == 0:
                        e.wait_ge(SC["y_done"], q + 1)
                    e.tensor_tensor(hs[:, par, c * 8 * TR:(c + 1) * 8 * TR].rearrange("p (d t) -> p d t", t=TR),
                                    ps[:, 2 + 2 * (c % 2):4 + 2 * (c % 2), :].rearrange("p a (d t) -> p (a d) t", t=TR),
                                    bT[:, bass.ds(t0, TR)].unsqueeze(1).to_broadcast([P, 8, TR]),
                                    ALU.mult).then_inc(SC["in_done"], 1)
                e.wait_ge(SC["da_cut"], q + 1)
                e.wait_ge(SC["in_done"], 4 * q + 4 + 2)
                e.tensor_tensor_scan(hs[:, par, :], da[:, par, :], hs[:, par, :], 0.0, ALU.mult,
                                     ALU.add).then_inc(SC["h_done"], 1)

            def scan_vector():
                layernorm(SC)
                e.wait_ge(SC["xn_ready"], NT)
                e.wait_ge(w_in, 64)
                e.sem_inc(SC["arena_free"], 1)
                link(e.tensor_tensor(std[:], rstd[:], rstd[:], ALU.mult))
                link(e.tensor_tensor(std[:], std[:], mv[:, :, 1], ALU.mult))
                e.tensor_scalar(veps[:], std[:], RMS_EPS, None, ALU.add).then_inc(SC["rms_ready"], 1)
                e.wait_ge(SC["rms_std"], 1)
                link(e.reciprocal(rstd[:], std[:]))
                for i in range(NT):
                    e.scalar_tensor_tensor(out=xr[:, i, :], in0=xn[:, i, :], scalar=rstd[:, i:i + 1], in1=nw[:],
                                           op0=ALU.mult, op1=ALU.mult).then_inc(SC["xr_ready"], 1)
                e.wait_ge(SC["rate_exp"], 1)
                e.tensor_scalar(arate[:], arate[:], -1.0, None, ALU.mult).then_inc(SC["rate_ready"], 1)
                e.wait_ge(SC["dt_done"], 1)
                e.tensor_scalar(z, ps[:, 0:4, :].rearrange("p a b -> p (a b)"), dtb[:, 0:1], None,
                                ALU.add).then_inc(SC["z_ready"], 1)
                e.wait_ge(SC["ln_ready"], 1)
                link(e.scalar_tensor_tensor(out=z, in0=z, scalar=0.0, in1=soft, op0=ALU.max, op1=ALU.add))
                link(e.tensor_tensor(xnT[:], z, xnT[:], ALU.mult))
                for v, full in enumerate((z, xnT[:])):
                    link(e.tensor_copy(parts[:, v, 0, :], full))
                    link(e.tensor_tensor(full, full, parts[:, v, 0, :], ALU.subtract))
                    link(e.tensor_copy(parts[:, v, 1, :], full))
                    link(e.tensor_tensor(full, full, parts[:, v, 1, :], ALU.subtract))
                    e.tensor_copy(parts[:, v, 2, :], full).then_inc(SC["split"], 1)
                e.wait_ge(SC["split"], 2)
                e.wait_ge(parts_out, 32)
                e.wait_ge(SC["sel_ready"], 1)
                e.sem_inc(SC["prep_done"], 1)
                e.sem_inc(SC["in_done"], 2)
                e.sem_inc(SC["h_done"], 2)
                scan_unit(0, 0, 0)
                with e.Fori(0, NSU // 2 - 1) as i:
                    scan_unit(2 * i + 1, 1, (i // 2) * TR)
                    scan_unit(2 * i + 2, 0, ((i + 1) // 2) * TR)
                scan_unit(NSU - 1, 1, (NTR - 1) * TR)
                e.wait_ge(SC["xsT_ready"], NTB)
                for g in range(NTB):
                    e.wait_ge(SC["yT_turned"], g + 1)
                    for k in range(TPB):
                        row = TPB * g + k
                        xv = xnT[:].rearrange("p (b r j t) -> p r j b t", b=B, r=2 * NTR, j=4)[:, row]
                        yv = ps[:, 2 + g % 2, k * P:(k + 1) * P].rearrange("p (j b t) -> p j b t", j=4, b=B)
                        ins = e.tensor_tensor(xv, xv, yv, ALU.add)
                    ins.then_inc(SC["yT_ready"], 1)
                e.wait_ge(SC["yT_ready"], NTB)
                e.sem_inc(SC["g_ready"], 1)
                for g in range(NTB):
                    e.wait_ge(SC["proj_done"], g + 1)
                    xs = xf[:, g * TB:(g + 1) * TB]
                    e.tensor_tensor(xs, xs, ps[:, 4 + g, :], ALU.add).then_inc(SC["proj_added"], 1)
                e.wait_ge(SC["proj_added"], NTB)

            e.wait_ge(x_in, 16)
            e.wait_ge(consts_in, CONSTS)
            for name, kind in plan:
                if kind == "attention":
                    attention_vector()
                elif kind == "scan":
                    scan_vector()
                else:
                    moe_vector(MOE[name], kind)
            e.sem_inc(x_final, 1)


def constants():
    e = np.arange(E)
    n = np.arange(P)
    freq = np.power(np.float32(10000.0), np.float32(-2.0) * np.arange(D // 2, dtype=np.float32) / np.float32(D))
    angle = np.arange(S, dtype=np.float32)[:, None] * freq[None, :].astype(np.float32)
    tiled = lambda v: v.astype(np.float32).reshape(ST_, P, D // 2).transpose(1, 0, 2)
    later = np.where(n[None, :] > n[:, None], np.float32(MASKED), np.float32(0.0))
    k = np.arange(ROWS)
    same_r = (k % DG)[:, None, None] == np.arange(DG)[None, :, None]
    same_b = (k // (3 * DG))[:, None, None] == (np.arange(P) // STATE)[None, None, :]
    return {
        "sel": (same_r & same_b).astype(np.float32).reshape(ROWS, DG * P),
        "cos": tiled(np.cos(angle)), "sin": tiled(np.sin(angle)),
        "masks": np.stack([later, later.T], axis=1),
        "ident": np.eye(P, dtype=np.float32),
        "earlier": (e[None, :] < e[:, None]).astype(np.float32),
    }


def kernel(**inputs):
    import concourse.bacc as bacc
    from concourse.bass_utils import run_bass_kernel_spmd as run

    def a(name):
        return np.asarray(inputs[name])

    arrays = {
        "x": a("L0_attn_x").reshape(T, D),
        "rw0": a("L0_ffn_router_w"), "rb0": a("L0_ffn_router_b"),
        "up0": a("L0_ffn_expert_up").transpose(2, 0, 1),
        "dn0": a("L0_ffn_expert_down").reshape(E, D, F0 // P, P).transpose(3, 0, 2, 1),
        "rw1": a("L1_ffn_w_router"), "rb1": a("L1_ffn_b_router"),
        "up1": a("L1_ffn_w1").transpose(1, 0, 2),
        "dn1": a("L1_ffn_w2").reshape(E, F1 // P, P, D).transpose(2, 0, 1, 3),
        "b1": a("L1_ffn_b1").reshape(E, F1 // P, P).transpose(2, 0, 1),
        "b2": a("L1_ffn_b2"),
        "xpw": a("L1_attn_x_proj_w").T, "dtw": a("L1_attn_dt_proj_w").T,
        "dtb": a("L1_attn_dt_proj_b").reshape(D, 1), "dskip": a("L1_attn_D").reshape(D, 1),
        "opw": a("L1_attn_out_proj_w").T, "norm_w": a("L1_attn_norm_w"),
        "a_log": np.concatenate([a("L1_attn_A_log").T] * B, axis=0),
        "wqkv": np.concatenate([a("L0_attn_Wq"), a("L0_attn_Wk"), a("L0_attn_Wv")], axis=1),
        "bq": a("L0_attn_bq"), "bk": a("L0_attn_bk"), "bv": a("L0_attn_bv"),
        "wo": a("L0_attn_Wo"), "bo": a("L0_attn_bo"),
        **constants(),
    }
    arrays = {f"{k}_dram": np.ascontiguousarray(v) for k, v in arrays.items()}
    nc = bacc.Bacc("TRN2", target_bir_lowering=False, num_devices=1)
    t_in = {k[:-5]: nc.dram_tensor(k, v.shape, mybir.dt.from_np(v.dtype), kind="ExternalInput").ap()
            for k, v in arrays.items()}
    out = nc.dram_tensor("out_dram", (T, D), F32, kind="ExternalOutput").ap()
    scratch = nc.dram_tensor("parts_dram", (2, 3, D, T), BF16, kind="Internal").ap()
    build(nc, t_in, scratch, out)
    r = run(nc, [arrays], core_ids=[0])
    return r.results[0]["out_dram"].reshape(B, S, D)
```

```python
from contextlib import ExitStack

import numpy as np

import concourse.bass as bass
from concourse import mybir

ACT = mybir.ActivationFunctionType
ALU = mybir.AluOpType
AX = mybir.AxisListType
F32 = mybir.dt.float32
F32R = mybir.dt.float32r
BF16 = mybir.dt.bfloat16

P = 128
D = 128
B, S = 2, 1024
T = B * S
NT = T // P
TB = 512
NTB = T // TB
TPB = TB // P
E = 8
F0 = 512
F1 = 256
LN_EPS = 1e-5
H, HD = 16, 8
HG = 4
HR = 64
HP = P // HR
Q_PARTS = ((0, 8, 40), (16, 24), (48,))
K_PARTS = ((0, 16, 48), (8, 24), (40,))
AT_MAX = 32
NG = H // HG
NU = B * NG
ST_ = S // P
SCALE = HD ** -0.5
MASKED = -1e30
STATE = 64
RANK = 8
CHUNK = 64
RMS_EPS = 1e-6
TR, DQ = 128, 32
NTR, NDQ = S // TR, D // DQ
NSU = NTR * NDQ
DG = 16
ROWS = B * 3 * DG
QT = S // 4
ARENA = 153 * 256
PLAN = [("a", 0), ("b", "attention"), ("c", 0), ("d", 1), ("e", "scan"), ("f", 1)]
CONSTS = 16 * 24
ACC_END = NTB * E + 2


def build(nc, t_in, scratch, out):
    with ExitStack() as ctx:
        def sb(name, shape, dt=F32):
            return ctx.enter_context(nc.sbuf_tensor(name, shape, dt))

        def sem(name):
            return ctx.enter_context(nc.semaphore(name))

        x = sb("x", [P, NT, D])
        xf = x[:].rearrange("p i d -> p (i d)")
        xn = sb("xn", [P, NT, D])
        xnT = sb("xnT", [P, T])
        ident = sb("ident", [P, P])
        stats = sb("stats", [P, NT, 6])
        mv = sb("mv", [P, NT, 2])
        veps = sb("veps", [P, NT])
        std = sb("std", [P, NT])
        rstd = sb("rstd", [P, NT])
        lg = sb("lg", [P, NT, E])
        rowmax = sb("rowmax", [P, NT])
        probs = sb("probs", [P, NT, E])
        earlier = sb("earlier", [P, E, E])
        rank = sb("rank", [P, NT, E])
        comb = sb("comb", [P, NT, E])
        combf = comb[:].rearrange("p i e -> p (i e)")
        rw = [sb("rw0", [P, E]), sb("rw1", [P, E])]
        rb = [sb("rb0", [P, E]), sb("rb1", [P, E])]
        b1c = sb("b1c", [P, E, F1 // P])
        b2r = sb("b2r", [E, D])
        wqkv = sb("wqkv", [P, 3 * D])
        bqkv = sb("bqkv", [P, 3 * D])
        wo = sb("wo", [P, D])
        bo = sb("bo", [P, D])
        identb = sb("identb", [P, P], BF16)
        hide_q = sb("hide_q", [P, P], BF16)
        hide_k = sb("hide_k", [P, P], BF16)
        maxima = sb("maxima", [P, ST_, HG, 2])
        maxf = maxima[:].rearrange("p i h t -> p (i h t)")
        negmax = sb("negmax", [P, ST_, HG])
        osum = sb("osum", [P, 4, HG, 1])
        xpw = sb("xpw", [P, RANK + 2 * STATE])
        dtw = sb("dtw", [RANK, D])
        dtb = sb("dtb", [P, 1])
        dskip = sb("dskip", [P, 1])
        nw = sb("nw", [P, D])
        opw = sb("opw", [P, D])
        arate = sb("arate", [P, D])
        up1 = sb("up1", [P, E, F1])
        dn1 = sb("dn1", [P, E, F1 // P, D])

        arena = sb("arena", [P, ARENA])
        top = [0]

        def carve(n):
            top[0] += n
            assert top[0] <= ARENA, top[0]
            return arena[:, top[0] - n:top[0]]

        hidf = carve(2 * F0 // P * TB)
        hid = hidf.rearrange("p (a c t) -> p a c t", a=2, c=F0 // P)
        beats = carve(NT * E * E).rearrange("p (r e) -> p r e", e=E)
        tiesf = carve(NT * E * E)
        ties = tiesf.rearrange("p (r e) -> p r e", e=E)
        spare = carve(2 * T - NT * E * E)
        combT = arena[0:E, top[0] - T:top[0]]
        up0 = carve(E * F0).rearrange("p (e f) -> p e f", e=E)
        dn0 = carve(F0 // P * E * D).rearrange("p (e c d) -> p e c d", e=E, c=F0 // P)
        rtmp = hidf
        qkf = carve(NT * 2 * D)
        qk = qkf.rearrange("p (i c d) -> p i c d", c=2, d=D)
        probT = qkf.rearrange("p (s h q) -> p s h q", s=2, h=HG)
        rot = carve(2 * T + P)
        rotv = rot[:, 0:2 * T].rearrange("p (c i d) -> p c i d", c=2, d=D)
        vflat = carve(T + P)
        vall = vflat[:, 0:T].rearrange("p (i d) -> p i d", d=D)
        cos = carve(ST_ * D // 2).rearrange("p (i f) -> p i f", i=ST_)
        sin = carve(ST_ * D // 2).rearrange("p (i f) -> p i f", i=ST_)
        maskf = carve(2 * P).rearrange("p (a b) -> p a b", a=2)
        ctxv = xn[:]
        pads = [carve(2 * ST_ * HG * HR // 2).bitcast(BF16).rearrange("p (s i h c) -> p s i h c", s=2, i=ST_, h=HG)
                for _ in range(2)]
        qpad, kpad = pads
        rests = [carve(ST_ * HG * HD).rearrange("p (i h c) -> p i h c", i=ST_, h=HG) for _ in range(2)]
        qm = carve(2 * HG // HP * S // 2).bitcast(BF16).rearrange("p (s a t) -> p s a t", s=2, t=S)
        kz = hidf.bitcast(BF16).rearrange("p (s h t) -> p s h t", s=2, h=HG)
        qzf = arena[:, 2 * F0 // P * TB:2 * F0 // P * TB + 2 * T]
        qz = qzf[:, 0:T].bitcast(BF16).rearrange("p (h t) -> p h t", h=HG)
        qT = qzf[:, T:T + S].bitcast(BF16).rearrange("p (a t) -> p a t", t=S)
        kT = qzf[:, T + S:T + 2 * S].bitcast(BF16).rearrange("p (a t) -> p a t", t=S)
        vpad = carve(2 * ST_ * HG * 32).rearrange("p (s i h c) -> p s i h c", s=2, i=ST_, h=HG)
        oT = carve(2 * 512).rearrange("p (a q) -> p a q", a=2)
        top[0] = 0
        dtp = carve(D // DG * S // 2).bitcast(BF16).rearrange("p (g t) -> p g t", t=S)
        upp = carve(D // DG * S // 2).bitcast(BF16).rearrange("p (g t) -> p g t", t=S)
        sel = carve(DG * P // 2).bitcast(BF16).rearrange("p (r m) -> p r m", m=P)
        bT = carve(S)
        cT = carve(S)
        cz = carve(TR * 32).rearrange("p (t c) -> p t c", c=32)
        ysb = carve(2 * D).rearrange("p (r d) -> p r d", d=D)
        yT = carve(B * TR).rearrange("p (b t) -> p b t", b=B)
        parts = carve(3 * 2 * QT).bitcast(BF16).rearrange("p (v a b t) -> p v a b t", v=2, a=3, b=B)
        prep0 = top[0]
        da = carve(2 * DQ * TR).rearrange("p (s n) -> p s n", s=2)
        hs = carve(2 * DQ * TR).rearrange("p (s n) -> p s n", s=2)
        top[0] = prep0
        xr = carve(T).rearrange("p (i d) -> p i d", d=D)
        xd = carve(T)
        soft = carve(T).rearrange("p (b t) -> p b t", b=B)
        loT = carve(T)[0:RANK].rearrange("p (k t) -> p k t", k=4)
        selftmp = carve(DG * P)
        zt = xn[:].rearrange("p i d -> p (i d)").rearrange("p (b t) -> p b t", b=B)
        ut = xnT[:].rearrange("p (b t) -> p b t", b=B)
        ps = ctx.enter_context(nc.psum_tensor("ps", [P, 8, 512], F32))

        consts_in = sem("consts_in")
        x_in = sem("x_in")
        w_in = sem("w_in")
        stored = sem("stored")
        x_final = sem("x_final")
        parts_out = sem("parts_out")
        parts_in = sem("parts_in")
        chain = sem("chain")
        chained = [0]
        pool_step = sem("pool_step")
        pool_steps = [0]

        MOE = {}
        for name in ("a", "c", "d", "f"):
            MOE[name] = {k: sem(f"{name}_{k}") for k in (
                "var_ready", "std_ready", "xn_ready", "tp_done", "xnT_ready", "logits_done", "shifted",
                "exp_done", "comb_ready", "comb_turned", "combT_ready", "bias_done", "bias_added", "up_done", "act_done", "down_done", "acc_done")}
        AT = {k: sem(f"att_{k}") for k in (
            "var_ready", "std_ready", "xn_ready", "tp_done", "xnT_ready", "qkv_done", "qkv_copied", "rotated",
            "masks_ready", "pads_ready", "pads_clear", "parts", "waited", "unit_split", "v_placed", "turned", "turned_copied", "returned",
            "returned_copied", "qz_ready", "kz_ready", "s_done", "max_done", "max_part", "negmax_ready",
            "st_done", "exp_done", "pv_done", "o_copied", "o_turned", "o_summed", "o_normed", "ctxT_turned", "ctxT_ready",
            "proj_done", "proj_added")}
        SC = {k: sem(f"scan_{k}") for k in (
            "var_ready", "std_ready", "xn_ready", "arena_free", "sel_in", "sel_ready", "rms_ready", "rms_std", "xr_ready",
            "xr_turned", "xrT_ready", "rows_zeroed", "c_zeroed", "xn_turned", "xd_ready", "bc_done", "lo_done", "bT_ready",
            "c_placed", "waited", "loT_ready", "dt_done", "z_ready", "exp_ready", "ln_ready", "rate_exp", "rate_ready", "u_ready",
            "split0", "split1", "skip_done", "prep_done", "dt_cast", "da_done", "da_cut", "u_cast", "in_done", "h_done", "y_done",
            "y_copied", "y_turned", "yT_ready", "proj_done", "proj_added")}
        plan = PLAN

        block = ctx.enter_context(nc.Block())

        s_blocks = [(h, group, w)
                    for group, w in [([(0, 0), (4, 1)], P), ([(1, 0), (5, 1)], 2 * P), ([(2, 0)], 3 * P),
                                     ([(3, 0)], 4 * P), ([(6, 1)], 3 * P), ([(7, 1)], 4 * P)]
                    + [([(i, 0)], 4 * P) for i in range(4, ST_)]
                    for h in range(HG)]
        NSB = len(s_blocks)
        steps = [(0, j) for j in range(4)] + [(1, j) for j in range(ST_)]
        NST = len(steps)
        NTU = 2 * HG // HP * 2
        NRE = NTU // 2

        def span(m):
            half, j = steps[m]
            q0 = max(0, j * P - half * 512)
            return q0, 512 - q0

        def piece(n):
            return n // 2 % (HG // HP), n % 2

        def turn_items(v):
            return [("turn", v, n) for n in range(NTU)]

        def order(prev, pre, ahead):
            blocks = [("s", 1, n) for n in range(NSB)] if pre else []
            turns = turn_items(2) if ahead else []
            back = [("returned", 1, n) for n in range(NRE)] if pre else []
            for m in range(NST):
                side = []
                if m < NST - 3:
                    side = blocks[NSB * m // (NST - 3):NSB * (m + 1) // (NST - 3)]
                elif m == NST - 3:
                    side = turns[0:NRE]
                elif m == NST - 2:
                    side = back
                else:
                    side = turns[NRE:]
                yield ("st", 0, 2 * m)
                yield from side[0:len(side) // 2]
                yield ("st", 0, 2 * m + 1)
                if m >= 1:
                    yield ("pv", 0, m - 1)
                elif prev:
                    yield ("pv", -1, NST - 1)
                yield from side[len(side) // 2:]
                if m == 1 and prev:
                    yield ("ocopy", -1, 1)
                if m == 2 and prev:
                    yield ("oturn", -1, 1)
                if m == 2 and pre:
                    yield ("kz", 1, 0)
                if m == 5:
                    yield ("ocopy", 0, 0)
                if m == 6:
                    yield ("oturn", 0, 0)

        def opening():
            yield from turn_items(0)
            yield from [("s", 0, n) for n in range(NSB)]
            yield ("kz", 0, 0)
            yield from turn_items(1)[0:NRE]
            yield from [("returned", 0, n) for n in range(NRE)]
            yield from turn_items(1)[NRE:]

        closing = [("pv", -1, NST - 1), ("ocopy", -1, 1), ("oturn", -1, 1)]

        def units(go):
            def word(i, k):
                return (i + k // 2) // 2 * (ST_ * D) + (i + k // 2) % 2 * (2 * HG * HD) + k % 2 * (HG * HD)
            go(opening(), 0, 0, lambda k: word(0, k), True)
            go(order(False, True, True), 0, 0, lambda k: word(0, k))
            with go.engine.Fori(0, (NU - 4) // 2) as i:
                go(order(True, True, True), 2 * i + 1, 1, lambda k: word(i, 1 + k))
                go(order(True, True, True), 2 * i + 2, 0, lambda k: word(i, 2 + k))
            go(order(True, True, True), NU - 3, 1, lambda k: word(0, NU - 3 + k))
            go(order(True, True, False), NU - 2, 0, lambda k: word(0, NU - 2 + k))
            go(order(True, False, False), NU - 1, 1, lambda k: word(0, NU - 1 + k))
            go(closing, NU, 0, lambda k: word(0, NU + k))

        @block.sync
        def _(sp):
            sp.dma_start(x[:], t_in["x"].rearrange("(i p) d -> p i d", p=P)).then_inc(x_in, 16)
            for dst, name in ((ident[:], "ident"), (rw[0][:], "rw0"), (rw[1][:], "rw1"), (b2r[:], "b2")):
                sp.dma_start(dst, t_in[name]).then_inc(consts_in, 16)
            sp.dma_start(rb[0][:], t_in["rb0"].partition_broadcast(P)).then_inc(consts_in, 16)
            sp.dma_start(rb[1][:], t_in["rb1"].partition_broadcast(P)).then_inc(consts_in, 16)
            sp.dma_start(earlier[:], t_in["earlier"].partition_broadcast(P)).then_inc(consts_in, 16)
            sp.dma_start(b1c[:], t_in["b1"]).then_inc(consts_in, 16)
            for dst, name in ((wqkv, "wqkv"), (wo, "wo"), (cos, "cos"), (sin, "sin"), (maskf, "masks")):
                sp.dma_start(dst[:], t_in[name]).then_inc(consts_in, 16)
            for n, name in enumerate(("bq", "bk", "bv")):
                sp.dma_start(bqkv[:, n * D:(n + 1) * D], t_in[name].partition_broadcast(P)).then_inc(consts_in, 16)
            sp.dma_start(bo[:], t_in["bo"].partition_broadcast(P)).then_inc(consts_in, 16)
            for dst, name in ((xpw, "xpw"), (dtw, "dtw"), (dtb, "dtb"), (dskip, "dskip"), (opw, "opw"),
                              (arate, "a_log")):
                sp.dma_start(dst[:], t_in[name]).then_inc(consts_in, 16)
            sp.dma_start(nw[:], t_in["norm_w"].partition_broadcast(P)).then_inc(consts_in, 16)
            for dst, name in ((up0, "up0"), (dn0, "dn0"), (up1, "up1"), (dn1, "dn1")):
                sp.dma_start(dst[:], t_in[name]).then_inc(w_in, 16)
            if ("e", "scan") in plan:
                sp.wait_ge(SC["arena_free"], 1)
                sp.dma_start(selftmp[0:ROWS, :], t_in["sel"]).then_inc(SC["sel_in"], 16)
                for k in range(4):
                    for v, dst in enumerate((dtp, upp)):
                        sp.wait_ge(SC[f"split{v}"], k + 1)
                        sp.dma_start(scratch[k, v].rearrange("a d b t -> d a b t"), parts[:, v]).then_inc(parts_out, 16)
                        sp.wait_ge(parts_out, 16 * (2 * k + v + 1))
                        for b in range(B):
                            for a in range(3):
                                r0 = (b * 3 + a) * DG
                                sp.dma_start(dst[r0:r0 + DG, :, k * QT:(k + 1) * QT],
                                             scratch[k, v, a, :, b].rearrange("(g r) t -> r g t", r=DG)
                                             ).then_inc(parts_in, 16)
            sp.wait_ge(x_final, 1)
            sp.dma_start(out.rearrange("(i p) d -> p i d", p=P), x[:]).then_inc(stored, 16)
            sp.wait_ge(stored, 16)

        def moe_tensor(e, s, kind):
            nf = (F0, F1)[kind] // P
            up, dn = ((up0, dn0), (up1, dn1))[kind]
            turn_tokens(e, s)
            for i in range(NT):
                mm = e.matmul(ps[:, 6, i * E:(i + 1) * E], xnT[:, i * P:(i + 1) * P], rw[kind][:],
                              start=True, stop=True)
            mm.then_inc(s["logits_done"], 1)
            if kind == 1:
                e.wait_ge(s["comb_ready"], 1)
                for i in range(NT):
                    mm = e.transpose(ps[0:E, i // TPB, i % TPB * P:(i % TPB + 1) * P], comb[:, i, :], ident[:])
                mm.then_inc(s["comb_turned"], 1)
                e.wait_ge(s["combT_ready"], 1)
                for i in range(NT):
                    mm = e.matmul(ps[:, i // TPB, i % TPB * P:(i % TPB + 1) * P], combT[:, i * P:(i + 1) * P], b2r[:],
                                  start=True, stop=True)
                mm.then_inc(s["bias_done"], 1)
                e.wait_ge(s["bias_added"], 1)
            e.sem_inc(s["down_done"], 2)
            e.wait_ge(w_in, 64)
            with e.Fori(0, NTB) as tb:
                for ex in range(E + 1):
                    if ex < E:
                        for fc in range(nf):
                            e.wait_ge(s["act_done"], tb * (E * nf) + ex * nf + fc + 1)
                            e.matmul(ps[:, fc, :], up[:, ex, fc * P:(fc + 1) * P], xnT[:, bass.ts(tb, TB)],
                                     start=True, stop=True).then_inc(s["up_done"], 1)
                    if ex >= 1:
                        k = ex - 1
                        e.wait_ge(s["acc_done"], tb * E + k + 1)
                        e.wait_ge(s["act_done"], tb * (E * nf) + (k + 2) * nf)
                        for j in range(TPB):
                            for fc in range(nf):
                                mm = e.matmul(ps[:, 4 + k % 2, j * P:(j + 1) * P],
                                              hid[:, k % 2, fc, j * P:(j + 1) * P], dn[:, k, fc, :],
                                              start=(fc == 0), stop=(fc == nf - 1))
                        mm.then_inc(s["down_done"], 1)

        def turn_tokens(e, s):
            for g in range(NTB):
                for j in range(TPB):
                    e.wait_ge(s["xn_ready"], TPB * g + j + 1)
                    mm = e.transpose(ps[:, 6 + g % 2, j * P:(j + 1) * P], xn[:, TPB * g + j, :], ident[:])
                mm.then_inc(s["tp_done"], 1)
                if g >= 1:
                    e.wait_ge(s["xnT_ready"], g)
            e.wait_ge(s["xnT_ready"], NTB)

        def unit_tensor(e, items, u, par, first):
            for what, k, n in items:
                v, vp = u + k, (par + k) % 2
                if what == "turn":
                    pair, half = piece(n)
                    if n == 0:
                        e.wait_ge(AT["unit_split"], v + 1)
                    if n < 2 and not (first and k == 0):
                        e.wait_ge(AT["max_done"], NSB * v)
                    elif n >= 2 and (n not in (NRE, NRE + 1) or (first and k == 0)):
                        e.wait_ge(AT["turned_copied"], NTU * v + n - 1)
                    elif n >= 2:
                        e.wait_ge(AT["returned_copied"], NRE * v)
                    for j in range(4):
                        mm = e.matmul(ps[:, n % 2, j * P:(j + 1) * P],
                                      pads[n // NRE][:, vp, 4 * half + j, HP * pair:HP * pair + HP, :].rearrange("p h c -> p (h c)"),
                                      identb[:], start=True, stop=True)
                    mm.then_inc(AT["turned"], 1)
                elif what == "returned":
                    pair, half = piece(n)
                    if n == 0:
                        e.wait_ge(AT["negmax_ready"], v + 1)
                    if n >= 2:
                        e.wait_ge(AT["returned_copied"], NRE * v + n - 1)
                    elif not (isinstance(v, int) and v == NU - 1):
                        e.wait_ge(AT["turned_copied"], NTU * v + NTU + NRE)
                    for j in range(4):
                        mm = e.matmul(ps[:, n % 2, j * P:(j + 1) * P],
                                      qpad[:, vp, 4 * half + j, HP * pair:HP * pair + HP, :].rearrange("p h c -> p (h c)"),
                                      identb[:], start=True, stop=True)
                    mm.then_inc(AT["returned"], 1)
                elif what == "s":
                    h, group, w = s_blocks[n]
                    if n == 0:
                        e.wait_ge(AT["turned_copied"], NTU * v + NTU)
                        e.wait_ge(AT["qz_ready"], 2 * v + 2)
                    elif n >= 2:
                        e.wait_ge(AT["max_done"], NSB * v + n - 1)
                    for m, (i, half) in enumerate(group):
                        diag = i // 4 == half
                        mm = e.matmul(ps[:, n % 2, m * w:(m + 1) * w], qz[:, h, i * P:(i + 1) * P],
                                      kT[:, h // HP, half * 512:half * 512 + w], start=True, stop=not diag)
                        if diag:
                            mm = e.matmul(ps[:, n % 2, (m + 1) * w - P:(m + 1) * w], identb[:], hide_q[:],
                                          start=False, stop=True)
                    mm.then_inc(AT["s_done"], 1)
                elif what == "st":
                    m, pair = n // 2, n % 2
                    half, j = steps[m]
                    q0, w = span(m)
                    if n == 0:
                        e.wait_ge(AT["returned_copied"], NRE * v + NRE)
                        e.wait_ge(AT["kz_ready"], v + 1)
                    e.wait_ge(AT["exp_done"], 2 * NST * v + n + 1)
                    for h in range(2):
                        bank = 2 + 2 * pair + h
                        diag = j // 4 == half
                        mm = e.matmul(ps[:, bank, 0:w], kz[:, vp, 2 * pair + h, j * P:(j + 1) * P],
                                      qm[:, vp, pair, half * 512 + q0:half * 512 + 512], start=True, stop=not diag)
                        if diag:
                            mm = e.matmul(ps[:, bank, 0:P], identb[:], hide_k[:], start=False, stop=True)
                    mm.then_inc(AT["st_done"], 1)
                elif what == "pv":
                    half, j = steps[n]
                    q0, w = span(n)
                    e.wait_ge(AT["exp_done"], 2 * NST * v + 2 * n + 4)
                    if n == 0:
                        e.wait_ge(AT["v_placed"], v + 1)
                    if j == 0:
                        e.wait_ge(AT["o_normed"], 2 * v + half + 1)
                    for h in range(HG):
                        mm = e.matmul(ps[32 * h:32 * h + 32, 6 + half, q0:512], vpad[:, vp, j, h, :],
                                      probT[:, n % 2, h, 0:w], start=(j == 0), stop=(w == P),
                                      skip_group_check=True)
                    mm.then_inc(AT["pv_done"], 1)
                elif what == "oturn":
                    e.wait_ge(AT["o_copied"], 2 * v + n + 1)
                    for j in range(4):
                        mm = e.transpose(ps[:, 6 + n, j * P:(j + 1) * P], oT[:, n, j * P:(j + 1) * P], ident[:])
                    mm.then_inc(AT["o_turned"], 1)

        def attention_tensor(e):
            turn_tokens(e, AT)
            for i in range(NT):
                if i >= 4:
                    e.wait_ge(AT["qkv_copied"], 2 * (i - 3))
                e.matmul(ps[:, i % 4, 0:3 * D], xnT[:, i * P:(i + 1) * P], wqkv[:],
                         start=True, stop=True).then_inc(AT["qkv_done"], 1)
            e.wait_ge(AT["masks_ready"], 3)
            e.wait_ge(AT["qkv_copied"], 2 * NT)
            e.sem_inc(AT["pv_done"], 2)
            def go(items, u, par, at, first=False):
                unit_tensor(e, items, u, par, first)
            go.engine = e
            units(go)
            e.wait_ge(AT["o_normed"], 2 * NU + 2)
            for g in range(NTB):
                if g >= 2:
                    e.wait_ge(AT["ctxT_ready"], g - 1)
                for j in range(TPB):
                    mm = e.transpose(ps[:, g % 2, j * P:(j + 1) * P], ctxv[:, TPB * g + j, :], ident[:])
                mm.then_inc(AT["ctxT_turned"], 1)
            for g in range(NTB):
                e.wait_ge(AT["ctxT_ready"], g + 1)
                for j in range(TPB):
                    i = TPB * g + j
                    mm = e.matmul(ps[:, 2 + g, j * P:(j + 1) * P], xnT[:, i * P:(i + 1) * P], wo[:],
                                  start=True, stop=True)
                mm.then_inc(AT["proj_done"], 1)

        def spread(e, bank, j, r, operand, g0, t0):
            return e.matmul(ps[:, bank, j * TR:(j + 1) * TR], sel[:, r % DG, :],
                            operand.rearrange("p g t -> p (g t)")[:, bass.ds(g0 + r // DG * S + t0, TR)],
                            start=True, stop=True)

        def spread_dt(e, q, n, g0, t0):
            e.wait_ge(SC["da_done"], 8 * q + n + 1)
            for j in range(4):
                mm = spread(e, n % 2, j, 4 * n + j, dtp, g0, t0)
            mm.then_inc(SC["dt_cast"], 1)

        def spread_u(e, q, c, g0, t0):
            e.wait_ge(SC["in_done"], 4 * q + c + 1)
            for k in range(2):
                for j in range(4):
                    mm = spread(e, 2 + 2 * (c % 2) + k, j, 8 * c + 4 * k + j, upp, g0, t0)
            mm.then_inc(SC["u_cast"], 1)

        def scan_out(e, q, par, tr, n):
            if n == 0:
                e.wait_ge(SC["h_done"], q + 3)
                e.wait_ge(SC["c_placed"], 2 * tr + 2)
                e.wait_ge(SC["y_copied"], q + 2)
            h = hs[:, par, :].rearrange("p (d t) -> p d t", t=TR)
            rb = n // 4
            for k in range(4 * (n % 4), 4 * (n % 4) + 4):
                for j in range(4):
                    t = rb * 64 + j * 16 + k
                    mm = e.matmul(ps[32 * j:32 * j + 32, 6, rb * DQ:(rb + 1) * DQ], cz[:, t, :], h[:, :, t], start=(k == 0), stop=(k == 15), skip_group_check=True)
            if n == 7:
                mm.then_inc(SC["y_done"], 1)

        def scan_turn(e, tr):
            e.wait_ge(SC["y_copied"], NDQ * tr + NDQ + 2)
            e.wait_ge(SC["proj_added"], tr + 1)
            for rb in range(2):
                mm = e.transpose(ps[:, 7, rb * P:(rb + 1) * P], ysb[:, rb, :], ident[:])
            mm.then_inc(SC["y_turned"], 1)

        def scan_project(e, tr):
            e.wait_ge(SC["yT_ready"], tr + 1)
            for b in range(B):
                mm = e.matmul(ps[:, 7, (2 + b) * D:(3 + b) * D], yT[:, b, :], opw[:], start=True, stop=True)
            mm.then_inc(SC["proj_done"], 1)

        def scan_step(e, q, dq, tr, first=False, last=False):
            here = (dq * 2 * S, tr * TR)
            after = ((dq + 1) % NDQ * 2 * S, (tr + (dq + 1) // NDQ) * TR)
            if dq == NDQ - 1 and not last:
                e.wait_ge(parts_in, 16 * 12 * ((tr + 1) // 2 + 1))
            for n in range(8):
                if not (last and dq == NDQ - 1):
                    spread_dt(e, q + 1, n, *after)
                if n == 1:
                    spread_u(e, q, 2, *here)
                if n == 3:
                    spread_u(e, q, 3, *here)
                if not (first and dq == 0):
                    scan_out(e, q - 1, (dq + 1) % 2, tr if dq >= 1 else tr - 1, n)
                if n == 4 and not first and dq == 1:
                    scan_turn(e, tr - 1)
                if n == 4 and not first and dq == 2:
                    scan_project(e, tr - 1)
                if not (last and dq == NDQ - 1) and n in (5, 7):
                    spread_u(e, q + 1, (n - 5) // 2, *after)

        def scan_tensor(e):
            for g in range(NTB):
                for j in range(TPB):
                    e.wait_ge(SC["xr_ready"], TPB * g + j + 1)
                    mm = e.transpose(ps[:, g, j * P:(j + 1) * P], xr[:, TPB * g + j, :], ident[:])
                mm.then_inc(SC["xr_turned"], 1)
            for g in range(NTB):
                for j in range(TPB):
                    mm = e.transpose(ps[:, 4 + g, j * P:(j + 1) * P], xn[:, TPB * g + j, :], ident[:])
                mm.then_inc(SC["xn_turned"], 1)
            e.wait_ge(SC["xrT_ready"], NTB)
            for k in range(4):
                e.matmul(ps[0:RANK, k, :], xpw[:, 0:RANK], ut[:, :, k * QT:(k + 1) * QT],
                         start=True, stop=True).then_inc(SC["lo_done"], 1)
            for k in range(4):
                e.wait_ge(SC["loT_ready"], k + 1)
                e.matmul(ps[:, k, :], dtw[:], loT[:, k, :], start=True, stop=True).then_inc(SC["dt_done"], 1)
            e.wait_ge(SC["xd_ready"], NTB)
            for c in range(2):
                for h in range(2):
                    for b in range(B):
                        mm = e.matmul(ps[64 * b:64 * b + 64, 4 + 2 * c + h, :],
                                      xpw[:, RANK + c * STATE:RANK + (c + 1) * STATE],
                                      ut[:, b, h * 512:(h + 1) * 512], start=True, stop=True)
                mm.then_inc(SC["bc_done"], 1)
            e.wait_ge(SC["z_ready"], 4)
            for i in range(NT):
                mm = e.matmul(ps[:, i // TPB, i % TPB * P:(i % TPB + 1) * P], xd[:, i * P:(i + 1) * P], opw[:],
                              start=True, stop=True)
            mm.then_inc(SC["skip_done"], 1)
            e.wait_ge(SC["prep_done"], 1)
            e.wait_ge(SC["bT_ready"], 2)
            e.wait_ge(SC["sel_ready"], 1)
            e.wait_ge(SC["rows_zeroed"], 1)
            e.wait_ge(parts_in, 16 * 12)
            e.sem_inc(SC["y_done"], 2)
            for n in range(8):
                spread_dt(e, 0, n, 0, 0)
            for c in range(2):
                spread_u(e, 0, c, 0, 0)
            for dq in range(NDQ):
                scan_step(e, dq, dq, 0, first=True)
            with e.Fori(1, NTR - 1) as tr:
                for dq in range(NDQ):
                    scan_step(e, tr * NDQ + dq, dq, tr)
            for dq in range(NDQ):
                scan_step(e, NSU - NDQ + dq, dq, NTR - 1, last=True)
            for n in range(8):
                scan_out(e, NSU - 1, 1, NTR - 1, n)
            scan_turn(e, NTR - 1)
            scan_project(e, NTR - 1)

        @block.tensor
        def _(e):
            e.wait_ge(consts_in, CONSTS)
            for name, kind in plan:
                if kind == "attention":
                    attention_tensor(e)
                elif kind == "scan":
                    scan_tensor(e)
                else:
                    moe_tensor(e, MOE[name], kind)

        def moe_scalar(e, s, kind):
            nf = (F0, F1)[kind] // P
            e.wait_ge(s["var_ready"], 1)
            e.activation(std[:], veps[:], ACT.Sqrt).then_inc(s["std_ready"], 1)
            for g in range(NTB):
                e.wait_ge(s["tp_done"], g + 1)
                e.copy(xnT[:, g * TB:(g + 1) * TB], ps[:, 6 + g % 2, :]).then_inc(s["xnT_ready"], 1)
            e.wait_ge(s["shifted"], 1)
            e.activation(lg[:], lg[:], ACT.Exp).then_inc(s["exp_done"], 1)
            if kind == 1:
                e.wait_ge(s["comb_turned"], 1)
                e.copy(combT, ps[0:E, 0:4, :].rearrange("p a b -> p (a b)")).then_inc(s["combT_ready"], 1)
            e.sem_inc(s["act_done"], nf)
            with e.Fori(0, NTB) as tb:
                for ex in range(E):
                    e.wait_ge(s["down_done"], tb * E + ex + 1)
                    for fc in range(nf):
                        e.wait_ge(s["up_done"], tb * (E * nf) + ex * nf + fc + 1)
                        if kind == 0:
                            a = e.activation(hid[:, ex % 2, fc, :], ps[:, fc, :], ACT.Gelu)
                        else:
                            a = e.activation(hid[:, ex % 2, fc, :], ps[:, fc, :], ACT.Relu, bias=b1c[:, ex, fc:fc + 1])
                        a.then_inc(s["act_done"], 1)

        def unit_scalar(e, items, u, par, first):
            for what, k, n in items:
                v, vp = u + k, (par + k) % 2
                if what == "turn":
                    pair, half = piece(n)
                    if n == 0 and not (first and k == 0):
                        e.wait_ge(AT["qz_ready"], 2 * v)
                    if n == NRE and not (first and k == 0):
                        e.wait_ge(AT["kz_ready"], v)
                    e.wait_ge(AT["turned"], NTU * v + n + 1)
                    e.copy((qT, kT)[n // NRE][:, pair, half * 512:half * 512 + 512],
                           ps[:, n % 2, :]).then_inc(AT["turned_copied"], 1)
                elif what == "returned":
                    pair, half = piece(n)
                    e.wait_ge(AT["returned"], NRE * v + n + 1)
                    e.copy(qm[:, vp, pair, half * 512:half * 512 + 512],
                           ps[:, n % 2, :]).then_inc(AT["returned_copied"], 1)
                elif what == "st":
                    m, pair = n // 2, n % 2
                    q0, w = span(m)
                    if pair == 0:
                        e.wait_ge(AT["pv_done"], NST * v + m + 1)
                    e.wait_ge(AT["st_done"], 2 * NST * v + n + 1)
                    e.activation(probT[:, m % 2, 2 * pair:2 * pair + 2, 0:w],
                                 ps[:, 2 + 2 * pair:4 + 2 * pair, 0:w], ACT.Exp,
                                 scale=SCALE).then_inc(AT["exp_done"], 1)
                elif what == "ocopy":
                    e.wait_ge(AT["pv_done"], NST * v + (4, NST)[n] + 2)
                    e.copy(oT[:, n, :], ps[:, 6 + n, :]).then_inc(AT["o_copied"], 1)

        def attention_scalar(e):
            e.wait_ge(AT["var_ready"], 1)
            e.activation(std[:], veps[:], ACT.Sqrt).then_inc(AT["std_ready"], 1)
            for g in range(NTB):
                e.wait_ge(AT["tp_done"], g + 1)
                e.copy(xnT[:, g * TB:(g + 1) * TB], ps[:, 6 + g % 2, :]).then_inc(AT["xnT_ready"], 1)
            e.copy(identb[:], ident[:]).then_inc(AT["masks_ready"], 1)
            e.copy(hide_q[:], maskf[:, 0, :]).then_inc(AT["masks_ready"], 1)
            e.copy(hide_k[:], maskf[:, 1, :]).then_inc(AT["masks_ready"], 1)
            e.wait_ge(AT["rotated"], 1)
            e.sem_inc(AT["exp_done"], 2)
            def go(items, u, par, at, first=False):
                unit_scalar(e, items, u, par, first)
            go.engine = e
            units(go)
            for g in range(NTB):
                e.wait_ge(AT["ctxT_turned"], g + 1)
                e.copy(xnT[:, g * TB:(g + 1) * TB], ps[:, g % 2, :]).then_inc(AT["ctxT_ready"], 1)

        def scan_exp(e, q, dq):
            e.wait_ge(SC["h_done"], q + 1)
            for n in range(8):
                e.wait_ge(SC["dt_cast"], 8 * q + n + 1)
                for j in range(4):
                    r = 4 * n + j
                    ins = e.activation(da[:, dq % 2, r * TR:(r + 1) * TR], ps[:, n % 2, j * TR:(j + 1) * TR], ACT.Exp,
                                       scale=arate[:, dq * DQ + r:dq * DQ + r + 1])
                ins.then_inc(SC["da_done"], 1)

        def scan_keep(e, q, dq, tr, first=False):
            e.wait_ge(SC["y_done"], q + 3)
            if dq == 0 and not first:
                e.wait_ge(SC["y_turned"], tr)
            e.copy(ysb[:, :, dq * DQ:(dq + 1) * DQ], ps[:, 6, 0:2 * DQ].rearrange(
                "p (r d) -> p r d", d=DQ)).then_inc(SC["y_copied"], 1)

        def scan_turned(e, tr):
            e.wait_ge(SC["y_turned"], tr + 1)
            e.wait_ge(SC["proj_added"], tr + 1)
            e.copy(yT.rearrange("p b (g k) -> p b g k", k=16),
                   ps[:, 7, 0:B * TR].rearrange("p (g b k) -> p b g k", b=B, k=16)).then_inc(SC["yT_ready"], 1)

        def scan_scalar(e):
            e.wait_ge(SC["var_ready"], 1)
            e.activation(std[:], veps[:], ACT.Sqrt).then_inc(SC["std_ready"], 1)
            e.wait_ge(SC["rms_ready"], 1)
            e.activation(std[:], veps[:], ACT.Sqrt).then_inc(SC["rms_std"], 1)
            for g in range(NTB):
                e.wait_ge(SC["xr_turned"], g + 1)
                e.copy(xnT[:, g * TB:(g + 1) * TB], ps[:, g, :]).then_inc(SC["xrT_ready"], 1)
            e.wait_ge(SC["xrT_ready"], NTB)
            for k in range(4):
                e.wait_ge(SC["lo_done"], k + 1)
                e.copy(loT[:, k, :], ps[0:RANK, k, :]).then_inc(SC["loT_ready"], 1)
            for g in range(NTB):
                e.wait_ge(SC["xn_turned"], g + 1)
                e.activation(xd[:, g * TB:(g + 1) * TB], ps[:, 4 + g, :], ACT.Copy,
                             scale=dskip[:, 0:1]).then_inc(SC["xd_ready"], 1)
            for n, (k0, k1) in enumerate(((0, 1), (1, 4))):
                sl = soft[:, :, k0 * QT:k1 * QT]
                e.wait_ge(SC["z_ready"], k1)
                e.activation(sl, sl, ACT.Exp, scale=-1.0).then_inc(SC["exp_ready"], 1)
                e.wait_ge(SC["exp_ready"], n + 1)
                e.activation(sl, sl, ACT.Ln, bias=1.0).then_inc(SC["ln_ready"], 1)
            e.wait_ge(SC["bc_done"], 1)
            e.copy(bT, ps[:, 4:6, :].rearrange("p a b -> p (a b)")).then_inc(SC["bT_ready"], 1)
            e.wait_ge(SC["bc_done"], 2)
            e.copy(cT, ps[:, 6:8, :].rearrange("p a b -> p (a b)")).then_inc(SC["bT_ready"], 1)
            e.activation(arate[:], arate[:], ACT.Exp).then_inc(SC["rate_exp"], 1)
            e.wait_ge(SC["sel_in"], 16)
            e.copy(sel[0:ROWS].rearrange("p r m -> p (r m)"), selftmp[0:ROWS, :]).then_inc(SC["sel_ready"], 1)
            e.wait_ge(SC["prep_done"], 1)
            e.wait_ge(SC["rate_ready"], 1)
            e.sem_inc(SC["da_done"], 2)
            e.sem_inc(SC["y_copied"], 2)
            for q in range(NDQ):
                scan_exp(e, q, q)
                if q >= 2:
                    scan_keep(e, q - 2, q - 2, 0, first=True)
            with e.Fori(1, NTR) as tr:
                for dq in range(NDQ):
                    scan_exp(e, tr * NDQ + dq, dq)
                    if dq == 2:
                        scan_turned(e, tr - 1)
                    if dq == 2:
                        scan_keep(e, tr * NDQ, 0, tr)
                    elif dq == 3:
                        scan_keep(e, tr * NDQ + 1, 1, tr)
                    else:
                        scan_keep(e, tr * NDQ + dq - 2, dq + 2, tr - 1)
            scan_keep(e, NSU - 2, 2, NTR - 1)
            scan_keep(e, NSU - 1, 3, NTR - 1)
            scan_turned(e, NTR - 1)

        @block.scalar
        def _(e):
            e.wait_ge(consts_in, CONSTS)
            for name, kind in plan:
                if kind == "attention":
                    attention_scalar(e)
                elif kind == "scan":
                    scan_scalar(e)
                else:
                    moe_scalar(e, MOE[name], kind)

        def split_parts(e, then, v, full):
            then(e.tensor_copy(parts[:, v, 0], full))
            then(e.tensor_tensor(full, full, parts[:, v, 0], ALU.subtract))
            then(e.tensor_copy(parts[:, v, 1], full))
            then(e.tensor_tensor(full, full, parts[:, v, 1], ALU.subtract))
            e.tensor_copy(parts[:, v, 2], full).then_inc(SC[f"split{v}"], 1)

        @block.gpsimd
        def _(e):
            def pool_chain(ins):
                pool_steps[0] += 1
                ins.then_inc(pool_step, 1)
                e.wait_ge(pool_step, pool_steps[0])

            def heads(flat, at):
                return flat[:, bass.ds(at, ST_ * D)].rearrange("p (i d) -> p i d", d=D)[:, :, 0:HG * HD].rearrange(
                    "p i (h c) -> p i h c", h=HG)

            def place_v(u, par, at):
                e.tensor_copy(vpad[:, par, :, :, 0:HD], heads(vflat, at)).then_inc(AT["v_placed"], 1)

            def split(u, par, at):
                done = [0]

                def finish(ins):
                    done[0] += 1
                    ins.then_inc(AT["parts"], 1)
                    e.wait_ge(AT["parts"], 5 * u + done[0])
                    e.sem_inc(AT["waited"], 1)

                e.memset(qpad[:, par, :, :, AT_MAX:AT_MAX + 3], 0.0)
                full = [heads(rot, at + c * T) for c in range(2)]
                for a in range(3):
                    for c, cols in enumerate((Q_PARTS, K_PARTS)):
                        for n in cols[a]:
                            ins = e.tensor_copy(pads[c][:, par, :, :, n:n + HD], full[c] if a == 0 else rests[c])
                    finish(ins)
                    if a < 2:
                        for c, cols in enumerate((Q_PARTS, K_PARTS)):
                            n = cols[a][0]
                            ins = e.tensor_tensor(rests[c], full[c] if a == 0 else rests[c],
                                                  pads[c][:, par, :, :, n:n + HD], ALU.subtract)
                        finish(ins)
                e.sem_inc(AT["unit_split"], 1)

            def pool_unit(u, par, at, more=True):
                e.wait_ge(AT["pv_done"], NST * u + 2)
                e.sem_inc(AT["waited"], 1)
                place_v(u + 1, 1 - par, at(1))
                if more:
                    e.wait_ge(AT["returned"], NRE * u + NRE)
                    e.wait_ge(AT["turned"], NTU * u + NTU)
                    e.sem_inc(AT["waited"], 1)
                    split(u + 2, par, at(2))

            if ("b", "attention") in plan:
                e.memset(qpad[:], 0.0)
                e.memset(kpad[:], 0.0)
                e.memset(vpad[:], 0.0).then_inc(AT["pads_ready"], 1)
                e.wait_ge(AT["pads_ready"], 1)
                e.memset(kpad[:, :, :, :, AT_MAX:AT_MAX + 3], 1.0)
                e.memset(vpad[:, :, :, :, HD:HD + 1], 1.0)
                e.wait_ge(AT["rotated"], 1)
                split(0, 0, 0)
                e.memset(kz, 0.0)
                e.memset(qz, 0.0).then_inc(AT["pads_clear"], 1)
                place_v(0, 0, 0)
                split(1, 1, HG * HD)

                def pool_go(items, u, par, at, first=False):
                    if not first and not (isinstance(u, int) and u >= NU - 1):
                        pool_unit(u, par, at, not (isinstance(u, int) and u == NU - 2))
                pool_go.engine = e
                units(pool_go)

            if ("e", "scan") in plan:
                e.wait_ge(SC["arena_free"], 1)
                e.memset(sel[ROWS:P], 0.0)
                e.memset(dtp[ROWS:P], 0.0)
                e.memset(upp[ROWS:P], 0.0).then_inc(SC["rows_zeroed"], 1)
                e.wait_ge(SC["rows_zeroed"], 1)
                e.sem_inc(SC["waited"], 1)
                e.memset(cz, 0.0).then_inc(SC["c_zeroed"], 1)

                def split_quarter(k):
                    for v, full in enumerate((zt, ut)):
                        if k == 0 and v == 0:
                            continue
                        e.wait_ge(SC["u_ready"], min(k, 1) + 1)
                        if k >= 1:
                            e.wait_ge(parts_out, 16 * (2 * k - 1 + v))
                        split_parts(e, pool_chain, v, full[:, :, k * QT:(k + 1) * QT])

                def place_c(tr):
                    for b in range(B):
                        rows = slice(64 * b, 64 * b + 64)
                        to = cz.rearrange("p t c -> p (t c)")[rows].rearrange("p (g k) -> p g k", g=TR // 16)[
                            :, :, 16 * b:16 * b + 15 * 33 + 1:33]
                        e.tensor_copy(to, cT[rows, bass.ds(tr * TR, TR)].rearrange("p (g k) -> p g k", k=16)
                                      ).then_inc(SC["c_placed"], 1)
                    e.wait_ge(SC["c_placed"], 2 * tr + 2)
                    e.sem_inc(SC["waited"], 1)

                def place_next_c(tr):
                    e.wait_ge(SC["y_done"], NDQ * tr + 2)
                    e.sem_inc(SC["waited"], 1)
                    place_c(tr)

                split_quarter(0)
                e.wait_ge(SC["split1"], 1)
                e.wait_ge(SC["bT_ready"], 2)
                e.wait_ge(SC["c_zeroed"], 1)
                place_c(0)
                for k in range(1, 4):
                    split_quarter(k)
                    e.wait_ge(SC["split1"], k + 1)
                    place_next_c(k)
                with e.Fori(4, NTR) as tr:
                    place_next_c(tr)

        @block.vector
        def _(e):
            def link(ins):
                chained[0] += 1
                ins.then_inc(chain, 1)
                e.wait_ge(chain, chained[0])

            def layernorm(s):
                for i in range(NT):
                    ins = e.bn_stats(stats[:, i, :], x[:, i, :])
                link(ins)
                for i in range(NT):
                    ins = e.bn_aggr(mv[:, i, :], stats[:, i, :])
                link(ins)
                e.tensor_scalar(veps[:], mv[:, :, 1], LN_EPS, None, ALU.add).then_inc(s["var_ready"], 1)
                e.wait_ge(s["std_ready"], 1)
                link(e.reciprocal(rstd[:], std[:]))
                for i in range(NT):
                    e.tensor_scalar(xn[:, i, :], x[:, i, :], mv[:, i, 0:1], rstd[:, i:i + 1],
                                    ALU.subtract, ALU.mult).then_inc(s["xn_ready"], 1)

            def route(s, kind):
                def per_token(v):
                    return v.unsqueeze(2).to_broadcast([P, NT, E])
                e.wait_ge(s["logits_done"], 1)
                link(e.tensor_tensor(lg[:], ps[:, 6, 0:NT * E].rearrange("p (i e) -> p i e", e=E),
                                     rb[kind][:].unsqueeze(1).to_broadcast([P, NT, E]), ALU.add))
                link(e.tensor_reduce(rowmax[:], lg[:], AX.X, ALU.max))
                e.tensor_tensor(lg[:], lg[:], per_token(rowmax[:]), ALU.subtract).then_inc(s["shifted"], 1)
                e.wait_ge(s["exp_done"], 1)
                link(e.tensor_reduce(rowmax[:], lg[:], AX.X, ALU.add))
                link(e.reciprocal(rowmax[:], rowmax[:]))
                link(e.tensor_tensor(probs[:], lg[:], per_token(rowmax[:]), ALU.mult))
                pr = probs[:].rearrange("p i e -> p (i e)")
                mine = pr.unsqueeze(2).to_broadcast([P, NT * E, E])
                beats4 = beats[:].rearrange("p (i e) f -> p i e f", e=E)
                ties4 = ties[:].rearrange("p (i e) f -> p i e f", e=E)
                mine4 = probs[:].unsqueeze(3).to_broadcast([P, NT, E, E])
                other4 = probs[:].unsqueeze(2).to_broadcast([P, NT, E, E])
                e.tensor_tensor(beats4, other4, mine4, ALU.is_gt)
                link(e.tensor_tensor(ties4, other4, mine4, ALU.is_equal))
                link(e.tensor_tensor(ties4, ties4, earlier[:].unsqueeze(1).to_broadcast([P, NT, E, E]), ALU.mult))
                link(e.tensor_tensor(beats[:], beats[:], ties[:], ALU.add))
                link(e.tensor_reduce(rank[:].rearrange("p i e -> p (i e)"), beats[:], AX.X, ALU.add))
                link(e.tensor_scalar(rank[:], rank[:], float((2, 1)[kind]), 0.5, ALU.is_lt, ALU.mult))
                link(e.tensor_tensor(comb[:], probs[:], rank[:], ALU.mult))
                e.sem_inc(s["comb_ready"], 1)
                if kind == 1:
                    e.wait_ge(s["bias_done"], 1)
                    e.tensor_tensor(xf, xf, ps[:, 0:4, :].rearrange("p a b -> p (a b)"),
                                    ALU.add).then_inc(s["bias_added"], 1)
                    e.wait_ge(s["bias_added"], 1)

            def moe_vector(s, kind):
                layernorm(s)
                route(s, kind)
                e.sem_inc(s["acc_done"], 2)
                with e.Fori(0, NTB) as tb:
                    for ex in range(E):
                        e.wait_ge(s["acc_done"], tb * E + ex + 2)
                        e.wait_ge(s["down_done"], tb * E + ex + 3)
                        for j in range(TPB):
                            xs = xf[:, bass.ds(tb * TB + j * P, P)]
                            ins = e.scalar_tensor_tensor(out=xs, in0=ps[:, 4 + ex % 2, j * P:(j + 1) * P],
                                                         scalar=combf[:, bass.ds(tb * (TPB * E) + j * E + ex, 1)],
                                                         in1=xs, op0=ALU.mult, op1=ALU.add)
                        ins.then_inc(s["acc_done"], 1)
                e.wait_ge(s["acc_done"], ACC_END)

            def unit_vector(items, u, par, at, first):
                for what, k, n in items:
                    v, vp = u + k, (par + k) % 2
                    if what == "turn" and n in (1, 3):
                        pair = piece(n)[0]
                        e.wait_ge(AT["turned_copied"], NTU * v + n + 1)
                        if first and k == 0 and n == 1:
                            e.wait_ge(AT["pads_clear"], 1)
                        for h in range(HP):
                            rows = slice(h * HR, (h + 1) * HR)
                            ins = e.tensor_copy(qz[rows, HP * pair + h, :], qT[rows, pair, :])
                        ins.then_inc(AT["qz_ready"], 1)
                    elif what == "kz":
                        e.wait_ge(AT["turned_copied"], NTU * v + NTU)
                        if not first:
                            e.wait_ge(AT["exp_done"], 2 * NST * u + 2)
                        for h in range(HG):
                            rows = slice(h % HP * HR, (h % HP + 1) * HR)
                            ins = e.tensor_copy(kz[rows, vp, h, :], kT[rows, h // HP, :])
                        ins.then_inc(AT["kz_ready"], 1)
                    elif what == "s":
                        h, group, w = s_blocks[n]
                        ng = len(group)
                        at_max = [i * HG * 2 + h * 2 + half for i, half in group]
                        e.wait_ge(AT["s_done"], NSB * v + n + 1)
                        e.tensor_reduce(maxf[:, at_max[0]:at_max[-1] + 1:max(1, at_max[-1] - at_max[0])],
                                        ps[:, n % 2, 0:ng * w].rearrange("p (g k) -> p g k", g=ng),
                                        AX.X, ALU.max).then_inc(AT["max_done"], 1)
                        if n == NSB - 1:
                            e.wait_ge(AT["max_done"], NSB * v + NSB)
                            e.tensor_reduce(negmax[:], maxima[:], AX.X, ALU.max, negate=True).then_inc(AT["max_part"], 1)
                            e.wait_ge(AT["max_part"], 5 * v + 1)
                            for a in range(3):
                                col = qpad[:, vp, :, :, AT_MAX + a]
                                ins = e.tensor_copy(col, negmax[:])
                                if a < 2:
                                    ins.then_inc(AT["max_part"], 1)
                                    e.wait_ge(AT["max_part"], 5 * v + 2 * a + 2)
                                    e.tensor_tensor(negmax[:], negmax[:], col, ALU.subtract).then_inc(AT["max_part"], 1)
                                    e.wait_ge(AT["max_part"], 5 * v + 2 * a + 3)
                            ins.then_inc(AT["negmax_ready"], 1)
                    elif what == "oturn":
                        e.wait_ge(AT["o_turned"], 2 * v + n + 1)
                        o = ps[:, 6 + n, :].rearrange("p (i h c) -> p i h c", i=4, h=HG)
                        e.wait_ge(AT["o_normed"], 2 * v + n + 2)
                        ins = e.reciprocal(osum[:], o[:, :, :, HD:HD + 1])
                        ins.then_inc(AT["o_summed"], 1)
                        e.wait_ge(AT["o_summed"], 2 * v + n + 1)
                        for i in range(4):
                            ins = e.tensor_tensor(
                                ctxv.rearrange("p i d -> p (i d)")[:, bass.ds(at(k) + (4 * n + i) * D, HG * HD)].rearrange(
                                    "p (h c) -> p h c", h=HG),
                                o[:, i, :, 0:HD], osum[:, i, :, :].to_broadcast([P, HG, HD]), ALU.mult)
                        ins.then_inc(AT["o_normed"], 1)

            def attention_vector():
                layernorm(AT)
                for i in range(NT):
                    e.wait_ge(AT["qkv_done"], i + 1)
                    e.tensor_tensor(qk[:, i].rearrange("p c d -> p (c d)"), ps[:, i % 4, 0:2 * D], bqkv[:, 0:2 * D],
                                    ALU.add).then_inc(AT["qkv_copied"], 1)
                    e.tensor_tensor(vall[:, i, :], ps[:, i % 4, 2 * D:3 * D], bqkv[:, 2 * D:3 * D],
                                    ALU.add).then_inc(AT["qkv_copied"], 1)
                e.wait_ge(AT["qkv_copied"], 2 * NT)
                half = D // 2
                t1 = rtmp[:, 0:ST_ * half].rearrange("p (i f) -> p i f", f=half)
                t2 = rtmp[:, ST_ * half:2 * ST_ * half].rearrange("p (i f) -> p i f", f=half)
                for c in range(2):
                    for b in range(B):
                        tiles = slice(b * ST_, (b + 1) * ST_)
                        even, odd = qk[:, tiles, c, 0::2], qk[:, tiles, c, 1::2]
                        for part, (ea, oa) in enumerate(((cos, sin), (sin, cos))):
                            e.tensor_tensor(t1, even, ea[:], ALU.mult)
                            link(e.tensor_tensor(t2, odd, oa[:], ALU.mult))
                            link(e.tensor_tensor(rotv[:, c, tiles, part * half:(part + 1) * half], t1, t2,
                                                 ALU.subtract))
                link(e.memset(maxima[:], MASKED))
                e.sem_inc(AT["rotated"], 1)
                e.sem_inc(AT["o_normed"], 2)
                def go(items, u, par, at, first=False):
                    unit_vector(items, u, par, at, first)
                go.engine = e
                units(go)
                for g in range(NTB):
                    e.wait_ge(AT["proj_done"], g + 1)
                    xs = xf[:, g * TB:(g + 1) * TB]
                    e.tensor_tensor(xs, xs, ps[:, 2 + g, :], ALU.add).then_inc(AT["proj_added"], 1)
                e.wait_ge(AT["proj_added"], NTB)
                link(e.tensor_tensor(x[:], x[:], bo[:].unsqueeze(1).to_broadcast([P, NT, D]), ALU.add))

            def scan_unit(q, par, t0):
                half = DQ * TR // 2
                e.wait_ge(SC["y_done"], q + 1)
                for c in range(4):
                    e.wait_ge(SC["u_cast"], 4 * q + c + 1)
                    e.tensor_tensor(hs[:, par, c * 8 * TR:(c + 1) * 8 * TR].rearrange("p (d t) -> p d t", t=TR),
                                    ps[:, 2 + 2 * (c % 2):4 + 2 * (c % 2), :].rearrange("p a (d t) -> p (a d) t", t=TR),
                                    bT[:, bass.ds(t0, TR)].unsqueeze(1).to_broadcast([P, 8, TR]),
                                    ALU.mult).then_inc(SC["in_done"], 1)
                    if c == 1:
                        e.wait_ge(SC["da_done"], 8 * q + 8 + 2)
                        e.memset(da[:, par, 0::CHUNK], 0.0).then_inc(SC["da_cut"], 1)
                    if c >= 2:
                        if c == 2:
                            e.wait_ge(SC["da_cut"], q + 1)
                        e.wait_ge(SC["in_done"], 4 * q + 2 * c - 2 + 2)
                        part = slice((c - 2) * half, (c - 1) * half)
                        ins = e.tensor_tensor_scan(hs[:, par, part], da[:, par, part], hs[:, par, part], 0.0, ALU.mult,
                                                   ALU.add)
                ins.then_inc(SC["h_done"], 1)

            def scan_vector():
                layernorm(SC)
                e.wait_ge(SC["xn_ready"], NT)
                e.wait_ge(w_in, 64)
                e.sem_inc(SC["arena_free"], 1)
                link(e.tensor_tensor(std[:], rstd[:], rstd[:], ALU.mult))
                link(e.tensor_tensor(std[:], std[:], mv[:, :, 1], ALU.mult))
                e.tensor_scalar(veps[:], std[:], RMS_EPS, None, ALU.add).then_inc(SC["rms_ready"], 1)
                e.wait_ge(SC["rms_std"], 1)
                link(e.reciprocal(rstd[:], std[:]))
                for i in range(NT):
                    e.scalar_tensor_tensor(out=xr[:, i, :], in0=xn[:, i, :], scalar=rstd[:, i:i + 1], in1=nw[:],
                                           op0=ALU.mult, op1=ALU.mult).then_inc(SC["xr_ready"], 1)
                e.wait_ge(SC["xn_turned"], NTB)
                for n, (k0, k1) in enumerate(((0, 1), (1, 4))):
                    for k in range(k0, k1):
                        part = slice(k * QT, (k + 1) * QT)
                        e.wait_ge(SC["dt_done"], k + 1)
                        link(e.tensor_scalar(zt[:, :, part], ps[:, k, :].rearrange("p (b t) -> p b t", b=B), dtb[:, 0:1],
                                             None, ALU.add))
                        e.scalar_tensor_tensor(out=soft[:, :, part], in0=zt[:, :, part], scalar=-1.0, in1=zt[:, :, part],
                                               op0=ALU.mult, op1=ALU.max).then_inc(SC["z_ready"], 1)
                    part = slice(k0 * QT, k1 * QT)
                    e.wait_ge(SC["ln_ready"], n + 1)
                    link(e.scalar_tensor_tensor(out=zt[:, :, part], in0=zt[:, :, part], scalar=0.0, in1=soft[:, :, part],
                                                op0=ALU.max, op1=ALU.add))
                    if n == 0:
                        e.wait_ge(SC["bc_done"], 2)
                    e.tensor_tensor(ut[:, :, part], zt[:, :, part], ut[:, :, part], ALU.mult).then_inc(SC["u_ready"], 1)
                    if n == 0:
                        e.wait_ge(SC["u_ready"], 1)
                        split_parts(e, link, 0, zt[:, :, part])
                e.wait_ge(SC["rate_exp"], 1)
                e.tensor_scalar(arate[:], arate[:], -1.0, None, ALU.mult).then_inc(SC["rate_ready"], 1)
                e.wait_ge(SC["skip_done"], 1)
                e.tensor_tensor(xf, xf, ps[:, 0:4, :].rearrange("p a b -> p (a b)"), ALU.add).then_inc(SC["prep_done"], 1)
                e.wait_ge(SC["prep_done"], 1)
                e.wait_ge(SC["sel_ready"], 1)
                e.sem_inc(SC["in_done"], 2)
                e.sem_inc(SC["h_done"], 2)
                e.sem_inc(SC["proj_added"], 1)

                def scan_add(tr):
                    e.wait_ge(SC["proj_done"], tr + 1)
                    xs = xf.rearrange("p (b t) -> p b t", b=B)[:, :, bass.ds(tr * P, P)]
                    e.tensor_tensor(xs, xs, ps[:, 7, B * D:2 * B * D].rearrange("p (b d) -> p b d", b=B),
                                    ALU.add).then_inc(SC["proj_added"], 1)

                for dq in range(NDQ):
                    scan_unit(dq, dq % 2, 0)
                with e.Fori(1, NTR) as tr:
                    for dq in range(NDQ):
                        scan_unit(tr * NDQ + dq, dq % 2, tr * TR)
                        if dq == 2:
                            scan_add(tr - 1)
                scan_add(NTR - 1)
                e.wait_ge(SC["proj_added"], NTR + 1)

            e.wait_ge(x_in, 16)
            e.wait_ge(consts_in, CONSTS)
            for name, kind in plan:
                if kind == "attention":
                    attention_vector()
                elif kind == "scan":
                    scan_vector()
                else:
                    moe_vector(MOE[name], kind)
            e.sem_inc(x_final, 1)


def constants():
    e = np.arange(E)
    n = np.arange(P)
    freq = np.power(np.float32(10000.0), np.float32(-2.0) * np.arange(D // 2, dtype=np.float32) / np.float32(D))
    angle = np.arange(S, dtype=np.float32)[:, None] * freq[None, :].astype(np.float32)
    tiled = lambda v: v.astype(np.float32).reshape(ST_, P, D // 2).transpose(1, 0, 2)
    later = np.where(n[None, :] > n[:, None], np.float32(MASKED), np.float32(0.0))
    k = np.arange(ROWS)
    same_r = (k % DG)[:, None, None] == np.arange(DG)[None, :, None]
    same_b = (k // (3 * DG))[:, None, None] == (np.arange(P) // STATE)[None, None, :]
    return {
        "sel": (same_r & same_b).astype(np.float32).reshape(ROWS, DG * P),
        "cos": tiled(np.cos(angle)), "sin": tiled(np.sin(angle)),
        "masks": np.stack([later, later.T], axis=1),
        "ident": np.eye(P, dtype=np.float32),
        "earlier": (e[None, :] < e[:, None]).astype(np.float32),
    }


def kernel(**inputs):
    import concourse.bacc as bacc
    from concourse.bass_utils import run_bass_kernel_spmd as run

    def a(name):
        return np.asarray(inputs[name])

    arrays = {
        "x": a("L0_attn_x").reshape(T, D),
        "rw0": a("L0_ffn_router_w"), "rb0": a("L0_ffn_router_b"),
        "up0": a("L0_ffn_expert_up").transpose(2, 0, 1),
        "dn0": a("L0_ffn_expert_down").reshape(E, D, F0 // P, P).transpose(3, 0, 2, 1),
        "rw1": a("L1_ffn_w_router"), "rb1": a("L1_ffn_b_router"),
        "up1": a("L1_ffn_w1").transpose(1, 0, 2),
        "dn1": a("L1_ffn_w2").reshape(E, F1 // P, P, D).transpose(2, 0, 1, 3),
        "b1": a("L1_ffn_b1").reshape(E, F1 // P, P).transpose(2, 0, 1),
        "b2": a("L1_ffn_b2"),
        "xpw": a("L1_attn_x_proj_w").T, "dtw": a("L1_attn_dt_proj_w").T,
        "dtb": a("L1_attn_dt_proj_b").reshape(D, 1), "dskip": a("L1_attn_D").reshape(D, 1),
        "opw": a("L1_attn_out_proj_w").T, "norm_w": a("L1_attn_norm_w"),
        "a_log": np.concatenate([a("L1_attn_A_log").T] * B, axis=0),
        "wqkv": np.concatenate([a("L0_attn_Wq"), a("L0_attn_Wk"), a("L0_attn_Wv")], axis=1),
        "bq": a("L0_attn_bq"), "bk": a("L0_attn_bk"), "bv": a("L0_attn_bv"),
        "wo": a("L0_attn_Wo"), "bo": a("L0_attn_bo"),
        **constants(),
    }
    arrays = {f"{k}_dram": np.ascontiguousarray(v) for k, v in arrays.items()}
    nc = bacc.Bacc("TRN2", target_bir_lowering=False, num_devices=1)
    t_in = {k[:-5]: nc.dram_tensor(k, v.shape, mybir.dt.from_np(v.dtype), kind="ExternalInput").ap()
            for k, v in arrays.items()}
    out = nc.dram_tensor("out_dram", (T, D), F32, kind="ExternalOutput").ap()
    scratch = nc.dram_tensor("parts_dram", (4, 2, 3, D, B, QT), BF16, kind="Internal").ap()
    build(nc, t_in, scratch, out)
    r = run(nc, [arrays], core_ids=[0])
    return r.results[0]["out_dram"].reshape(B, S, D)
```

```python
from contextlib import ExitStack

import numpy as np

import concourse.bass as bass
from concourse import mybir

ACT = mybir.ActivationFunctionType
ALU = mybir.AluOpType
AX = mybir.AxisListType
F32 = mybir.dt.float32
F32R = mybir.dt.float32r
BF16 = mybir.dt.bfloat16

P = 128
D = 128
B, S = 2, 1024
T = B * S
NT = T // P
TB = 512
NTB = T // TB
TPB = TB // P
E = 8
F0 = 512
F1 = 256
LN_EPS = 1e-5
H, HD = 16, 8
HG = 4
HR = 64
HP = P // HR
Q_PARTS = ((0, 8, 40), (16, 24), (48,))
K_PARTS = ((0, 16, 48), (8, 24), (40,))
AT_MAX = 32
NG = H // HG
NU = B * NG
ST_ = S // P
SCALE = HD ** -0.5
MASKED = -1e30
STATE = 64
RANK = 8
CHUNK = 64
RMS_EPS = 1e-6
TR, DQ = 128, 32
NTR, NDQ = S // TR, D // DQ
NSU = NTR * NDQ
DG = 16
ROWS = B * 3 * DG
QT = S // 4
ARENA = 164 * 256
PLAN = [("a", 0), ("b", "attention"), ("c", 0), ("d", 1), ("e", "scan"), ("f", 1)]
CONSTS, LATER = 16 * 8, 16 * 16
CP = 32
SLOTS = 4
ROUTE = 11


def build(nc, t_in, scratch, out):
    with ExitStack() as ctx:
        def sb(name, shape, dt=F32):
            return ctx.enter_context(nc.sbuf_tensor(name, shape, dt))

        def sem(name):
            return ctx.enter_context(nc.semaphore(name))

        x = sb("x", [P, NT, D])
        xf = x[:].rearrange("p i d -> p (i d)")
        xn = sb("xn", [P, NT, D])
        xnT = sb("xnT", [P, T])
        ident = sb("ident", [P, P])
        stats = sb("stats", [P, TPB, 6])
        mv = sb("mv", [P, TPB, 2])
        veps = sb("veps", [P, NT])
        std = sb("std", [P, NT])
        rstd = sb("rstd", [P, NT])
        lg = sb("lg", [P, TPB, E])
        rowmax = sb("rowmax", [P, TPB])
        probs = sb("probs", [P, TPB, E])
        earlier = sb("earlier", [P, E, E])
        rank = sb("rank", [P, TPB, E])
        comb = sb("comb", [P, NT, E])
        logitsT = sb("logitsT", [E, TB])
        combnow = sb("combnow", [P, TPB, E])
        sel_e = sb("sel_e", [P, E, P], BF16)
        sel_row = sb("sel_row", [P, E])
        xn0f = xn[:, 0:TPB, :].rearrange("p i d -> p (i d)")
        allvar = sb("allvar", [P, NT])
        allrstd = sb("allrstd", [P, NT])
        combf = comb[:].rearrange("p i e -> p (i e)")
        rw = [sb("rw0", [P, E]), sb("rw1", [P, E])]
        rb = [sb("rb0", [P, E]), sb("rb1", [P, E])]
        b1c = sb("b1c", [P, E, F1 // P])
        b2r = sb("b2r", [E, D])
        wqkv = sb("wqkv", [P, 3 * D])
        bqkv = sb("bqkv", [P, 3 * D])
        wo = sb("wo", [P, D])
        bo = sb("bo", [P, D])
        identb = sb("identb", [P, P], BF16)
        hide_q = sb("hide_q", [P, P], BF16)
        hide_k = sb("hide_k", [P, P], BF16)
        maxima = sb("maxima", [P, ST_, HG, 2])
        maxf = maxima[:].rearrange("p i h t -> p (i h t)")
        negmax = sb("negmax", [P, ST_, HG])
        osum = sb("osum", [P, 4, HG, 1])
        xpw = sb("xpw", [P, RANK + 2 * STATE])
        dtw = sb("dtw", [RANK, D])
        dtb = sb("dtb", [P, 1])
        dskip = sb("dskip", [P, 1])
        nw = sb("nw", [P, D])
        opw = sb("opw", [P, D])
        arate = sb("arate", [P, D])

        with ExitStack() as shared:
            def sbr(name, shape):
                return shared.enter_context(nc.sbuf_tensor(name, shape, F32R))
            wup = sbr("wup", [P, 2, E, F0])
            wdn = sbr("wdn", [P, 2, E, F0 // P, D])
            hr = sbr("hr", [P, 2, 2, F0 // P, TB])
            xp = sbr("xp", [P, 2, T])
        arena = sb("arena", [P, ARENA])
        top = [0]

        def carve(n):
            top[0] += n
            assert top[0] <= ARENA, top[0]
            return arena[:, top[0] - n:top[0]]

        top[0] = 2 * E * F0 + 2 * E * F0 // P * D + 4 * F0 // P * TB + 2 * T
        beats, ties = [carve(TPB * E * E).rearrange("p (i e f) -> p i e f", e=E, f=E) for _ in range(2)]
        hid = carve(2 * F0 // P * TB).rearrange("p (a c t) -> p a c t", a=2, c=F0 // P)
        weighted = carve(2 * TB).rearrange("p (a t) -> p a t", a=2)
        weight = carve(TB)
        acc = carve(TB)
        comb3 = carve(TPB * 3 * CP // 2).bitcast(BF16).rearrange("p (i a c) -> p i a c", a=3, c=CP)
        comb3T = carve(TB // 2).bitcast(BF16)[0:3 * CP]
        stage_w = carve(SLOTS * 2 * F0).rearrange("p (s w f) -> p s w f", s=SLOTS, w=2)
        up1, dn1 = stage_w[:, 0:SLOTS // 2], stage_w[:, SLOTS // 2:SLOTS]
        up1 = up1.rearrange("p s w f -> p (s w f)").rearrange("p (e f) -> p e f", e=E)
        dn1 = dn1.rearrange("p s w f -> p (s w f)").rearrange("p (e c d) -> p e c d", e=E, c=F1 // P)
        combT = weight[0:E]
        table = carve(ST_ * D)
        cos, sin = [table[:, n * ST_ * D // 2:(n + 1) * ST_ * D // 2].rearrange("p (i f) -> p i f", i=ST_) for n in range(2)]
        maskf = carve(2 * P).rearrange("p (a b) -> p a b", a=2)
        kept = top[0] - SLOTS * 2 * F0 - ST_ * D - 2 * P
        top[0] = 0
        kzf = carve(2 * T)
        qzf = carve(2 * T)
        qkf = carve(NT * 2 * D)
        qk = qkf.rearrange("p (i c d) -> p i c d", c=2, d=D)
        probT = qkf.rearrange("p (s h q) -> p s h q", s=2, h=HG)
        rot = carve(2 * T + P)
        rotv = rot[:, 0:2 * T].rearrange("p (c i d) -> p c i d", c=2, d=D)
        vflat = carve(T + P)
        vall = vflat[:, 0:T].rearrange("p (i d) -> p i d", d=D)
        ctxv = xn[:]
        pads = [carve(2 * ST_ * HG * HR // 2).bitcast(BF16).rearrange("p (s i h c) -> p s i h c", s=2, i=ST_, h=HG)
                for _ in range(2)]
        qpad, kpad = pads
        rests = [carve(ST_ * HG * HD).rearrange("p (i h c) -> p i h c", i=ST_, h=HG) for _ in range(2)]
        qmf = carve(2 * HG // HP * S // 2)
        qm = qmf.bitcast(BF16).rearrange("p (s a t) -> p s a t", s=2, t=S)
        kz = kzf.bitcast(BF16).rearrange("p (s h t) -> p s h t", s=2, h=HG)
        qz = qzf[:, 0:T].bitcast(BF16).rearrange("p (h t) -> p h t", h=HG)
        qT = qzf[:, T:T + S].bitcast(BF16).rearrange("p (a t) -> p a t", t=S)
        kT = [f.bitcast(BF16).rearrange("p (a t) -> p a t", t=S) for f in (qzf[:, T + S:T + 2 * S], table)]
        vpad = carve(2 * ST_ * HG * 32).rearrange("p (s i h c) -> p s i h c", s=2, i=ST_, h=HG)
        oT = carve(2 * 512).rearrange("p (a q) -> p a q", a=2)
        assert top[0] <= kept
        top[0] = 0
        dtp = carve(D // DG * S // 2).bitcast(BF16).rearrange("p (g t) -> p g t", t=S)
        upp = carve(D // DG * S // 2).bitcast(BF16).rearrange("p (g t) -> p g t", t=S)
        sel = carve(DG * P // 2).bitcast(BF16).rearrange("p (r m) -> p r m", m=P)
        bT = carve(S)
        cT = carve(S)
        cz = carve(TR * 32).rearrange("p (t c) -> p t c", c=32)
        ysb = carve(2 * D).rearrange("p (r d) -> p r d", d=D)
        yT = carve(B * TR).rearrange("p (b t) -> p b t", b=B)
        parts = carve(3 * 2 * QT).bitcast(BF16).rearrange("p (v a b t) -> p v a b t", v=2, a=3, b=B)
        prep0 = top[0]
        da = carve(2 * DQ * TR).rearrange("p (s n) -> p s n", s=2)
        hs = carve(2 * DQ * TR).rearrange("p (s n) -> p s n", s=2)
        top[0] = prep0
        xr = carve(T).rearrange("p (i d) -> p i d", d=D)
        xd = carve(T)
        soft = carve(T).rearrange("p (b t) -> p b t", b=B)
        loT = carve(T)[0:RANK].rearrange("p (k t) -> p k t", k=4)
        selftmp = carve(DG * P)
        assert prep0 + 4 * DQ * TR <= kept
        zt = xn[:].rearrange("p i d -> p (i d)").rearrange("p (b t) -> p b t", b=B)
        ut = xnT[:].rearrange("p (b t) -> p b t", b=B)
        ps = ctx.enter_context(nc.psum_tensor("ps", [P, 8, 512], F32))

        consts_in = sem("consts_in")
        later_in = sem("later_in")
        x_in = sem("x_in")
        w_in = [sem(f"w_in{n}") for n in range(SLOTS)]
        relu_weights_in = sem("relu_weights_in")
        identb_ready = sem("identb_ready")
        sel_ready = sem("sel_ready")
        stored = sem("stored")
        x_final = sem("x_final")
        parts_out = sem("parts_out")
        parts_in = sem("parts_in")
        chain = sem("chain")
        chained = [0]
        rstd_ready = sem("rstd_ready")
        pool_step = sem("pool_step")
        pool_steps = [0]

        LN = {k: sem(f"ln_{k}") for k in (
            "step", "waited", "var_ready", "std_ready", "xn_ready", "tp_done", "xnT_ready", "rest_ready", "logitsT_done",
            "logitsT_ready", "logits_done", "shifted", "exp_done", "route_step")}
        MX = {k: sem(f"mix_{k}") for k in (
            "w1_done", "up_parts", "dn_parts", "up_done", "act_done", "rest_vector", "rest_pool", "down_done", "weight_cast", "weight_copied", "y_read",
            "acc_done", "acc_turned", "x_done", "comb_step", "comb_split", "comb_turned", "combT_ready", "waited")}

        def at_least(e, s, v):
            if not (isinstance(v, int) and v <= 0):
                e.wait_ge(s, v)

        RELU = {}
        for name, kind in PLAN:
            if kind == 1:
                RELU[name] = {k: sem(f"{name}_{k}") for k in (
                    "up_done", "act_done", "down_done", "acc_done", "comb_copied", "comb_turned", "combT_ready", "bias_done",
                    "bias_added")}

        stages = []
        count = {"norm": 0, "turn": 0, "route": 0, "act": 0}
        for n, (name, kind) in enumerate(PLAN):
            ready = NTB - 1 if n > 0 and PLAN[n - 1][1] in (0, 1) else 0
            stages.append({"name": name, "kind": kind, "ready": ready, **count})
            count["norm"] += NTB
            count["turn"] += NTB if kind != "scan" else 0
            count["route"] += NTB if kind in (0, 1) else 0
            count["act"] += NTB * E * F0 // P if kind == 0 else 0
        gelus = [st for st in stages if st["kind"] == 0]
        assert all(st["route"] == n * NTB for n, st in enumerate(gelus))
        stage_of = {st["kind"]: st for st in stages if st["kind"] in ("attention", "scan")}

        def tasks_of(st):
            if st["kind"] == "scan":
                return ["stats", "norm"]
            if st["kind"] == "attention":
                return ["stats", "norm", "turn"]
            return ["stats", "norm", "turn", "logits", "logits back", "shift", "route"]

        def opening_tasks(st):
            blocks = range(st["ready"], NTB)
            return [(st, w, g) for g in blocks for w in tasks_of(st)]

        def first_tasks(st):
            if st["ready"]:
                return [], {ex: [(st, w, NTB - 1)] for ex, w in enumerate(tasks_of(st))}
            t = lambda w, g: (st, w, g)
            before = [t("stats", 0), t("norm", 0), t("turn", 0), t("logits", 0), t("stats", 1), t("logits back", 0),
                      t("shift", 0), t("norm", 1), t("route", 0)]
            before = [b for b in before if b not in early_tasks]
            if st["kind"] == 1:
                return (before,
                        {0: [t("turn", 1), t("logits", 1), t("stats", 2)], 1: [t("logits back", 1), t("norm", 2), t("shift", 1)],
                         2: [t("turn", 2), t("route", 1), t("stats", 3)], 3: [t("logits", 2), t("norm", 3)],
                         4: [t("turn", 3), t("logits back", 2), t("shift", 2)], 5: [t("logits", 3), t("route", 2)],
                         6: [t("logits back", 3), t("shift", 3)], 7: [t("route", 3)]})
            before.insert(len(before) - 1, t("stats", 2))
            return (before,
                    {0: [t("turn", 1), t("norm", 2)], 1: [t("logits", 1)],
                     2: [t("logits back", 1), t("turn", 2), t("shift", 1)],
                     3: [t("route", 1), t("stats", 3)], 4: [t("logits", 2), t("norm", 3)],
                     5: [t("turn", 3), t("logits back", 2), t("shift", 2)], 6: [t("logits", 3), t("route", 2)],
                     7: [t("logits back", 3), t("shift", 3)], 8: [t("route", 3)]})

        def next_tasks(st, tb, lag=0):
            if st is None:
                return {}
            return {ex + lag if ex < 4 else ex + 2 * lag: [(st, w, tb - 1)] for ex, w in enumerate(tasks_of(st))}

        AT = {k: sem(f"att_{k}") for k in (
            "qkv_done", "qkv_copied", "qkv_taken", "rotated",
            "masks_ready", "pads_ready", "pads_clear", "parts", "waited", "unit_split", "v_placed", "turned", "turned_copied", "returned",
            "returned_copied", "qz_ready", "kz_ready", "s_done", "max_done", "max_part", "negmax_ready",
            "st_done", "exp_done", "pv_done", "o_copied", "o_turned", "o_summed", "o_normed", "ctxT_turned", "ctxT_ready",
            "proj_done", "proj_added")}
        SC = {k: sem(f"scan_{k}") for k in (
            "arena_free", "sel_in", "sel_ready", "rms_ready", "rms_std", "xr_ready",
            "xr_turned", "xrT_ready", "rows_zeroed", "c_zeroed", "xn_turned", "xd_ready", "bc_done", "lo_done", "bT_ready",
            "c_placed", "waited", "loT_ready", "dt_done", "z_ready", "exp_ready", "ln_ready", "rate_exp", "rate_ready", "u_ready",
            "split0", "split1", "skip_done", "prep_done", "dt_cast", "da_done", "da_cut", "u_cast", "in_done", "h_done", "y_done",
            "y_copied", "y_turned", "yT_ready", "proj_done", "proj_added")}

        block = ctx.enter_context(nc.Block())

        s_blocks = [(h, group, w)
                    for group, w in [([(0, 0), (4, 1)], P), ([(1, 0), (5, 1)], 2 * P), ([(2, 0)], 3 * P),
                                     ([(3, 0)], 4 * P), ([(6, 1)], 3 * P), ([(7, 1)], 4 * P)]
                    + [([(i, 0)], 4 * P) for i in range(4, ST_)]
                    for h in range(HG)]
        NSB = len(s_blocks)
        steps = [(0, j) for j in range(4)] + [(1, j) for j in range(ST_)]
        NST = len(steps)
        NTU = 2 * HG // HP * 2
        NRE = NTU // 2

        def span(m):
            half, j = steps[m]
            q0 = max(0, j * P - half * 512)
            return q0, 512 - q0

        def piece(n):
            return n // 2 % (HG // HP), n % 2

        def turn_items(v):
            return [("turn", v, n) for n in range(NTU)]

        def order(prev, pre, ahead):
            blocks = [("s", 1, n) for n in range(NSB)] if pre else []
            turns = turn_items(2) if ahead else []
            share = [1 if m < NST - 2 else 0 for m in range(NST)]
            for m in range(NST):
                side = blocks[NSB * sum(share[:m]) // sum(share):NSB * sum(share[:m + 1]) // sum(share)]
                yield ("st", 0, 2 * m)
                yield from side[0:1]
                yield from turns[2 * (m - 7):2 * (m - 7) + 1] if m >= 7 else []
                yield ("st", 0, 2 * m + 1)
                yield from side[1:2]
                if m >= 1:
                    yield ("pv", 0, m - 1)
                elif prev:
                    yield ("pv", -1, NST - 1)
                yield from side[2:3]
                yield from turns[2 * (m - 7) + 1:2 * (m - 7) + 2] if m >= 7 else []
                yield from side[3:]
                if m == 1 and prev:
                    yield ("ocopy", -1, 1)
                if m == 2 and prev:
                    yield ("oturn", -1, 1)
                if 4 <= m < 4 + HG and pre:
                    yield ("kz", 1, m - 4)
                if m == 5:
                    yield ("ocopy", 0, 0)
                if m == 6:
                    yield ("oturn", 0, 0)
                if m == NST - 1:
                    if pre:
                        yield from [("returned", 1, n) for n in range(NRE)]
                    if ahead:
                        yield from [("qz", 2, pair) for pair in range(HG // HP)]

        EARLY = NTB - NTB // B
        after = [stages[n + 1] for n, st in enumerate(stages[:-1]) if st["kind"] == "attention"]
        early_tasks = [(after[0], "stats", 0), (after[0], "norm", 0), (after[0], "stats", 1)] if after else []

        def last():
            extra = {1: [("ctx", 0, 0)], 2: [("ctx", 0, 1), ("proj", 0, 0)], 3: [("proj", 0, 1)],
                     **{5 + n: [("task", 0, n)] for n in range(len(early_tasks))}}
            m = -1
            for what, k, n in order(True, False, False):
                if what == "st" and n % 2 == 0:
                    yield from extra.get(m, [])
                    m += 1
                yield what, k, n

        def opening():
            yield from turn_items(0)
            yield from [("qz", 0, pair) for pair in range(HG // HP)]
            yield from [("kz", 0, h) for h in range(HG)]
            yield from [("s", 0, n) for n in range(NSB)]
            yield from turn_items(1)
            yield from [("returned", 0, n) for n in range(NRE)]
            yield from [("qz", 1, pair) for pair in range(HG // HP)]

        closing = [("pv", -1, NST - 1), ("ocopy", -1, 1), ("oturn", -1, 1)]

        def units(go):
            def word(i, k):
                return (i + k // 2) // 2 * (ST_ * D) + (i + k // 2) % 2 * (2 * HG * HD) + k % 2 * (HG * HD)
            go(opening(), 0, 0, lambda k: word(0, k), True)
            go(order(False, True, True), 0, 0, lambda k: word(0, k))
            with go.engine.Fori(0, (NU - 4) // 2) as i:
                go(order(True, True, True), 2 * i + 1, 1, lambda k: word(i, 1 + k))
                go(order(True, True, True), 2 * i + 2, 0, lambda k: word(i, 2 + k))
            go(order(True, True, True), NU - 3, 1, lambda k: word(0, NU - 3 + k))
            go(order(True, True, False), NU - 2, 0, lambda k: word(0, NU - 2 + k))
            go(last(), NU - 1, 1, lambda k: word(0, NU - 1 + k))
            go(closing, NU, 0, lambda k: word(0, NU + k))

        @block.sync
        def _(sp):
            sp.dma_start(x[:], t_in["x"].rearrange("(i p) d -> p i d", p=P)).then_inc(x_in, 16)
            for dst, name in ((ident[:], "ident"), (rw[0][:], "rw0"), (rw[1][:], "rw1"), (b2r[:], "b2")):
                sp.dma_start(dst, t_in[name]).then_inc(consts_in, 16)
            sp.dma_start(rb[0][:], t_in["rb0"].partition_broadcast(P)).then_inc(consts_in, 16)
            sp.dma_start(rb[1][:], t_in["rb1"].partition_broadcast(P)).then_inc(consts_in, 16)
            sp.dma_start(earlier[:], t_in["earlier"].partition_broadcast(P)).then_inc(consts_in, 16)
            sp.dma_start(b1c[:], t_in["b1"]).then_inc(consts_in, 16)
            def gelu_weights(st, experts):
                for ex in experts:
                    n = st["route"] // NTB * E + ex
                    at_least(sp, MX["dn_parts"], n - SLOTS + 1)
                    for w, name in enumerate(("up0", "dn0")):
                        sp.dma_start(stage_w[:, n % SLOTS, w, :], t_in[name][:, ex]).then_inc(w_in[n % SLOTS], 16)
            for st in gelus[:1]:
                gelu_weights(st, range(SLOTS))
            for dst, name in ((wqkv, "wqkv"), (wo, "wo"), (cos, "cos"), (sin, "sin"), (maskf, "masks")):
                sp.dma_start(dst[:], t_in[name]).then_inc(later_in, 16)
            for n, name in enumerate(("bq", "bk", "bv")):
                sp.dma_start(bqkv[:, n * D:(n + 1) * D], t_in[name].partition_broadcast(P)).then_inc(later_in, 16)
            sp.dma_start(bo[:], t_in["bo"].partition_broadcast(P)).then_inc(later_in, 16)
            for dst, name in ((xpw, "xpw"), (dtw, "dtw"), (dtb, "dtb"), (dskip, "dskip"), (opw, "opw"),
                              (arate, "a_log")):
                sp.dma_start(dst[:], t_in[name]).then_inc(later_in, 16)
            sp.dma_start(nw[:], t_in["norm_w"].partition_broadcast(P)).then_inc(later_in, 16)
            for n, st in enumerate(gelus):
                gelu_weights(st, range(0 if n else SLOTS, E))
            at_least(sp, MX["dn_parts"], len(gelus) * E)
            for dst, name in ((up1, "up1"), (dn1, "dn1")):
                sp.dma_start(dst, t_in[name]).then_inc(relu_weights_in, 16)
            if "scan" in stage_of:
                sp.wait_ge(SC["arena_free"], 1)
                sp.dma_start(selftmp[0:ROWS, :], t_in["sel"]).then_inc(SC["sel_in"], 16)
                for k in range(4):
                    for v, dst in enumerate((dtp, upp)):
                        sp.wait_ge(SC[f"split{v}"], k + 1)
                        sp.dma_start(scratch[k, v].rearrange("a d b t -> d a b t"), parts[:, v]).then_inc(parts_out, 16)
                        sp.wait_ge(parts_out, 16 * (2 * k + v + 1))
                        for b in range(B):
                            for a in range(3):
                                r0 = (b * 3 + a) * DG
                                sp.dma_start(dst[r0:r0 + DG, :, k * QT:(k + 1) * QT],
                                             scratch[k, v, a, :, b].rearrange("(g r) t -> r g t", r=DG)
                                             ).then_inc(parts_in, 16)
            sp.wait_ge(x_final, 1)
            sp.dma_start(out.rearrange("(i p) d -> p i d", p=P), x[:]).then_inc(stored, 16)
            sp.wait_ge(stored, 16)

        def task_tensor(e, st, what, g):
            if what == "turn":
                n = st["turn"] + g
                e.wait_ge(LN["xn_ready"], st["norm"] + g + 1)
                if not (isinstance(n, int) and n == 0):
                    e.wait_ge(LN["xnT_ready"], n)
                for j in range(TPB):
                    mm = e.transpose(ps[:, 6, j * P:(j + 1) * P], xn[:, j, :], ident[:])
                mm.then_inc(LN["tp_done"], 1)
            elif what == "logits":
                n = st["route"] + g
                e.wait_ge(LN["xnT_ready"], st["turn"] + g + 1)
                if not (isinstance(n, int) and n == 0):
                    e.wait_ge(LN["shifted"], n)
                e.matmul(ps[0:E, 7, :], rw[st["kind"]][:], xnT[:, bass.ts(g, TB)], start=True, stop=True
                         ).then_inc(LN["logitsT_done"], 1)
            elif what == "logits back":
                e.wait_ge(LN["logitsT_ready"], st["route"] + g + 1)
                for j in range(TPB):
                    mm = e.matmul(ps[:, 7, j * E:(j + 1) * E], logitsT[:, j * P:(j + 1) * P], ident[0:E, 0:E],
                                  start=True, stop=True)
                mm.then_inc(LN["logits_done"], 1)

        def gelu_mixture_tensor(e, st, nxt):
            nf = F0 // P
            before, along = first_tasks(st)
            for task in before:
                task_tensor(e, *task)

            def turn_sum(tb):
                e.wait_ge(MX["acc_done"], (E - 1) * (st["route"] + tb + 1))
                turned = st["turn"] + NTB + (tb - 1 if nxt and nxt["kind"] != "scan" else 0)
                e.wait_ge(LN["xnT_ready"], turned if not isinstance(tb, int) or tb > 0 else st["turn"] + NTB)
                for j in range(TPB):
                    mm = e.transpose(ps[:, 6, j * P:(j + 1) * P], acc[:, j * P:(j + 1) * P], ident[:])
                mm.then_inc(MX["acc_turned"], 1)

            def products(out, left, right, first, last):
                for n, (a, b) in enumerate(((0, 0), (0, 1), (1, 0))):
                    mm = e.matmul(out, left(a), right(b), start=(first and n == 0), stop=(last and n == 2))
                return mm

            def block(tb, tasks, first):
                blk = st["route"] + tb
                for ex in range(E + 1):
                    n = blk * E + ex
                    if ex == 0:
                        e.wait_ge(LN["rest_ready"], blk + 1)
                    if ex < E:
                        if first:
                            e.wait_ge(MX["up_parts"], n - st["route"] * E + st["route"] // NTB * E + 1)
                        for fc in range(nf):
                            m = st["act"] + tb * (E * nf) + ex * nf + fc
                            at_least(e, MX["act_done"], m - nf + 1)
                            products(ps[:, fc, :], lambda a: wup[:, a, ex, fc * P:(fc + 1) * P],
                                     lambda b: xp[:, b, bass.ts(tb, TB)], True, True).then_inc(MX["up_done"], 1)
                    if ex == 1 and not first:
                        turn_sum(tb - 1)
                    if ex == 0:
                        e.wait_ge(MX["comb_split"], blk + 1)
                        at_least(e, MX["y_read"], n)
                        for j in range(TPB):
                            mm = e.matmul(ps[0:3 * CP, 5, j * P:(j + 1) * P], comb3[:, j].rearrange("p a c -> p (a c)"),
                                          identb[:], start=True, stop=True)
                        mm.then_inc(MX["comb_turned"], 1)
                    if ex >= 1:
                        k = ex - 1
                        if k == 0:
                            e.wait_ge(MX["combT_ready"], blk + 1)
                        at_least(e, MX["y_read"], blk * E + k)
                        e.matmul(ps[:, 5, :], sel_e[0:3 * CP, k, :], comb3T, start=True, stop=True
                                 ).then_inc(MX["weight_cast"], 1)
                        half = (st["act"] + tb * (E * nf) + k * nf) // 2 if isinstance(tb, int) else \
                            tb * (E * nf // 2) + (st["act"] + k * nf) // 2
                        e.wait_ge(MX["rest_vector"], half + nf // 2)
                        e.wait_ge(MX["rest_pool"], half + nf // 2)
                        if first:
                            e.wait_ge(MX["dn_parts"], st["route"] // NTB * E + k + 1)
                        for fc in range(nf):
                            mm = products(ps[:, 4, :], lambda a: wdn[:, a, k, fc, :], lambda b: hr[:, k % 2, b, fc, :],
                                          fc == 0, fc == nf - 1)
                        mm.then_inc(MX["down_done"], 1)
                    for task in tasks.get(ex, []):
                        task_tensor(e, *task)

            block(0, along, True)
            with e.Fori(1, NTB - 1) as tb:
                block(tb, next_tasks(nxt, tb, 1), False)
            block(NTB - 1, next_tasks(nxt, NTB - 1, 1), False)
            turn_sum(NTB - 1)

        def relu_mixture_tensor(e, st, nxt):
            s = RELU[st["name"]]
            nf = F1 // P
            before, along = first_tasks(st)
            for task in before:
                task_tensor(e, *task)
            if st["ready"]:
                e.wait_ge(LN["xnT_ready"], st["turn"] + 1)
            e.sem_inc(s["down_done"], 2)
            e.wait_ge(relu_weights_in, 32)

            def block(tb, tasks):
                for ex in range(E + 1):
                    if ex == 0:
                        e.wait_ge(LN["xnT_ready"], st["turn"] + tb + 1)
                    if ex < E:
                        for fc in range(nf):
                            e.wait_ge(s["act_done"], tb * (E * nf) + ex * nf + fc + 1)
                            e.matmul(ps[:, fc, :], up1[:, ex, fc * P:(fc + 1) * P], xnT[:, bass.ts(tb, TB)],
                                     start=True, stop=True).then_inc(s["up_done"], 1)
                    if ex >= 1:
                        k = ex - 1
                        e.wait_ge(s["acc_done"], tb * E + k + 1)
                        e.wait_ge(s["act_done"], tb * (E * nf) + (k + 2) * nf)
                        for j in range(TPB):
                            for fc in range(nf):
                                mm = e.matmul(ps[:, 4 + k % 2, j * P:(j + 1) * P],
                                              hid[:, k % 2, fc, j * P:(j + 1) * P], dn1[:, k, fc, :],
                                              start=(fc == 0), stop=(fc == nf - 1))
                        mm.then_inc(s["down_done"], 1)
                    for task in tasks.get(ex, []):
                        task_tensor(e, *task)
                    if ex == 1:
                        e.wait_ge(s["comb_copied"], tb + 1)
                        for j in range(TPB):
                            mm = e.transpose(ps[0:E, 2, j * P:(j + 1) * P], combnow[:, j, :], ident[:])
                        mm.then_inc(s["comb_turned"], 1)
                    if ex == 3:
                        e.wait_ge(s["combT_ready"], tb + 1)
                        e.wait_ge(s["bias_added"], tb + 1)
                        for j in range(TPB):
                            mm = e.matmul(ps[:, 3, j * P:(j + 1) * P], combT[:, j * P:(j + 1) * P], b2r[:],
                                          start=True, stop=True)
                        mm.then_inc(s["bias_done"], 1)

            block(0, along)
            with e.Fori(1, NTB) as tb:
                block(tb, next_tasks(nxt, tb))

        def unit_tensor(e, items, u, par, first):
            for what, k, n in items:
                v, vp = u + k, (par + k) % 2
                if what == "turn":
                    pair, half = piece(n)
                    if n == 0:
                        e.wait_ge(AT["unit_split"], 2 * v + 2)
                    bank = 6 + n % 2 if first else 6
                    if n == 0 and not first:
                        e.wait_ge(AT["o_normed"], 2 * v - 1)
                    elif first:
                        if n >= 2 or k == 1:
                            e.wait_ge(AT["turned_copied"], NTU * v + n - 1)
                    else:
                        e.wait_ge(AT["turned_copied"], NTU * v + n)
                    for j in range(4):
                        mm = e.matmul(ps[:, bank, j * P:(j + 1) * P],
                                      pads[n // NRE][:, vp, 4 * half + j, HP * pair:HP * pair + HP, :].rearrange("p h c -> p (h c)"),
                                      identb[:], start=True, stop=True)
                    mm.then_inc(AT["turned"], 1)
                elif what == "returned":
                    pair, half = n % 2, n // 2
                    if n == 0:
                        e.wait_ge(AT["negmax_ready"], v + 1)
                    if n >= 2:
                        e.wait_ge(AT["returned_copied"], NRE * v + n - 1)
                    for j in range(4):
                        mm = e.matmul(ps[:, n % 2, j * P:(j + 1) * P],
                                      qpad[:, vp, 4 * half + j, HP * pair:HP * pair + HP, :].rearrange("p h c -> p (h c)"),
                                      identb[:], start=True, stop=True)
                    mm.then_inc(AT["returned"], 1)
                elif what == "s":
                    h, group, w = s_blocks[n]
                    if n == 0:
                        e.wait_ge(AT["turned_copied"], NTU * v + NTU)
                        e.wait_ge(AT["qz_ready"], 2 * v + 2)
                        if not (first and k == 0):
                            e.wait_ge(AT["returned_copied"], NRE * v)
                    elif n >= 2:
                        e.wait_ge(AT["max_done"], NSB * v + n - 1)
                    for m, (i, half) in enumerate(group):
                        diag = i // 4 == half
                        mm = e.matmul(ps[:, n % 2, m * w:(m + 1) * w], qz[:, h, i * P:(i + 1) * P],
                                      kT[vp][:, h // HP, half * 512:half * 512 + w], start=True, stop=not diag)
                        if diag:
                            mm = e.matmul(ps[:, n % 2, (m + 1) * w - P:(m + 1) * w], identb[:], hide_q[:],
                                          start=False, stop=True)
                    mm.then_inc(AT["s_done"], 1)
                elif what == "st":
                    m, pair = n // 2, n % 2
                    half, j = steps[m]
                    q0, w = span(m)
                    if n == 0:
                        e.wait_ge(AT["returned_copied"], NRE * v + NRE // 2)
                        e.wait_ge(AT["kz_ready"], v + 1)
                    if pair == 0 and steps[m] == (1, 0):
                        e.wait_ge(AT["returned_copied"], NRE * v + NRE)
                    e.wait_ge(AT["exp_done"], 2 * NST * v + n + 1)
                    for h in range(2):
                        bank = 2 + 2 * pair + h
                        diag = j // 4 == half
                        mm = e.matmul(ps[:, bank, 0:w], kz[:, vp, 2 * pair + h, j * P:(j + 1) * P],
                                      qm[:, vp, pair, half * 512 + q0:half * 512 + 512], start=True, stop=not diag)
                        if diag:
                            mm = e.matmul(ps[:, bank, 0:P], identb[:], hide_k[:], start=False, stop=True)
                    mm.then_inc(AT["st_done"], 1)
                elif what == "pv":
                    half, j = steps[n]
                    q0, w = span(n)
                    e.wait_ge(AT["exp_done"], 2 * NST * v + 2 * n + 4)
                    if n == 0:
                        e.wait_ge(AT["v_placed"], v + 1)
                    if j == 0:
                        e.wait_ge(AT["o_normed"], 2 * v + half + 1)
                    if n == 0:
                        e.wait_ge(AT["turned_copied"], min(v + 2, NU) * NTU if isinstance(v, int) else NTU * v + 2 * NTU)
                    for h in range(HG):
                        mm = e.matmul(ps[32 * h:32 * h + 32, 6 + half, q0:512], vpad[:, vp, j, h, :],
                                      probT[:, n % 2, h, 0:w], start=(j == 0), stop=(w == P),
                                      skip_group_check=True)
                    mm.then_inc(AT["pv_done"], 1)
                elif what == "ctx":
                    if n == 0:
                        e.wait_ge(AT["o_normed"], 2 * (NU // B) + 2)
                        e.wait_ge(AT["returned_copied"], NRE * NU)
                    context(e, n)
                elif what == "proj":
                    project(e, n, n)
                elif what == "task":
                    task_tensor(e, *early_tasks[n])
                elif what == "oturn":
                    e.wait_ge(AT["o_copied"], 2 * v + n + 1)
                    for j in range(4):
                        mm = e.transpose(ps[:, 6 + n, j * P:(j + 1) * P], oT[:, n, j * P:(j + 1) * P], ident[:])
                    mm.then_inc(AT["o_turned"], 1)

        def context(e, g):
            for j in range(TPB):
                mm = e.transpose(ps[:, g % 2, j * P:(j + 1) * P], ctxv[:, TPB * g + j, :], ident[:])
            mm.then_inc(AT["ctxT_turned"], 1)

        def project(e, g, bank):
            e.wait_ge(AT["ctxT_ready"], g + 1)
            for j in range(TPB):
                i = TPB * g + j
                mm = e.matmul(ps[:, bank, j * P:(j + 1) * P], xnT[:, i * P:(i + 1) * P], wo[:], start=True, stop=True)
            mm.then_inc(AT["proj_done"], 1)

        def attention_tensor(e):
            st = stage_of["attention"]
            for task in opening_tasks(st):
                task_tensor(e, *task)
            for i in range(NT):
                e.wait_ge(LN["xnT_ready"], st["turn"] + i // TPB + 1)
                if 4 <= i < ST_ + 4:
                    e.wait_ge(AT["qkv_copied"], 2 * (i - 3))
                elif i >= 4:
                    e.wait_ge(AT["qkv_taken"], 2 * (i - 3 - ST_))
                e.matmul(ps[:, i % 4, 0:3 * D], xnT[:, i * P:(i + 1) * P], wqkv[:],
                         start=True, stop=True).then_inc(AT["qkv_done"], 1)
            e.wait_ge(AT["masks_ready"], 2)
            e.wait_ge(AT["qkv_taken"], 2 * (NT - ST_))
            e.sem_inc(AT["pv_done"], 2)
            def go(items, u, par, at, first=False):
                unit_tensor(e, items, u, par, first)
            go.engine = e
            units(go)
            e.wait_ge(AT["o_normed"], 2 * NU + 2)
            for g in range(EARLY, NTB):
                e.wait_ge(AT["proj_added"], g - 1)
                context(e, g)
            for g in range(EARLY, NTB):
                project(e, g, 2 + g)

        def spread(e, bank, j, r, operand, g0, t0):
            return e.matmul(ps[:, bank, j * TR:(j + 1) * TR], sel[:, r % DG, :],
                            operand.rearrange("p g t -> p (g t)")[:, bass.ds(g0 + r // DG * S + t0, TR)],
                            start=True, stop=True)

        def spread_dt(e, q, n, g0, t0):
            e.wait_ge(SC["da_done"], 8 * q + n + 1)
            for j in range(4):
                mm = spread(e, n % 2, j, 4 * n + j, dtp, g0, t0)
            mm.then_inc(SC["dt_cast"], 1)

        def spread_u(e, q, c, g0, t0):
            e.wait_ge(SC["in_done"], 4 * q + c + 1)
            for k in range(2):
                for j in range(4):
                    mm = spread(e, 2 + 2 * (c % 2) + k, j, 8 * c + 4 * k + j, upp, g0, t0)
            mm.then_inc(SC["u_cast"], 1)

        def scan_out(e, q, par, tr, n):
            if n == 0:
                e.wait_ge(SC["h_done"], q + 3)
                e.wait_ge(SC["c_placed"], 2 * tr + 2)
                e.wait_ge(SC["y_copied"], q + 2)
            h = hs[:, par, :].rearrange("p (d t) -> p d t", t=TR)
            rb = n // 4
            for k in range(4 * (n % 4), 4 * (n % 4) + 4):
                for j in range(4):
                    t = rb * 64 + j * 16 + k
                    mm = e.matmul(ps[32 * j:32 * j + 32, 6, rb * DQ:(rb + 1) * DQ], cz[:, t, :], h[:, :, t], start=(k == 0), stop=(k == 15), skip_group_check=True)
            if n == 7:
                mm.then_inc(SC["y_done"], 1)

        def scan_turn(e, tr):
            e.wait_ge(SC["y_copied"], NDQ * tr + NDQ + 2)
            e.wait_ge(SC["proj_added"], tr + 1)
            for rb in range(2):
                mm = e.transpose(ps[:, 7, rb * P:(rb + 1) * P], ysb[:, rb, :], ident[:])
            mm.then_inc(SC["y_turned"], 1)

        def scan_project(e, tr):
            e.wait_ge(SC["yT_ready"], tr + 1)
            for b in range(B):
                mm = e.matmul(ps[:, 7, (2 + b) * D:(3 + b) * D], yT[:, b, :], opw[:], start=True, stop=True)
            mm.then_inc(SC["proj_done"], 1)

        def scan_step(e, q, dq, tr, first=False, last=False):
            here = (dq * 2 * S, tr * TR)
            after = ((dq + 1) % NDQ * 2 * S, (tr + (dq + 1) // NDQ) * TR)
            if dq == NDQ - 1 and not last:
                e.wait_ge(parts_in, 16 * 12 * ((tr + 1) // 2 + 1))
            for n in range(8):
                if not (last and dq == NDQ - 1):
                    spread_dt(e, q + 1, n, *after)
                if n == 1:
                    spread_u(e, q, 2, *here)
                if n == 3:
                    spread_u(e, q, 3, *here)
                if not (first and dq == 0):
                    scan_out(e, q - 1, (dq + 1) % 2, tr if dq >= 1 else tr - 1, n)
                if n == 4 and not first and dq == 1:
                    scan_turn(e, tr - 1)
                if n == 4 and not first and dq == 2:
                    scan_project(e, tr - 1)
                if not (last and dq == NDQ - 1) and n in (5, 7):
                    spread_u(e, q + 1, (n - 5) // 2, *after)

        def scan_tensor(e):
            for g in range(NTB):
                for j in range(TPB):
                    e.wait_ge(SC["xr_ready"], TPB * g + j + 1)
                    mm = e.transpose(ps[:, g, j * P:(j + 1) * P], xr[:, TPB * g + j, :], ident[:])
                mm.then_inc(SC["xr_turned"], 1)
            for g in range(NTB):
                for j in range(TPB):
                    mm = e.transpose(ps[:, 4 + g, j * P:(j + 1) * P], xn[:, TPB * g + j, :], ident[:])
                mm.then_inc(SC["xn_turned"], 1)
            e.wait_ge(SC["xrT_ready"], NTB)
            for k in range(4):
                e.matmul(ps[0:RANK, k, :], xpw[:, 0:RANK], ut[:, :, k * QT:(k + 1) * QT],
                         start=True, stop=True).then_inc(SC["lo_done"], 1)
            for k in range(4):
                e.wait_ge(SC["loT_ready"], k + 1)
                e.matmul(ps[:, k, :], dtw[:], loT[:, k, :], start=True, stop=True).then_inc(SC["dt_done"], 1)
            e.wait_ge(SC["xd_ready"], NTB)
            for c in range(2):
                for h in range(2):
                    for b in range(B):
                        mm = e.matmul(ps[64 * b:64 * b + 64, 4 + 2 * c + h, :],
                                      xpw[:, RANK + c * STATE:RANK + (c + 1) * STATE],
                                      ut[:, b, h * 512:(h + 1) * 512], start=True, stop=True)
                mm.then_inc(SC["bc_done"], 1)
            e.wait_ge(SC["z_ready"], 4)
            for i in range(NT):
                mm = e.matmul(ps[:, i // TPB, i % TPB * P:(i % TPB + 1) * P], xd[:, i * P:(i + 1) * P], opw[:],
                              start=True, stop=True)
            mm.then_inc(SC["skip_done"], 1)
            e.wait_ge(SC["prep_done"], 1)
            e.wait_ge(SC["bT_ready"], 2)
            e.wait_ge(SC["sel_ready"], 1)
            e.wait_ge(SC["rows_zeroed"], 1)
            e.wait_ge(parts_in, 16 * 12)
            e.sem_inc(SC["y_done"], 2)
            for n in range(8):
                spread_dt(e, 0, n, 0, 0)
            for c in range(2):
                spread_u(e, 0, c, 0, 0)
            for dq in range(NDQ):
                scan_step(e, dq, dq, 0, first=True)
            with e.Fori(1, NTR - 1) as tr:
                for dq in range(NDQ):
                    scan_step(e, tr * NDQ + dq, dq, tr)
            for dq in range(NDQ):
                scan_step(e, NSU - NDQ + dq, dq, NTR - 1, last=True)
            for n in range(8):
                scan_out(e, NSU - 1, 1, NTR - 1, n)
            scan_turn(e, NTR - 1)
            scan_project(e, NTR - 1)

        def run_stages(e, attention, scan, gelu_mixture, relu_mixture):
            later = [n for n, st in enumerate(stages) if n > 0 or st["kind"] != 0][:1]
            for n, st in enumerate(stages):
                if n in later:
                    e.wait_ge(later_in, LATER)
                if st["kind"] == "attention":
                    attention(e)
                elif st["kind"] == "scan":
                    scan(e)
                else:
                    mixture = relu_mixture if st["kind"] == 1 else gelu_mixture
                    mixture(e, st, stages[n + 1] if n + 1 < len(stages) else None)

        @block.tensor
        def _(e):
            e.wait_ge(consts_in, CONSTS)
            e.wait_ge(identb_ready, 1)
            e.wait_ge(sel_ready, 1)
            run_stages(e, attention_tensor, scan_tensor, gelu_mixture_tensor, relu_mixture_tensor)

        def task_scalar(e, st, what, g):
            if what == "stats":
                e.wait_ge(LN["var_ready"], st["norm"] + g + 1)
                e.activation(std[:, 0:TPB], veps[:, 0:TPB], ACT.Sqrt).then_inc(LN["std_ready"], 1)
            elif what == "turn":
                e.wait_ge(LN["tp_done"], st["turn"] + g + 1)
                if st["kind"] == 0:
                    e.copy(xp[:, 0, bass.ts(g, TB)], ps[:, 6, :])
                e.copy(xnT[:, bass.ts(g, TB)], ps[:, 6, :]).then_inc(LN["xnT_ready"], 1)
            elif what == "logits":
                e.wait_ge(LN["logitsT_done"], st["route"] + g + 1)
                e.copy(logitsT[:], ps[0:E, 7, :]).then_inc(LN["logitsT_ready"], 1)
            elif what == "shift":
                e.wait_ge(LN["shifted"], st["route"] + g + 1)
                e.activation(lg[:], lg[:], ACT.Exp).then_inc(LN["exp_done"], 1)

        def gelu_mixture_scalar(e, st, nxt):
            nf = F0 // P
            before, along = first_tasks(st)
            for task in before:
                task_scalar(e, *task)

            def block(tb, tasks):
                blk = st["route"] + tb
                for ex in range(E):
                    at_least(e, MX["down_done"], blk * E + ex - 1)
                    for fc in range(nf):
                        e.wait_ge(MX["up_done"], st["act"] + tb * (E * nf) + ex * nf + fc + 1)
                        for to in (hid[:, ex % 2, fc, :], hr[:, ex % 2, 0, fc, :]):
                            a = e.activation(to, ps[:, fc, :], ACT.Gelu)
                        a.then_inc(MX["act_done"], 1)
                    if ex == 0:
                        e.wait_ge(MX["comb_turned"], blk + 1)
                        e.copy(comb3T, ps[0:3 * CP, 5, :]).then_inc(MX["combT_ready"], 1)
                    for task in tasks.get(ex, []):
                        task_scalar(e, *task)

            block(0, along)
            with e.Fori(1, NTB - 1) as tb:
                block(tb, next_tasks(nxt, tb, 1))
            block(NTB - 1, next_tasks(nxt, NTB - 1, 1))

        def relu_mixture_scalar(e, st, nxt):
            s = RELU[st["name"]]
            nf = F1 // P
            before, along = first_tasks(st)
            for task in before:
                task_scalar(e, *task)
            e.sem_inc(s["act_done"], nf)

            def block(tb, tasks):
                for ex in range(E):
                    e.wait_ge(s["down_done"], tb * E + ex + 1)
                    for fc in range(nf):
                        e.wait_ge(s["up_done"], tb * (E * nf) + ex * nf + fc + 1)
                        e.activation(hid[:, ex % 2, fc, :], ps[:, fc, :], ACT.Relu, bias=b1c[:, ex, fc:fc + 1]
                                     ).then_inc(s["act_done"], 1)
                    for task in tasks.get(ex, []):
                        task_scalar(e, *task)
                    if ex == 1:
                        e.wait_ge(s["comb_turned"], tb + 1)
                        e.wait_ge(s["bias_added"], tb + 1)
                        e.copy(combT, ps[0:E, 2, :]).then_inc(s["combT_ready"], 1)

            block(0, along)
            with e.Fori(1, NTB) as tb:
                block(tb, next_tasks(nxt, tb))

        def unit_scalar(e, items, u, par, first):
            for what, k, n in items:
                v, vp = u + k, (par + k) % 2
                if what == "turn":
                    pair, half = piece(n)
                    if n == 0 and not (first and k == 0):
                        e.wait_ge(AT["qz_ready"], 2 * v)
                    if n == NRE and first and k == 1:
                        e.wait_ge(AT["rotated"], 2)
                    if n == NRE and not first:
                        e.wait_ge(AT["kz_ready"], v - 1)
                    e.wait_ge(AT["turned"], NTU * v + n + 1)
                    e.copy((qT if n < NRE else kT[vp])[:, pair, half * 512:half * 512 + 512],
                           ps[:, 6 + n % 2 if first else 6, :]).then_inc(AT["turned_copied"], 1)
                elif what == "returned":
                    pair, half = n % 2, n // 2
                    e.wait_ge(AT["returned"], NRE * v + n + 1)
                    e.copy(qm[:, vp, pair, half * 512:half * 512 + 512],
                           ps[:, n % 2, :]).then_inc(AT["returned_copied"], 1)
                elif what == "st":
                    m, pair = n // 2, n % 2
                    q0, w = span(m)
                    if pair == 0:
                        e.wait_ge(AT["pv_done"], NST * v + m + 1)
                    e.wait_ge(AT["st_done"], 2 * NST * v + n + 1)
                    e.activation(probT[:, m % 2, 2 * pair:2 * pair + 2, 0:w],
                                 ps[:, 2 + 2 * pair:4 + 2 * pair, 0:w], ACT.Exp,
                                 scale=SCALE).then_inc(AT["exp_done"], 1)
                elif what == "ctx":
                    e.wait_ge(AT["ctxT_turned"], n + 1)
                    e.copy(xnT[:, n * TB:(n + 1) * TB], ps[:, n % 2, :]).then_inc(AT["ctxT_ready"], 1)
                elif what == "task":
                    task_scalar(e, *early_tasks[n])
                elif what == "ocopy":
                    e.wait_ge(AT["pv_done"], NST * v + (4, NST)[n] + 2)
                    e.copy(oT[:, n, :], ps[:, 6 + n, :]).then_inc(AT["o_copied"], 1)

        def attention_scalar(e):
            for task in opening_tasks(stage_of["attention"]):
                task_scalar(e, *task)
            e.copy(hide_q[:], maskf[:, 0, :]).then_inc(AT["masks_ready"], 1)
            e.copy(hide_k[:], maskf[:, 1, :]).then_inc(AT["masks_ready"], 1)
            for i in range(ST_, NT):
                e.wait_ge(AT["qkv_done"], i + 1)
                e.copy(qk[:, i].rearrange("p c d -> p (c d)"), ps[:, i % 4, 0:2 * D]).then_inc(AT["qkv_taken"], 1)
                e.copy(vall[:, i, :], ps[:, i % 4, 2 * D:3 * D]).then_inc(AT["qkv_taken"], 1)
            e.sem_inc(AT["exp_done"], 2)
            def go(items, u, par, at, first=False):
                unit_scalar(e, items, u, par, first)
            go.engine = e
            units(go)
            for g in range(EARLY, NTB):
                e.wait_ge(AT["ctxT_turned"], g + 1)
                e.copy(xnT[:, g * TB:(g + 1) * TB], ps[:, g % 2, :]).then_inc(AT["ctxT_ready"], 1)

        def scan_exp(e, q, dq):
            e.wait_ge(SC["h_done"], q + 1)
            for n in range(8):
                e.wait_ge(SC["dt_cast"], 8 * q + n + 1)
                for j in range(4):
                    r = 4 * n + j
                    ins = e.activation(da[:, dq % 2, r * TR:(r + 1) * TR], ps[:, n % 2, j * TR:(j + 1) * TR], ACT.Exp,
                                       scale=arate[:, dq * DQ + r:dq * DQ + r + 1])
                ins.then_inc(SC["da_done"], 1)

        def scan_keep(e, q, dq, tr, first=False):
            e.wait_ge(SC["y_done"], q + 3)
            if dq == 0 and not first:
                e.wait_ge(SC["y_turned"], tr)
            e.copy(ysb[:, :, dq * DQ:(dq + 1) * DQ], ps[:, 6, 0:2 * DQ].rearrange(
                "p (r d) -> p r d", d=DQ)).then_inc(SC["y_copied"], 1)

        def scan_turned(e, tr):
            e.wait_ge(SC["y_turned"], tr + 1)
            e.wait_ge(SC["proj_added"], tr + 1)
            e.copy(yT.rearrange("p b (g k) -> p b g k", k=16),
                   ps[:, 7, 0:B * TR].rearrange("p (g b k) -> p b g k", b=B, k=16)).then_inc(SC["yT_ready"], 1)

        def scan_scalar(e):
            for task in opening_tasks(stage_of["scan"]):
                task_scalar(e, *task)
            e.wait_ge(SC["rms_ready"], 1)
            e.activation(std[:], veps[:], ACT.Sqrt).then_inc(SC["rms_std"], 1)
            for g in range(NTB):
                e.wait_ge(SC["xr_turned"], g + 1)
                e.copy(xnT[:, g * TB:(g + 1) * TB], ps[:, g, :]).then_inc(SC["xrT_ready"], 1)
            e.wait_ge(SC["xrT_ready"], NTB)
            for k in range(4):
                e.wait_ge(SC["lo_done"], k + 1)
                e.copy(loT[:, k, :], ps[0:RANK, k, :]).then_inc(SC["loT_ready"], 1)
            for g in range(NTB):
                e.wait_ge(SC["xn_turned"], g + 1)
                e.activation(xd[:, g * TB:(g + 1) * TB], ps[:, 4 + g, :], ACT.Copy,
                             scale=dskip[:, 0:1]).then_inc(SC["xd_ready"], 1)
            for n, (k0, k1) in enumerate(((0, 1), (1, 4))):
                sl = soft[:, :, k0 * QT:k1 * QT]
                e.wait_ge(SC["z_ready"], k1)
                e.activation(sl, sl, ACT.Exp, scale=-1.0).then_inc(SC["exp_ready"], 1)
                e.wait_ge(SC["exp_ready"], n + 1)
                e.activation(sl, sl, ACT.Ln, bias=1.0).then_inc(SC["ln_ready"], 1)
            e.wait_ge(SC["bc_done"], 1)
            e.copy(bT, ps[:, 4:6, :].rearrange("p a b -> p (a b)")).then_inc(SC["bT_ready"], 1)
            e.wait_ge(SC["bc_done"], 2)
            e.copy(cT, ps[:, 6:8, :].rearrange("p a b -> p (a b)")).then_inc(SC["bT_ready"], 1)
            e.activation(arate[:], arate[:], ACT.Exp).then_inc(SC["rate_exp"], 1)
            e.wait_ge(SC["sel_in"], 16)
            e.copy(sel[0:ROWS].rearrange("p r m -> p (r m)"), selftmp[0:ROWS, :]).then_inc(SC["sel_ready"], 1)
            e.wait_ge(SC["prep_done"], 1)
            e.wait_ge(SC["rate_ready"], 1)
            e.sem_inc(SC["da_done"], 2)
            e.sem_inc(SC["y_copied"], 2)
            for q in range(NDQ):
                scan_exp(e, q, q)
                if q >= 2:
                    scan_keep(e, q - 2, q - 2, 0, first=True)
            with e.Fori(1, NTR) as tr:
                for dq in range(NDQ):
                    scan_exp(e, tr * NDQ + dq, dq)
                    if dq == 2:
                        scan_turned(e, tr - 1)
                    if dq == 2:
                        scan_keep(e, tr * NDQ, 0, tr)
                    elif dq == 3:
                        scan_keep(e, tr * NDQ + 1, 1, tr)
                    else:
                        scan_keep(e, tr * NDQ + dq - 2, dq + 2, tr - 1)
            scan_keep(e, NSU - 2, 2, NTR - 1)
            scan_keep(e, NSU - 1, 3, NTR - 1)
            scan_turned(e, NTR - 1)

        @block.scalar
        def _(e):
            e.wait_ge(consts_in, CONSTS)
            e.copy(identb[:], ident[:]).then_inc(identb_ready, 1)
            run_stages(e, attention_scalar, scan_scalar, gelu_mixture_scalar, relu_mixture_scalar)

        def split_parts(e, then, v, full):
            then(e.tensor_copy(parts[:, v, 0], full))
            then(e.tensor_tensor(full, full, parts[:, v, 0], ALU.subtract))
            then(e.tensor_copy(parts[:, v, 1], full))
            then(e.tensor_tensor(full, full, parts[:, v, 1], ALU.subtract))
            e.tensor_copy(parts[:, v, 2], full).then_inc(SC[f"split{v}"], 1)

        def heads(flat, at):
            return flat[:, bass.ds(at, ST_ * D)].rearrange("p (i d) -> p i d", d=D)[:, :, 0:HG * HD].rearrange(
                "p i (h c) -> p i h c", h=HG)

        def split_heads(e, finish, u, par, at, which):
            full = {c: heads(rot, at + c * T) for c in which}
            if 0 in which:
                e.memset(qpad[:, par, :, :, AT_MAX:AT_MAX + 3], 0.0)
            for a in range(3):
                for c in which:
                    for n in (Q_PARTS, K_PARTS)[c][a]:
                        ins = e.tensor_copy(pads[c][:, par, :, :, n:n + HD], full[c] if a == 0 else rests[c])
                finish(ins)
                if a < 2:
                    for c in which:
                        n = (Q_PARTS, K_PARTS)[c][a][0]
                        ins = e.tensor_tensor(rests[c], full[c] if a == 0 else rests[c],
                                              pads[c][:, par, :, :, n:n + HD], ALU.subtract)
                    finish(ins)

        def rotate(e, then, b):
            half = D // 2
            t1 = qmf[:, 0:ST_ * half].rearrange("p (i f) -> p i f", f=half)
            t2 = qmf[:, ST_ * half:2 * ST_ * half].rearrange("p (i f) -> p i f", f=half)
            tiles = slice(b * ST_, (b + 1) * ST_)
            for c in range(2):
                even, odd = qk[:, tiles, c, 0::2], qk[:, tiles, c, 1::2]
                for part, (ea, oa) in enumerate(((cos, sin), (sin, cos))):
                    e.tensor_tensor(t1, even, ea[:], ALU.mult)
                    then(e.tensor_tensor(t2, odd, oa[:], ALU.mult))
                    then(e.tensor_tensor(rotv[:, c, tiles, part * half:(part + 1) * half], t1, t2, ALU.subtract))
            e.sem_inc(AT["rotated"], 1)

        @block.gpsimd
        def _(e):
            def pool_chain(ins):
                pool_steps[0] += 1
                ins.then_inc(pool_step, 1)
                e.wait_ge(pool_step, pool_steps[0])

            def place_v(u, par, at):
                e.tensor_copy(vpad[:, par, :, :, 0:HD], heads(vflat, at)).then_inc(AT["v_placed"], 1)

            def split(u, par, at):
                done = [0]

                def finish(ins):
                    done[0] += 1
                    ins.then_inc(AT["parts"], 1)
                    e.wait_ge(AT["parts"], 5 * (u - 1) + done[0])
                    e.sem_inc(AT["waited"], 1)

                split_heads(e, finish, u, par, at, (0, 1))
                e.sem_inc(AT["unit_split"], 2)

            def pool_unit(u, par, at, more=True):
                e.wait_ge(AT["pv_done"], NST * u + 2)
                e.sem_inc(AT["waited"], 1)
                place_v(u + 1, 1 - par, at(1))
                if more:
                    e.wait_ge(AT["returned"], NRE * u + NRE)
                    e.wait_ge(AT["turned"], NTU * u + NTU)
                    e.sem_inc(AT["waited"], 1)
                    split(u + 2, par, at(2))

            def attention_pool(e):
                e.wait_ge(LN["xn_ready"], stage_of["attention"]["norm"] + NTB)
                e.memset(qpad[:], 0.0)
                e.memset(kpad[:], 0.0)
                e.memset(vpad[:], 0.0).then_inc(AT["pads_ready"], 1)
                e.wait_ge(AT["pads_ready"], 1)
                e.memset(kpad[:, :, :, :, AT_MAX:AT_MAX + 3], 1.0).then_inc(AT["pads_ready"], 1)
                e.memset(vpad[:, :, :, :, HD:HD + 1], 1.0)
                e.memset(kz, 0.0)
                e.memset(qz, 0.0).then_inc(AT["pads_clear"], 1)
                e.wait_ge(AT["rotated"], 1)
                place_v(0, 0, 0)
                e.wait_ge(AT["unit_split"], 2)
                split(1, 1, HG * HD)
                e.wait_ge(AT["qkv_taken"], 2 * (NT - ST_))
                q2 = qk[:, ST_:NT].rearrange("p i c d -> p i (c d)")
                e.tensor_tensor(q2, q2, bqkv[:, 0:2 * D].unsqueeze(1).to_broadcast([P, ST_, 2 * D]), ALU.add)
                v2 = vall[:, ST_:NT]
                pool_chain(e.tensor_tensor(v2, v2, bqkv[:, 2 * D:3 * D].unsqueeze(1).to_broadcast([P, ST_, D]), ALU.add))
                rotate(e, pool_chain, 1)

                def pool_go(items, u, par, at, first=False):
                    if not first and not (isinstance(u, int) and u >= NU - 1):
                        pool_unit(u, par, at, not (isinstance(u, int) and u == NU - 2))
                pool_go.engine = e
                units(pool_go)

            def scan_pool(e):
                e.wait_ge(SC["arena_free"], 1)
                e.memset(sel[ROWS:P], 0.0)
                e.memset(dtp[ROWS:P], 0.0)
                e.memset(upp[ROWS:P], 0.0).then_inc(SC["rows_zeroed"], 1)
                e.wait_ge(SC["rows_zeroed"], 1)
                e.sem_inc(SC["waited"], 1)
                e.memset(cz, 0.0).then_inc(SC["c_zeroed"], 1)

                def split_quarter(k):
                    for v, full in enumerate((zt, ut)):
                        if k == 0 and v == 0:
                            continue
                        e.wait_ge(SC["u_ready"], min(k, 1) + 1)
                        if k >= 1:
                            e.wait_ge(parts_out, 16 * (2 * k - 1 + v))
                        split_parts(e, pool_chain, v, full[:, :, k * QT:(k + 1) * QT])

                def place_c(tr):
                    for b in range(B):
                        rows = slice(64 * b, 64 * b + 64)
                        to = cz.rearrange("p t c -> p (t c)")[rows].rearrange("p (g k) -> p g k", g=TR // 16)[
                            :, :, 16 * b:16 * b + 15 * 33 + 1:33]
                        e.tensor_copy(to, cT[rows, bass.ds(tr * TR, TR)].rearrange("p (g k) -> p g k", k=16)
                                      ).then_inc(SC["c_placed"], 1)
                    e.wait_ge(SC["c_placed"], 2 * tr + 2)
                    e.sem_inc(SC["waited"], 1)

                def place_next_c(tr):
                    e.wait_ge(SC["y_done"], NDQ * tr + 2)
                    e.sem_inc(SC["waited"], 1)
                    place_c(tr)

                split_quarter(0)
                e.wait_ge(SC["split1"], 1)
                e.wait_ge(SC["bT_ready"], 2)
                e.wait_ge(SC["c_zeroed"], 1)
                place_c(0)
                for k in range(1, 4):
                    split_quarter(k)
                    e.wait_ge(SC["split1"], k + 1)
                    place_next_c(k)
                with e.Fori(4, NTR) as tr:
                    place_next_c(tr)

            def gelu_mixture_pool(e, st, nxt):
                nf = F0 // P

                def weight_rests(k):
                    n = st["route"] // NTB * E + k
                    e.wait_ge(MX["w1_done"], n + 1)
                    for w, to, done in ((0, wup[:, :, k, 0:nf * P], "up_parts"),
                                        (1, wdn[:, :, k, 0:nf, :].rearrange("p a c d -> p a (c d)"), "dn_parts")):
                        e.tensor_tensor(to[:, 1], stage_w[:, n % SLOTS, w, 0:nf * P], to[:, 0],
                                        ALU.subtract).then_inc(MX[done], 1)

                def block(tb, first):
                    blk = st["route"] + tb
                    for ex in range(E + 1):
                        if first:
                            for k in ([0, 1] if ex == 0 else [ex + 1] if ex + 1 < E else []):
                                weight_rests(k)
                        for fc in range(1, nf, 2) if ex < E else ():
                            e.wait_ge(MX["act_done"], st["act"] + tb * (E * nf) + ex * nf + fc + 1)
                            e.sem_inc(MX["waited"], 1)
                            e.tensor_tensor(hr[:, ex % 2, 1, fc, :], hid[:, ex % 2, fc, :], hr[:, ex % 2, 0, fc, :],
                                            ALU.subtract).then_inc(MX["rest_pool"], 1)
                        if ex > 1:
                            k = ex - 1
                            e.wait_ge(MX["y_read"], blk * E + k + 1)
                            at_least(e, MX["acc_done"], blk * (E - 1) + k - 1)
                            e.sem_inc(MX["waited"], 1)
                            e.tensor_tensor(acc, acc, weighted[:, k % 2, :], ALU.add).then_inc(MX["acc_done"], 1)

                block(0, True)
                with e.Fori(1, NTB - 1) as tb:
                    block(tb, False)
                block(NTB - 1, False)

            run_stages(e, attention_pool, scan_pool, gelu_mixture_pool, lambda e, st, nxt: None)

        @block.vector
        def _(e):
            def link(ins):
                chained[0] += 1
                ins.then_inc(chain, 1)
                e.wait_ge(chain, chained[0])

            def task_vector(st, what, g):
                blk = bass.ds(g * TPB, TPB)
                if what == "stats":
                    n = 2 * (st["norm"] + g)
                    if not (isinstance(n, int) and n == 0):
                        e.wait_ge(LN["xn_ready"], st["norm"] + g)
                        e.sem_inc(LN["waited"], 1)
                    for j in range(TPB):
                        ins = e.bn_stats(stats[:, j, :], xf[:, bass.ds(g * TB + j * P, P)])
                    ins.then_inc(LN["step"], 1)
                    e.wait_ge(LN["step"], n + 1)
                    e.sem_inc(LN["waited"], 1)
                    for j in range(TPB):
                        ins = e.bn_aggr(mv[:, j, :], stats[:, j, :])
                    ins.then_inc(LN["step"], 1)
                    e.wait_ge(LN["step"], n + 2)
                    e.tensor_scalar(veps[:, 0:TPB], mv[:, 0:TPB, 1], LN_EPS, None, ALU.add).then_inc(LN["var_ready"], 1)
                elif what == "norm":
                    n = st["norm"] + g
                    e.wait_ge(LN["std_ready"], n + 1)
                    turned = st["turn"] + g
                    if st["kind"] != "scan" and not (isinstance(turned, int) and turned == 0):
                        e.wait_ge(LN["tp_done"], turned)
                    to = (xn[:].rearrange("p i d -> p (i d)"), g * TB) if st["kind"] == "scan" else (xn0f, 0)
                    e.reciprocal(rstd[:, 0:TPB], std[:, 0:TPB]).then_inc(rstd_ready, 1)
                    e.wait_ge(rstd_ready, n + 1)
                    if st["kind"] == "scan":
                        e.tensor_copy(allvar[:, blk], mv[:, 0:TPB, 1])
                        e.tensor_copy(allrstd[:, blk], rstd[:, 0:TPB])
                    for j in range(TPB):
                        ins = e.tensor_scalar(to[0][:, bass.ds(to[1] + j * P, P)], xf[:, bass.ds(g * TB + j * P, P)],
                                              mv[:, j, 0:1], rstd[:, j:j + 1], ALU.subtract, ALU.mult)
                    ins.then_inc(LN["xn_ready"], 1)
                elif what == "logits" and st["kind"] == 0:
                    e.wait_ge(LN["xnT_ready"], st["turn"] + g + 1)
                    cols = bass.ts(g, TB)
                    e.tensor_tensor(xp[:, 1, cols], xnT[:, cols], xp[:, 0, cols], ALU.subtract).then_inc(LN["rest_ready"], 1)
                elif what == "shift":
                    n = ROUTE * (st["route"] + g)
                    kind = st["kind"]
                    l = lg[:]
                    e.wait_ge(LN["logits_done"], st["route"] + g + 1)
                    e.tensor_tensor(l, ps[:, 7, 0:TPB * E].rearrange("p (i e) -> p i e", e=E),
                                    rb[kind][:].unsqueeze(1).to_broadcast([P, TPB, E]), ALU.add).then_inc(LN["route_step"], 1)
                    e.wait_ge(LN["route_step"], n + 1)
                    e.tensor_reduce(rowmax[:], l, AX.X, ALU.max).then_inc(LN["route_step"], 1)
                    e.wait_ge(LN["route_step"], n + 2)
                    e.tensor_tensor(l, l, rowmax[:].unsqueeze(2).to_broadcast([P, TPB, E]),
                                    ALU.subtract).then_inc(LN["shifted"], 1)
                elif what == "route":
                    n = ROUTE * (st["route"] + g) + 2
                    done = [0]

                    def step(ins):
                        done[0] += 1
                        ins.then_inc(LN["route_step"], 1)
                        e.wait_ge(LN["route_step"], n + done[0])

                    e.wait_ge(LN["exp_done"], st["route"] + g + 1)
                    l, pr, rm = lg[:], probs[:], rowmax[:]
                    step(e.tensor_reduce(rm, l, AX.X, ALU.add))
                    step(e.reciprocal(rm, rm))
                    step(e.tensor_tensor(pr, l, rm.unsqueeze(2).to_broadcast([P, TPB, E]), ALU.mult))
                    mine = pr.unsqueeze(3).to_broadcast([P, TPB, E, E])
                    other = pr.unsqueeze(2).to_broadcast([P, TPB, E, E])
                    e.tensor_tensor(beats, other, mine, ALU.is_gt)
                    step(e.tensor_tensor(ties, other, mine, ALU.is_equal))
                    step(e.tensor_tensor(ties, ties, earlier[:].unsqueeze(1).to_broadcast([P, TPB, E, E]), ALU.mult))
                    step(e.tensor_tensor(beats, beats, ties, ALU.add))
                    step(e.tensor_reduce(rank[:], beats, AX.X, ALU.add))
                    step(e.tensor_scalar(rank[:], rank[:], float((2, 1)[st["kind"]]), 0.5, ALU.is_lt,
                                         ALU.mult))
                    step(e.tensor_tensor(comb[:, blk, :], pr, rank[:], ALU.mult))
                    assert done[0] == ROUTE - 2

            def gelu_mixture_vector(e, st, nxt):
                nf = F0 // P
                before, along = first_tasks(st)

                def round_weights(k):
                    n = st["route"] // NTB * E + k
                    e.wait_ge(w_in[n % SLOTS], 32 * (n // SLOTS + 1))
                    e.tensor_copy(wup[:, 0, k, 0:nf * P], stage_w[:, n % SLOTS, 0, 0:nf * P])
                    e.tensor_copy(wdn[:, 0, k, 0:nf, :].rearrange("p c d -> p (c d)"), stage_w[:, n % SLOTS, 1, 0:nf * P]
                                  ).then_inc(MX["w1_done"], 1)

                def add_sum(tb):
                    e.wait_ge(MX["acc_turned"], st["route"] + tb + 1)
                    xs = xf[:, bass.ts(tb, TB)]
                    e.tensor_tensor(xs, xs, ps[:, 6, :], ALU.add).then_inc(MX["x_done"], 1)
                    e.wait_ge(MX["x_done"], st["route"] + tb + 1)

                round_weights(0)
                for task in before:
                    task_vector(*task)

                def split_comb(tb):
                    blk = st["route"] + tb
                    e.wait_ge(LN["route_step"], ROUTE * (blk + 1))
                    now = comb[:, bass.ds(tb * TPB, TPB), :]
                    for a in range(3):
                        ins = e.tensor_copy(comb3[:, :, a, 0:E], now if a == 0 else combnow[:])
                        if a < 2:
                            ins.then_inc(MX["comb_step"], 1)
                            e.wait_ge(MX["comb_step"], 4 * blk + 2 * a + 1)
                            e.tensor_tensor(combnow[:], now if a == 0 else combnow[:], comb3[:, :, a, 0:E],
                                            ALU.subtract).then_inc(MX["comb_step"], 1)
                            e.wait_ge(MX["comb_step"], 4 * blk + 2 * a + 2)
                    ins.then_inc(MX["comb_split"], 1)

                def block(tb, tasks, first, last=False):
                    blk = st["route"] + tb
                    if first:
                        split_comb(tb)
                    for ex in range(E + 1):
                        n_of = lambda k: blk * E + k + 1
                        if ex == 1 and not first:
                            add_sum(tb - 1)
                        if first and ex + 1 < E:
                            round_weights(ex + 1)
                        if ex == E and not last:
                            split_comb(tb + 1)
                        if ex < E:
                            for fc in range(0, nf, 2):
                                e.wait_ge(MX["act_done"], st["act"] + tb * (E * nf) + ex * nf + fc + 1)
                                e.tensor_tensor(hr[:, ex % 2, 1, fc, :], hid[:, ex % 2, fc, :], hr[:, ex % 2, 0, fc, :],
                                                ALU.subtract).then_inc(MX["rest_vector"], 1)
                        if ex >= 1:
                            k = ex - 1
                            e.wait_ge(MX["weight_cast"], n_of(k))
                            e.tensor_copy(weight, ps[:, 5, :]).then_inc(MX["weight_copied"], 1)
                            e.wait_ge(MX["weight_copied"], n_of(k))
                            if k >= 3:
                                e.wait_ge(MX["acc_done"], blk * (E - 1) + k - 2)
                            e.wait_ge(MX["down_done"], n_of(k))
                            to = acc if k == 0 else weighted[:, k % 2, :]
                            e.tensor_tensor(to, ps[:, 4, :], weight, ALU.mult).then_inc(MX["y_read"], 1)
                        for task in tasks.get(ex, []):
                            task_vector(*task)

                block(0, along, True)
                with e.Fori(1, NTB - 1) as tb:
                    block(tb, next_tasks(nxt, tb, 1), False)
                block(NTB - 1, next_tasks(nxt, NTB - 1, 1), False, True)
                add_sum(NTB - 1)

            def relu_mixture_vector(e, st, nxt):
                s = RELU[st["name"]]
                before, along = first_tasks(st)
                for task in before:
                    task_vector(*task)
                e.sem_inc(s["acc_done"], 2)
                e.sem_inc(s["bias_added"], 1)

                def block(tb, tasks):
                    for ex in range(E):
                        e.wait_ge(s["acc_done"], tb * E + ex + 2)
                        if ex == 0:
                            if isinstance(tb, int):
                                e.wait_ge(LN["route_step"], ROUTE * (st["route"] + 1))
                            e.tensor_copy(combnow[:], comb[:, bass.ds(tb * TPB, TPB), :]).then_inc(s["comb_copied"], 1)
                        for task in tasks.get(ex, []):
                            task_vector(*task)
                        e.wait_ge(s["down_done"], tb * E + ex + 3)
                        for j in range(TPB):
                            xs = xf[:, bass.ds(tb * TB + j * P, P)]
                            ins = e.scalar_tensor_tensor(out=xs, in0=ps[:, 4 + ex % 2, j * P:(j + 1) * P],
                                                         scalar=combf[:, bass.ds(tb * (TPB * E) + j * E + ex, 1)],
                                                         in1=xs, op0=ALU.mult, op1=ALU.add)
                        ins.then_inc(s["acc_done"], 1)
                        if ex == 4:
                            e.wait_ge(s["bias_done"], tb + 1)
                            e.wait_ge(s["acc_done"], tb * E + ex + 3)
                            xs = xf[:, bass.ts(tb, TB)]
                            e.tensor_tensor(xs, xs, ps[:, 3, :], ALU.add).then_inc(s["bias_added"], 1)
                            e.wait_ge(s["bias_added"], tb + 2)

                block(0, along)
                with e.Fori(1, NTB) as tb:
                    block(tb, next_tasks(nxt, tb))
                e.wait_ge(s["acc_done"], NTB * E + 2)

            def add_projected(g, bank):
                e.wait_ge(AT["proj_done"], g + 1)
                xs = xf[:, g * TB:(g + 1) * TB]
                e.tensor_tensor(xs, xs, ps[:, bank, :], ALU.add).then_inc(AT["proj_added"], 1)
                e.wait_ge(AT["proj_added"], g + 1)
                xs = x[:, g * TPB:(g + 1) * TPB, :]
                link(e.tensor_tensor(xs, xs, bo[:].unsqueeze(1).to_broadcast([P, TPB, D]), ALU.add))

            def unit_vector(items, u, par, at, first):
                for what, k, n in items:
                    v, vp = u + k, (par + k) % 2
                    if what == "qz":
                        e.wait_ge(AT["turned_copied"], NTU * v + 2 * n + 2)
                        if first and k == 0:
                            e.wait_ge(AT["pads_clear"], 1)
                        for h in range(HP):
                            rows = slice(h * HR, (h + 1) * HR)
                            ins = e.tensor_copy(qz[rows, HP * n + h, :], qT[rows, n, :])
                        ins.then_inc(AT["qz_ready"], 1)
                    elif what == "kz":
                        if n == 0:
                            e.wait_ge(AT["turned_copied"], NTU * v + NTU)
                            if not first:
                                e.wait_ge(AT["exp_done"], 2 * NST * u + 2)
                        rows = slice(n % HP * HR, (n % HP + 1) * HR)
                        ins = e.tensor_copy(kz[rows, vp, n, :], kT[vp][rows, n // HP, :])
                        if n == HG - 1:
                            ins.then_inc(AT["kz_ready"], 1)
                    elif what == "s":
                        h, group, w = s_blocks[n]
                        ng = len(group)
                        at_max = [i * HG * 2 + h * 2 + half for i, half in group]
                        e.wait_ge(AT["s_done"], NSB * v + n + 1)
                        e.tensor_reduce(maxf[:, at_max[0]:at_max[-1] + 1:max(1, at_max[-1] - at_max[0])],
                                        ps[:, n % 2, 0:ng * w].rearrange("p (g k) -> p g k", g=ng),
                                        AX.X, ALU.max).then_inc(AT["max_done"], 1)
                        if n == NSB - 1:
                            e.wait_ge(AT["max_done"], NSB * v + NSB)
                            e.tensor_reduce(negmax[:], maxima[:], AX.X, ALU.max, negate=True).then_inc(AT["max_part"], 1)
                            e.wait_ge(AT["max_part"], 5 * v + 1)
                            for a in range(3):
                                col = qpad[:, vp, :, :, AT_MAX + a]
                                ins = e.tensor_copy(col, negmax[:])
                                if a < 2:
                                    ins.then_inc(AT["max_part"], 1)
                                    e.wait_ge(AT["max_part"], 5 * v + 2 * a + 2)
                                    e.tensor_tensor(negmax[:], negmax[:], col, ALU.subtract).then_inc(AT["max_part"], 1)
                                    e.wait_ge(AT["max_part"], 5 * v + 2 * a + 3)
                            ins.then_inc(AT["negmax_ready"], 1)
                    elif what == "proj":
                        add_projected(n, n)
                    elif what == "task":
                        task_vector(*early_tasks[n])
                    elif what == "oturn":
                        e.wait_ge(AT["o_turned"], 2 * v + n + 1)
                        o = ps[:, 6 + n, :].rearrange("p (i h c) -> p i h c", i=4, h=HG)
                        e.wait_ge(AT["o_normed"], 2 * v + n + 2)
                        ins = e.reciprocal(osum[:], o[:, :, :, HD:HD + 1])
                        ins.then_inc(AT["o_summed"], 1)
                        e.wait_ge(AT["o_summed"], 2 * v + n + 1)
                        for i in range(4):
                            ins = e.tensor_tensor(
                                ctxv.rearrange("p i d -> p (i d)")[:, bass.ds(at(k) + (4 * n + i) * D, HG * HD)].rearrange(
                                    "p (h c) -> p h c", h=HG),
                                o[:, i, :, 0:HD], osum[:, i, :, :].to_broadcast([P, HG, HD]), ALU.mult)
                        ins.then_inc(AT["o_normed"], 1)

            def attention_vector(e):
                for task in opening_tasks(stage_of["attention"]):
                    task_vector(*task)
                for i in range(ST_):
                    e.wait_ge(AT["qkv_done"], i + 1)
                    e.tensor_tensor(qk[:, i].rearrange("p c d -> p (c d)"), ps[:, i % 4, 0:2 * D], bqkv[:, 0:2 * D],
                                    ALU.add).then_inc(AT["qkv_copied"], 1)
                    e.tensor_tensor(vall[:, i, :], ps[:, i % 4, 2 * D:3 * D], bqkv[:, 2 * D:3 * D],
                                    ALU.add).then_inc(AT["qkv_copied"], 1)
                e.wait_ge(AT["qkv_copied"], 2 * ST_)
                rotate(e, link, 0)
                e.wait_ge(AT["pads_ready"], 2)
                split_heads(e, link, 0, 0, 0, (0, 1))
                e.sem_inc(AT["unit_split"], 2)
                link(e.memset(maxima[:], MASKED))
                e.sem_inc(AT["o_normed"], 2)
                def go(items, u, par, at, first=False):
                    unit_vector(items, u, par, at, first)
                go.engine = e
                units(go)
                for g in range(EARLY, NTB):
                    add_projected(g, 2 + g)

            def scan_unit(q, par, t0):
                half = DQ * TR // 2
                e.wait_ge(SC["y_done"], q + 1)
                for c in range(4):
                    e.wait_ge(SC["u_cast"], 4 * q + c + 1)
                    e.tensor_tensor(hs[:, par, c * 8 * TR:(c + 1) * 8 * TR].rearrange("p (d t) -> p d t", t=TR),
                                    ps[:, 2 + 2 * (c % 2):4 + 2 * (c % 2), :].rearrange("p a (d t) -> p (a d) t", t=TR),
                                    bT[:, bass.ds(t0, TR)].unsqueeze(1).to_broadcast([P, 8, TR]),
                                    ALU.mult).then_inc(SC["in_done"], 1)
                    if c == 1:
                        e.wait_ge(SC["da_done"], 8 * q + 8 + 2)
                        e.memset(da[:, par, 0::CHUNK], 0.0).then_inc(SC["da_cut"], 1)
                    if c >= 2:
                        if c == 2:
                            e.wait_ge(SC["da_cut"], q + 1)
                        e.wait_ge(SC["in_done"], 4 * q + 2 * c - 2 + 2)
                        part = slice((c - 2) * half, (c - 1) * half)
                        ins = e.tensor_tensor_scan(hs[:, par, part], da[:, par, part], hs[:, par, part], 0.0, ALU.mult,
                                                   ALU.add)
                ins.then_inc(SC["h_done"], 1)

            def scan_vector(e):
                for task in opening_tasks(stage_of["scan"]):
                    task_vector(*task)
                e.wait_ge(LN["xn_ready"], stage_of["scan"]["norm"] + NTB)
                e.sem_inc(SC["arena_free"], 1)
                link(e.tensor_tensor(std[:], allrstd[:], allrstd[:], ALU.mult))
                link(e.tensor_tensor(std[:], std[:], allvar[:], ALU.mult))
                e.tensor_scalar(veps[:], std[:], RMS_EPS, None, ALU.add).then_inc(SC["rms_ready"], 1)
                e.wait_ge(SC["rms_std"], 1)
                link(e.reciprocal(rstd[:], std[:]))
                for i in range(NT):
                    e.scalar_tensor_tensor(out=xr[:, i, :], in0=xn[:, i, :], scalar=rstd[:, i:i + 1], in1=nw[:],
                                           op0=ALU.mult, op1=ALU.mult).then_inc(SC["xr_ready"], 1)
                e.wait_ge(SC["xn_turned"], NTB)
                for n, (k0, k1) in enumerate(((0, 1), (1, 4))):
                    for k in range(k0, k1):
                        part = slice(k * QT, (k + 1) * QT)
                        e.wait_ge(SC["dt_done"], k + 1)
                        link(e.tensor_scalar(zt[:, :, part], ps[:, k, :].rearrange("p (b t) -> p b t", b=B), dtb[:, 0:1],
                                             None, ALU.add))
                        e.scalar_tensor_tensor(out=soft[:, :, part], in0=zt[:, :, part], scalar=-1.0, in1=zt[:, :, part],
                                               op0=ALU.mult, op1=ALU.max).then_inc(SC["z_ready"], 1)
                    part = slice(k0 * QT, k1 * QT)
                    e.wait_ge(SC["ln_ready"], n + 1)
                    link(e.scalar_tensor_tensor(out=zt[:, :, part], in0=zt[:, :, part], scalar=0.0, in1=soft[:, :, part],
                                                op0=ALU.max, op1=ALU.add))
                    if n == 0:
                        e.wait_ge(SC["bc_done"], 2)
                    e.tensor_tensor(ut[:, :, part], zt[:, :, part], ut[:, :, part], ALU.mult).then_inc(SC["u_ready"], 1)
                    if n == 0:
                        e.wait_ge(SC["u_ready"], 1)
                        split_parts(e, link, 0, zt[:, :, part])
                e.wait_ge(SC["rate_exp"], 1)
                e.tensor_scalar(arate[:], arate[:], -1.0, None, ALU.mult).then_inc(SC["rate_ready"], 1)
                e.wait_ge(SC["skip_done"], 1)
                e.tensor_tensor(xf, xf, ps[:, 0:4, :].rearrange("p a b -> p (a b)"), ALU.add).then_inc(SC["prep_done"], 1)
                e.wait_ge(SC["prep_done"], 1)
                e.wait_ge(SC["sel_ready"], 1)
                e.sem_inc(SC["in_done"], 2)
                e.sem_inc(SC["h_done"], 2)
                e.sem_inc(SC["proj_added"], 1)

                def scan_add(tr):
                    e.wait_ge(SC["proj_done"], tr + 1)
                    xs = xf.rearrange("p (b t) -> p b t", b=B)[:, :, bass.ds(tr * P, P)]
                    e.tensor_tensor(xs, xs, ps[:, 7, B * D:2 * B * D].rearrange("p (b d) -> p b d", b=B),
                                    ALU.add).then_inc(SC["proj_added"], 1)

                for dq in range(NDQ):
                    scan_unit(dq, dq % 2, 0)
                with e.Fori(1, NTR) as tr:
                    for dq in range(NDQ):
                        scan_unit(tr * NDQ + dq, dq % 2, tr * TR)
                        if dq == 2:
                            scan_add(tr - 1)
                scan_add(NTR - 1)
                e.wait_ge(SC["proj_added"], NTR + 1)

            e.wait_ge(x_in, 16)
            e.wait_ge(consts_in, CONSTS)
            link(e.tensor_tensor(sel_row[:], ident[:, 0:E], ident[:, CP:CP + E], ALU.add))
            link(e.tensor_tensor(sel_row[:], sel_row[:], ident[:, 2 * CP:2 * CP + E], ALU.add))
            e.tensor_copy(sel_e[:], sel_row[:].unsqueeze(2).to_broadcast([P, E, P])).then_inc(sel_ready, 1)
            link(e.memset(comb3, 0.0))
            run_stages(e, attention_vector, scan_vector, gelu_mixture_vector, relu_mixture_vector)
            e.sem_inc(x_final, 1)


def constants():
    e = np.arange(E)
    n = np.arange(P)
    freq = np.power(np.float32(10000.0), np.float32(-2.0) * np.arange(D // 2, dtype=np.float32) / np.float32(D))
    angle = np.arange(S, dtype=np.float32)[:, None] * freq[None, :].astype(np.float32)
    tiled = lambda v: v.astype(np.float32).reshape(ST_, P, D // 2).transpose(1, 0, 2)
    later = np.where(n[None, :] > n[:, None], np.float32(MASKED), np.float32(0.0))
    k = np.arange(ROWS)
    same_r = (k % DG)[:, None, None] == np.arange(DG)[None, :, None]
    same_b = (k // (3 * DG))[:, None, None] == (np.arange(P) // STATE)[None, None, :]
    return {
        "sel": (same_r & same_b).astype(np.float32).reshape(ROWS, DG * P),
        "cos": tiled(np.cos(angle)), "sin": tiled(np.sin(angle)),
        "masks": np.stack([later, later.T], axis=1),
        "ident": np.eye(P, dtype=np.float32),
        "earlier": (e[None, :] < e[:, None]).astype(np.float32),
    }


def kernel(**inputs):
    import concourse.bacc as bacc
    from concourse.bass_utils import run_bass_kernel_spmd as run

    def a(name):
        return np.asarray(inputs[name])

    arrays = {
        "x": a("L0_attn_x").reshape(T, D),
        "rw0": a("L0_ffn_router_w"), "rb0": a("L0_ffn_router_b"),
        "up0": a("L0_ffn_expert_up").transpose(2, 0, 1),
        "dn0": a("L0_ffn_expert_down").reshape(E, D, F0 // P, P).transpose(3, 0, 2, 1),
        "rw1": a("L1_ffn_w_router"), "rb1": a("L1_ffn_b_router"),
        "up1": a("L1_ffn_w1").transpose(1, 0, 2),
        "dn1": a("L1_ffn_w2").reshape(E, F1 // P, P, D).transpose(2, 0, 1, 3),
        "b1": a("L1_ffn_b1").reshape(E, F1 // P, P).transpose(2, 0, 1),
        "b2": a("L1_ffn_b2"),
        "xpw": a("L1_attn_x_proj_w").T, "dtw": a("L1_attn_dt_proj_w").T,
        "dtb": a("L1_attn_dt_proj_b").reshape(D, 1), "dskip": a("L1_attn_D").reshape(D, 1),
        "opw": a("L1_attn_out_proj_w").T, "norm_w": a("L1_attn_norm_w"),
        "a_log": np.concatenate([a("L1_attn_A_log").T] * B, axis=0),
        "wqkv": np.concatenate([a("L0_attn_Wq"), a("L0_attn_Wk"), a("L0_attn_Wv")], axis=1),
        "bq": a("L0_attn_bq"), "bk": a("L0_attn_bk"), "bv": a("L0_attn_bv"),
        "wo": a("L0_attn_Wo"), "bo": a("L0_attn_bo"),
        **constants(),
    }
    arrays = {f"{k}_dram": np.ascontiguousarray(v) for k, v in arrays.items()}
    nc = bacc.Bacc("TRN2", target_bir_lowering=False, num_devices=1)
    t_in = {k[:-5]: nc.dram_tensor(k, v.shape, mybir.dt.from_np(v.dtype), kind="ExternalInput").ap()
            for k, v in arrays.items()}
    out = nc.dram_tensor("out_dram", (T, D), F32, kind="ExternalOutput").ap()
    scratch = nc.dram_tensor("parts_dram", (4, 2, 3, D, B, QT), BF16, kind="Internal").ap()
    build(nc, t_in, scratch, out)
    r = run(nc, [arrays], core_ids=[0])
    return r.results[0]["out_dram"].reshape(B, S, D)
```
